# Optimizing a Trainium2 kernel written in Bass

```python
import numpy as np
import jax
import jax.numpy as jnp

def _softmax(x, axis=-1):
    return jax.nn.softmax(x, axis=axis)

def _gelu(x):
    return jax.nn.gelu(x, approximate=True)

def _silu(x):
    return jax.nn.silu(x)

def _sigmoid(x):
    return jax.nn.sigmoid(x)

def _layernorm(x, axis=-1, eps=1e-05):
    m = jnp.mean(x, axis=axis, keepdims=True)
    v = jnp.var(x, axis=axis, keepdims=True)
    return (x - m) / jnp.sqrt(v + eps)

def _scatter_add(tgt, idx, src, axis=0):
    return tgt.at[idx].add(src)

def _segment_sum(src, seg, n):
    return jax.ops.segment_sum(src, seg, n)
kernel_name = 'mk_gnn_resnorm_d4_gnn_r32_555e2f'

def setup_inputs(seed: int=0):
    np.random.seed(seed)
    _w = jnp.asarray

    def _rec_inputs():
        import jax
        import jax.numpy as jnp
        _gk = jax.random.key(seed)
        x = -0.000202 + 1 * jax.random.normal(jax.random.fold_in(_gk, 1), (3125, 64), jnp.float32)
        src = jax.random.randint(jax.random.fold_in(_gk, 2), (50000,), 0, 3125, jnp.int32)
        dst = jnp.minimum((3125 * jax.random.uniform(jax.random.fold_in(_gk, 3), (50000,)) ** 2.0).astype(jnp.int32), 99999)
        _o = jnp.argsort(dst, stable=True)
        src = src[_o]
        dst = dst[_o]
        edge_type_65 = jax.random.randint(jax.random.fold_in(_gk, 13), (50000,), 0, 65, jnp.int32)
        edge_weight = jax.random.uniform(jax.random.fold_in(_gk, 14), (50000,), jnp.float32, 0.0, 1)
        return (x, src, dst, edge_type_65, edge_weight)
    x, src, dst, edge_type_65, edge_weight = _rec_inputs()

    def _L0_gnn_setup():
        import jax, jax.numpy as jnp
        import numpy as np
        N = 3125
        E = 50000
        F_IN = 64
        H = 8
        C = 8
        NEG_SLOPE = 0.2

        def gat_layer(x, src, dst, W, a_src, a_dst, b):
            h = (x @ W).reshape(N, H, C)
            alpha_s = jnp.einsum('nhc,hc->nh', h, a_src)
            alpha_d = jnp.einsum('nhc,hc->nh', h, a_dst)
            e = jax.nn.leaky_relu(alpha_s[src] + alpha_d[dst], NEG_SLOPE)
            m = jax.ops.segment_max(e, dst, num_segments=N)
            ex = jnp.exp(e - m[dst])
            denom = jax.ops.segment_sum(ex, dst, num_segments=N)
            alpha = ex / (denom[dst] + 1e-16)
            out = jax.ops.segment_sum(h[src] * alpha[:, :, None], dst, num_segments=N)
            return out.reshape(N, H * C) + b
        key = jax.random.key(seed)
        ks = jax.random.split(key, 14)
        x = jax.random.normal(ks[0], (N, F_IN), dtype=jnp.float32)
        edge_index = jax.random.randint(ks[1], (2, E), 0, N, dtype=jnp.int64)
        inp = {'x': x, 'edge_index': edge_index}
        s = 1.0 / np.sqrt(F_IN)
        for li, kbase in zip((1, 2, 3), (2, 6, 10)):
            inp[f'W{li}'] = jax.random.uniform(ks[kbase], (F_IN, H * C), jnp.float32, -s, s)
            inp[f'a_src{li}'] = jax.random.uniform(ks[kbase + 1], (H, C), jnp.float32, -s, s)
            inp[f'a_dst{li}'] = jax.random.uniform(ks[kbase + 2], (H, C), jnp.float32, -s, s)
            inp[f'b{li}'] = jnp.zeros((H * C,), jnp.float32)
        return inp
    _L0_gnn_all = _L0_gnn_setup()
    _L0_gnn_in = {k: v for k, v in _L0_gnn_all.items() if k in ('W1', 'a_src1', 'a_dst1', 'b1', 'W2', 'a_src2', 'a_dst2', 'b2', 'W3', 'a_src3', 'a_dst3', 'b3')}
    del _L0_gnn_all

    def _L1_gnn_setup():
        import jax, jax.numpy as jnp
        import numpy as np
        N, E, D, R, L = (50000, 18750, 64, 65, 2)

        def _rgcn_conv(x, src, dst, edge_type, W_r, W_root, b):
            n, d = x.shape
            r = W_r.shape[0]
            seg = dst * r + edge_type
            msg = x[src]
            agg = jax.ops.segment_sum(msg, seg, num_segments=n * r).reshape(n, r, d)
            cnt = jax.ops.segment_sum(jnp.ones((msg.shape[0],), x.dtype), seg, num_segments=n * r).reshape(n, r, 1)
            mean = agg / jnp.maximum(cnt, 1.0)
            out = jnp.einsum('nrd,rdk->nk', mean, W_r)
            return out + x @ W_root + b
        key = jax.random.key(seed)
        ks = jax.random.split(key, 10)
        x = jax.random.normal(ks[0], (N, D), dtype=jnp.float32)
        edge_index = jax.random.randint(ks[1], (2, E), 0, N, dtype=jnp.int64)
        edge_type = jax.random.randint(ks[2], (E,), 0, R, dtype=jnp.int64)
        s = 1.0 / np.sqrt(D)
        W = jax.random.normal(ks[3], (L, R, D, D), dtype=jnp.float32) * s
        root = jax.random.normal(ks[4], (L, D, D), dtype=jnp.float32) * s
        bias = jax.random.normal(ks[5], (L, D), dtype=jnp.float32) * 0.01
        res_W = jax.random.normal(ks[6], (L, D, D), dtype=jnp.float32) * s
        res_b = jax.random.normal(ks[7], (L, D), dtype=jnp.float32) * 0.01
        return {'x': x, 'edge_index': edge_index, 'edge_type': edge_type, 'W': W, 'root': root, 'bias': bias, 'res_W': res_W, 'res_b': res_b}
    _L1_gnn_all = _L1_gnn_setup()
    _L1_gnn_in = {k: v for k, v in _L1_gnn_all.items() if k in ('W', 'root', 'bias', 'res_W', 'res_b')}
    del _L1_gnn_all

    def _L2_gnn_setup():
        import jax, jax.numpy as jnp
        import numpy as np
        N_NODES = 3125
        N_EDGES = 37500
        D_FEAT = 64
        key = jax.random.key(seed)
        k1, k2, k3 = jax.random.split(key, 3)
        feat = jax.random.normal(k1, (N_NODES, D_FEAT), dtype=jnp.float32)
        eps = jnp.zeros((1,), dtype=jnp.float32)
        edge_src = jax.random.randint(k2, (N_EDGES,), 0, N_NODES, dtype=jnp.int32)
        edge_dst = jax.random.randint(k3, (N_EDGES,), 0, N_NODES, dtype=jnp.int32)
        return {'feat': feat, 'eps': eps, 'edge_src': edge_src, 'edge_dst': edge_dst}
    _L2_gnn_all = _L2_gnn_setup()
    _L2_gnn_in = {k: v for k, v in _L2_gnn_all.items() if k in ('eps',)}
    del _L2_gnn_all

    def _L3_gnn_setup():
        import jax, jax.numpy as jnp
        import numpy as np
        N_NODES = 3125
        N_EDGES = 50000
        D = 64
        BN_EPS = 1e-05

        def _bn(x, gamma, beta):
            mu = jnp.mean(x, axis=0)
            var = jnp.var(x, axis=0)
            return gamma * (x - mu) * jax.lax.rsqrt(var + BN_EPS) + beta
        key = jax.random.key(seed)
        ks = jax.random.split(key, 8)
        h = jax.random.normal(ks[0], (N_NODES, D), dtype=jnp.float32)
        edge_weight = jax.random.uniform(ks[1], (N_EDGES,), dtype=jnp.float32)
        src = jax.random.randint(ks[2], (N_EDGES,), 0, N_NODES)
        dst = jax.random.randint(ks[3], (N_EDGES,), 0, N_NODES)
        W1 = jax.random.normal(ks[4], (D, D), dtype=jnp.float32) * (1.0 / np.sqrt(D))
        W2 = jax.random.normal(ks[5], (D, D), dtype=jnp.float32) * (1.0 / np.sqrt(D))
        return {'h': h, 'edge_weight': edge_weight, 'src': src, 'dst': dst, 'W1': W1, 'b1': jnp.zeros((D,), jnp.float32), 'gamma1': jnp.ones((D,), jnp.float32), 'beta1': jnp.zeros((D,), jnp.float32), 'W2': W2, 'b2': jnp.zeros((D,), jnp.float32), 'gamma2': jnp.ones((D,), jnp.float32), 'beta2': jnp.zeros((D,), jnp.float32)}
    _L3_gnn_all = _L3_gnn_setup()
    _L3_gnn_in = {k: v for k, v in _L3_gnn_all.items() if k in ('W1', 'b1', 'gamma1', 'beta1', 'W2', 'b2', 'gamma2', 'beta2')}
    del _L3_gnn_all
    return {'x': x, 'src': src, 'dst': dst, 'edge_type_65': edge_type_65, 'edge_weight': edge_weight, 'L0_gnn_W1': _L0_gnn_in['W1'], 'L0_gnn_a_src1': _L0_gnn_in['a_src1'], 'L0_gnn_a_dst1': _L0_gnn_in['a_dst1'], 'L0_gnn_b1': _L0_gnn_in['b1'], 'L0_gnn_W2': _L0_gnn_in['W2'], 'L0_gnn_a_src2': _L0_gnn_in['a_src2'], 'L0_gnn_a_dst2': _L0_gnn_in['a_dst2'], 'L0_gnn_b2': _L0_gnn_in['b2'], 'L0_gnn_W3': _L0_gnn_in['W3'], 'L0_gnn_a_src3': _L0_gnn_in['a_src3'], 'L0_gnn_a_dst3': _L0_gnn_in['a_dst3'], 'L0_gnn_b3': _L0_gnn_in['b3'], 'L1_gnn_W': _L1_gnn_in['W'], 'L1_gnn_root': _L1_gnn_in['root'], 'L1_gnn_bias': _L1_gnn_in['bias'], 'L1_gnn_res_W': _L1_gnn_in['res_W'], 'L1_gnn_res_b': _L1_gnn_in['res_b'], 'L2_gnn_eps': _L2_gnn_in['eps'], 'L3_gnn_W1': _L3_gnn_in['W1'], 'L3_gnn_b1': _L3_gnn_in['b1'], 'L3_gnn_gamma1': _L3_gnn_in['gamma1'], 'L3_gnn_beta1': _L3_gnn_in['beta1'], 'L3_gnn_W2': _L3_gnn_in['W2'], 'L3_gnn_b2': _L3_gnn_in['b2'], 'L3_gnn_gamma2': _L3_gnn_in['gamma2'], 'L3_gnn_beta2': _L3_gnn_in['beta2']}

def reference(x, src, dst, edge_type_65, edge_weight, L0_gnn_W1, L0_gnn_a_src1, L0_gnn_a_dst1, L0_gnn_b1, L0_gnn_W2, L0_gnn_a_src2, L0_gnn_a_dst2, L0_gnn_b2, L0_gnn_W3, L0_gnn_a_src3, L0_gnn_a_dst3, L0_gnn_b3, L1_gnn_W, L1_gnn_root, L1_gnn_bias, L1_gnn_res_W, L1_gnn_res_b, L2_gnn_eps, L3_gnn_W1, L3_gnn_b1, L3_gnn_gamma1, L3_gnn_beta1, L3_gnn_W2, L3_gnn_b2, L3_gnn_gamma2, L3_gnn_beta2):
    import jax
    import jax.numpy as jnp

    def _L0_gnn_ref(x, edge_index, W1, a_src1, a_dst1, b1, W2, a_src2, a_dst2, b2, W3, a_src3, a_dst3, b3):
        import jax, jax.numpy as jnp
        import numpy as np
        N = 3125
        E = 50000
        F_IN = 64
        H = 8
        C = 8
        NEG_SLOPE = 0.2

        def gat_layer(x, src, dst, W, a_src, a_dst, b):
            h = (x @ W).reshape(N, H, C)
            alpha_s = jnp.einsum('nhc,hc->nh', h, a_src)
            alpha_d = jnp.einsum('nhc,hc->nh', h, a_dst)
            e = jax.nn.leaky_relu(alpha_s[src] + alpha_d[dst], NEG_SLOPE)
            m = jax.ops.segment_max(e, dst, num_segments=N)
            ex = jnp.exp(e - m[dst])
            denom = jax.ops.segment_sum(ex, dst, num_segments=N)
            alpha = ex / (denom[dst] + 1e-16)
            out = jax.ops.segment_sum(h[src] * alpha[:, :, None], dst, num_segments=N)
            return out.reshape(N, H * C) + b
        loop = jnp.arange(N, dtype=edge_index.dtype)
        src = jnp.concatenate([edge_index[0], loop])
        dst = jnp.concatenate([edge_index[1], loop])
        h = jax.nn.relu(gat_layer(x, src, dst, W1, a_src1, a_dst1, b1))
        h = jax.nn.relu(gat_layer(h, src, dst, W2, a_src2, a_dst2, b2))
        return gat_layer(h, src, dst, W3, a_src3, a_dst3, b3)

    def _L1_gnn_ref(x, edge_index, edge_type, W, root, bias, res_W, res_b):
        import jax, jax.numpy as jnp
        import numpy as np
        N, E, D, R, L = (50000, 18750, 64, 65, 2)

        def _rgcn_conv(x, src, dst, edge_type, W_r, W_root, b):
            n, d = x.shape
            r = W_r.shape[0]
            seg = dst * r + edge_type
            msg = x[src]
            agg = jax.ops.segment_sum(msg, seg, num_segments=n * r).reshape(n, r, d)
            cnt = jax.ops.segment_sum(jnp.ones((msg.shape[0],), x.dtype), seg, num_segments=n * r).reshape(n, r, 1)
            mean = agg / jnp.maximum(cnt, 1.0)
            out = jnp.einsum('nrd,rdk->nk', mean, W_r)
            return out + x @ W_root + b
        src, dst = (edge_index[0], edge_index[1])
        h = x
        for l in range(W.shape[0]):
            conv = _rgcn_conv(h, src, dst, edge_type, W[l], root[l], bias[l])
            conv = jax.nn.relu(conv)
            res = jax.nn.relu(h @ res_W[l] + res_b[l])
            h = conv + res
        return h

    def _L2_gnn_ref(feat, eps, edge_src, edge_dst):
        import jax, jax.numpy as jnp
        import numpy as np
        N_NODES = 3125
        N_EDGES = 37500
        D_FEAT = 64
        messages = feat[edge_src]
        neigh = jax.ops.segment_sum(messages, edge_dst, num_segments=N_NODES)
        return (1.0 + eps) * feat + neigh

    def _L3_gnn_ref(h, edge_weight, src, dst, W1, b1, gamma1, beta1, W2, b2, gamma2, beta2):
        import jax, jax.numpy as jnp
        import numpy as np
        N_NODES = 3125
        N_EDGES = 50000
        D = 64
        BN_EPS = 1e-05

        def _bn(x, gamma, beta):
            mu = jnp.mean(x, axis=0)
            var = jnp.var(x, axis=0)
            return gamma * (x - mu) * jax.lax.rsqrt(var + BN_EPS) + beta
        msg = h[src] * edge_weight[:, None]
        agg = jax.ops.segment_sum(msg, dst, num_segments=h.shape[0])
        x = agg + h
        x = jax.nn.relu(_bn(x @ W1 + b1, gamma1, beta1))
        x = jax.nn.relu(_bn(x @ W2 + b2, gamma2, beta2))
        return x
    edge_index = jnp.stack([src, dst])
    x = _layernorm(x + _L0_gnn_ref(x, edge_index, L0_gnn_W1, L0_gnn_a_src1, L0_gnn_a_dst1, L0_gnn_b1, L0_gnn_W2, L0_gnn_a_src2, L0_gnn_a_dst2, L0_gnn_b2, L0_gnn_W3, L0_gnn_a_src3, L0_gnn_a_dst3, L0_gnn_b3), axis=-1)
    x = _layernorm(x + _L1_gnn_ref(x, edge_index, edge_type_65, L1_gnn_W, L1_gnn_root, L1_gnn_bias, L1_gnn_res_W, L1_gnn_res_b), axis=-1)
    x = _layernorm(x + _L2_gnn_ref(x, L2_gnn_eps, src, dst), axis=-1)
    x = _layernorm(x + _L3_gnn_ref(x, edge_weight, src, dst, L3_gnn_W1, L3_gnn_b1, L3_gnn_gamma1, L3_gnn_beta1, L3_gnn_W2, L3_gnn_b2, L3_gnn_gamma2, L3_gnn_beta2), axis=-1)
    return x

_drawn_inputs = setup_inputs


def setup_inputs(seed=0):
    import zlib

    import numpy as np

    out = dict(_drawn_inputs(seed))
    spreads = {'L0_gnn_b1': (0.0, 0.585),
     'L0_gnn_b2': (0.0, 0.1),
     'L0_gnn_b3': (0.0, 0.1),
     'L3_gnn_b1': (0.0, 2.0),
     'L3_gnn_gamma1': (1.0, 0.2),
     'L3_gnn_beta1': (0.0, 0.1),
     'L3_gnn_b2': (0.0, 2.0),
     'L3_gnn_gamma2': (1.0, 0.2),
     'L3_gnn_beta2': (0.0, 0.1)}
    factors = {'L0_gnn_W1': 8.0,
     'L0_gnn_a_src1': 8.0,
     'L0_gnn_a_dst1': 23.539,
     'L0_gnn_a_src2': 8.0,
     'L0_gnn_a_dst2': 8.0,
     'L0_gnn_a_src3': 8.0,
     'L0_gnn_a_dst3': 28.843,
     'L1_gnn_bias': 8.0,
     'L1_gnn_res_b': 8.0}
    for name, (base, spread) in spreads.items():
        noise = np.random.default_rng([zlib.crc32(name.encode()), seed]).standard_normal(out[name].shape)
        drawn = base * np.exp(spread * noise) if base else spread * noise
        out[name] = jnp.asarray(drawn.astype(out[name].dtype))
    for name, factor in factors.items():
        out[name] = (out[name] * factor).astype(out[name].dtype)
    return out
```

```python
from contextlib import ExitStack, contextmanager

import concourse.bass as bass
from concourse import mybir

F32 = mybir.dt.float32
I32 = mybir.dt.int32
BF16 = mybir.dt.bfloat16
ALU = mybir.AluOpType
ACT = mybir.ActivationFunctionType
X = mybir.AxisListType.X

P = 128
NODES, D = 3125, 64
EDGES = 50000
HEADS, C = 8, 8
REL = 65
TILES = -(-NODES // P)
LAST = NODES - (TILES - 1) * P
CHUNKS = -(-EDGES // P)
EB = -(-CHUNKS // P)
STEPS = CHUNKS + TILES
HALF = 8
ITERS = STEPS // (2 * HALF)
KB = 16
KG = STEPS // KB
SL = KG * P
PITCH, PERBANK = 84, 6
BANKS = -(-TILES // PERBANK)
CW = REL + 2
NEVER = 4000.0
BIG = 1.0e30
EPS = 1e-5
assert STEPS == 2 * HALF * ITERS == KB * KG and KB * HEADS == P


class Signal:

    def __init__(self, sem, base=0):
        self.sem, self.base = sem, base

    def wait(self, eng, count):
        eng.wait_ge(self.sem, count + self.base)


class Order:

    def __init__(self, eng, sem):
        self.eng, self.sem, self.total, self.loop_at = eng, sem, 0, None

    def done(self, ins):
        ins.then_inc(self.sem, 1)
        self.total += 1

    def wait(self):
        if self.loop_at is None:
            self.eng.wait_ge(self.sem, self.total)
        else:
            reg, first, per, base = self.loop_at
            self.eng.wait_ge(self.sem, reg * per + (self.total - first * per))

    def then(self, ins):
        self.done(ins)
        self.wait()

    @contextmanager
    def loop(self, reg, first, last, per):
        base = self.total
        self.loop_at = (reg, first, per, base)
        yield
        assert self.total == base + per, (self.total - base, per)
        self.total = base + (last - first) * per
        self.loop_at = None


def build(nc, a, out):
    with ExitStack() as ctx:
        def sb(name, shape, dt=F32):
            return ctx.enter_context(nc.sbuf_tensor(name, shape, dt))

        def sem(name):
            return ctx.enter_context(nc.semaphore(name))

        def dram(name, shape, dt=F32):
            return nc.dram_tensor(name, shape, dt).ap()

        arena = sb("arena", [P, 5 * SL])
        raw = arena[:, 0:4 * EB * P].bitcast(I32).rearrange("p (q b e) -> p q b e", q=4, b=EB)
        lists = arena[:, 4 * EB * P:8 * EB * P].rearrange("p (q b e) -> p q b e", q=4, b=EB)
        pick = arena[:, 8 * EB * P:8 * EB * P + EB * STEPS].rearrange("p (b s) -> p b s", b=EB)
        logit = arena[:, 0:SL].rearrange("p (s h) -> p s h", h=HEADS)
        own = arena[:, SL:2 * SL].rearrange("p (s h) -> p s h", h=HEADS)
        logit_T, own_T = arena[:, 2 * SL:3 * SL], arena[:, 3 * SL:4 * SL]
        smax, smax2 = arena[:, 4 * SL:5 * SL], arena[:, 0:SL]
        rel_w = arena[0:D, 0:CW * D]
        stage = arena[:, CW * D:3 * CW * D].rearrange("p (s c) -> p s c", s=2)
        rr = arena[:, 3 * CW * D:3 * CW * D + TILES * 2 * D].rearrange("p (t c) -> p t c", t=TILES)

        ring = sb("ring", [P, 2, HALF, D + HEADS])
        onehot = sb("onehot", [P, 2, HALF, P])
        onehot_T = sb("onehot_T", [P, 2, HALF, P])
        msg = sb("msg", [P, 2, HALF, D + 2 * HEADS])
        relhot = sb("relhot", [P, 2, HALF, REL])
        relsel = msg[:].rearrange("p a s c -> p (a s c)")[:, 0:HALF * REL].rearrange("p (s c) -> p s c", c=REL)
        gz = sb("gz", [P, HALF, HEADS])
        idx_now = sb("idx_now", [P, 2, HALF], I32)
        nodeq = sb("nodeq", [P, BANKS * 512])
        ht = sb("ht", [P, TILES, D + HEADS])
        x = sb("x", [P, TILES, D])
        y = sb("y", [P, TILES, D])
        u = sb("u", [P, TILES, D + 2 * HEADS])
        w1 = sb("w1", [P, TILES, D])
        w2 = sb("w2", [P, TILES, D])
        small = sb("small", [P, 6, TILES * HEADS])
        iota = sb("iota", [P, P])
        ident = sb("ident", [P, P])
        ones = sb("ones", [P, P])
        iota_rel = sb("iota_rel", [P, REL])
        iota_s = sb("iota_s", [P, STEPS])
        part = sb("part", [P, 1])
        zero = sb("zero", [1, 512])
        node_of = sb("node_of", [P, STEPS])
        key = sb("key", [P, STEPS])
        rel_of = sb("rel_of", [P, STEPS])
        weight = sb("weight", [P, STEPS])
        count = sb("count", [P, STEPS])
        first = sb("first", [P, STEPS])
        tile_of = sb("tile_of", [P, STEPS])
        tmp_s = sb("tmp_s", [P, STEPS])
        tmp_s2 = sb("tmp_s2", [P, STEPS])
        src_idx = sb("src_idx", [P, STEPS], I32)
        rel_idx = sb("rel_idx", [P, STEPS], I32)
        place = sb("place", [1, STEPS], I32)
        ends = sb("ends", [P, TILES - 1])
        joins = sb("joins", [P, SL + 1], BF16)
        in_first = sb("in_first", [P, SL], BF16)
        in_last = sb("in_last", [P, SL], BF16)
        rows = sb("rows", [1, 12, P])
        cols = sb("cols", [P, 2])
        wn = sb("wn", [D, D])
        vecs = sb("vecs", [P, 4, D])
        eps1 = sb("eps1", [P, 1])
        xs = sb("xs", [P, 5, D])
        xT = sb("xT", [D, 5, P])
        st = sb("st", [P, 8, D])
        ps = ctx.enter_context(nc.psum_tensor("ps", [P, 8, 512], F32))
        flat = ps[:].rearrange("p b n -> p (b n)")

        gat_table = dram("gat_table", [TILES * P, D + HEADS])
        x_table = dram("x_table", [TILES * P, D])
        rel_table = dram("rel_table", [TILES * P * REL, D])
        spill = dram("spill", [P, STEPS, D + HEADS])

        def per_head(ap):
            return ap.unsqueeze(3).broadcast_to([P, ap.shape[1], HEADS, C])

        def of_bank(m, b, col, n):
            k = min(PERBANK, TILES - b * PERBANK)
            v = m[:, b * 512:b * 512 + k * PITCH].rearrange("p (t c) -> p t c", c=PITCH)
            return v[:, :, col:col + n], slice(b * PERBANK, b * PERBANK + k)

        HV = 2 * ITERS
        shared = {}

        def signal(name, base=0):
            if name not in shared:
                shared[name] = sem(name)
            return Signal(shared[name], base)

        class Round:

            def __init__(self, n, name, kind, layer=0):
                self.kind, self.layer = kind, layer
                self.table_ready = signal("table_ready" if kind == "gat" else name + "_table_ready", n if kind == "gat" else 0)
                self.table = [signal(f"{name}_table{q}") for q in range(2)]
                self.staged = signal("staged", HV * n)
                self.gathered = [signal(f"{name}_gathered{q}") for q in range(2)]
                self.hot = signal("hot", HV * n)
                self.summed = signal("summed", HV * n)
                self.acc_read = signal("acc_read", n)
                self.finished = signal("finished", n)
                if kind == "gat":
                    m, q2 = layer, 16 * ITERS * layer
                    self.turned = signal("turned", 2 * HV * m)
                    self.turned_out = signal("turned_out", 2 * HV * m)
                    self.looked = signal("looked", HV * m)
                    self.taken = signal("taken", HV * m)
                    self.spilled = [signal(f"spilled{q}", q2) for q in range(2)]
                    self.back = [signal(f"back{q}", q2) for q in range(2)]
                    self.msgs = signal("msgs", HV * m)
                    self.acc_clear = signal("acc_clear", m)
                    self.regrouped = signal("regrouped", 2 * m)
                    self.to_heads = signal("to_heads", 2 * KG * m)
                    self.to_heads_out = signal("to_heads_out", 2 * KG * m)
                    self.scanned = signal("scanned", m)
                    self.ends_T = signal("ends_T", m)
                    self.carried = signal("carried", m)
                    self.carries_T = signal("carries_T", m)
                    self.less_max = signal("less_max", 2 * m)
                    self.exped = signal("exped", 2 * m)
                    self.to_edges = signal("to_edges", 2 * KG * m)
                    self.to_edges_out = signal("to_edges_out", 2 * KG * m)

        class Projection:

            def __init__(self, n, weights):
                self.w = signal(f"{weights}")
                self.inp = signal("proj_in", n)
                self.xs, self.tr, self.xT, self.mm, self.out = (
                    signal("proj_" + k, 5 * n) for k in ("xs", "turned", "xT", "made", "out"))

        gats = [(Projection(l, f"gat{l}_w"), Round(l, f"gat{l}", "gat", l)) for l in range(3)]
        bns = [Projection(3 + l, f"bn{l}_w") for l in range(2)]

        class Expansion:

            def __init__(self, l):
                self.w = signal(f"rel{l}_w")
                self.inp = signal("exp_in", l)
                self.xs, self.tr, self.xT = (signal("exp_" + k, TILES * l) for k in ("xs", "turned", "xT"))
                self.mm = signal("exp_made", 9 * TILES * l)
                self.out_v = signal("exp_out_v", 6 * TILES * l)
                self.out_a = signal("exp_out_a", 4 * TILES * l)

        rels = [(Expansion(l), Round(3 + l, f"rel{l}", "rel", l)) for l in range(2)]
        gin, wgin = Round(5, "gin", "sum"), Round(6, "wgin", "weighted")
        loaded, lists_loaded, pads_set = sem("loaded"), sem("lists_loaded"), sem("pads_set")
        const_ready, ends_counted, ends_summed = sem("const_ready"), sem("ends_counted"), sem("ends_summed")
        ones_ready = sem("ones_ready")
        picks_ready, picked, edge_lists_ready = sem("picks_ready"), sem("picked"), sem("edge_lists_ready")
        keys_ready, keys_T, keys_out = sem("keys_ready"), sem("keys_T"), sem("keys_out")
        key_rows, start_row, start_col, starts_T = sem("key_rows"), sem("start_row"), sem("start_col"), sem("starts_T")
        starts, starts_out, setup_read = sem("starts"), sem("starts_out"), sem("setup_read")
        bn_part, bn_total, bn_done = sem("bn_part"), sem("bn_total"), sem("bn_done")
        var_ready, std_ready = sem("var_ready"), sem("std_ready")
        x_final, out_written = sem("x_final"), sem("out_written")
        v_own = sem("v_own")
        gather_begun, tile_begun = sem("gather_begun"), sem("tile_begun")

        block = ctx.enter_context(nc.Block())

        def every(v, n=D):
            return v.rearrange("(a n) -> a n", a=1).broadcast_to([P, n])

        def halves(eng, body, last=ITERS):
            body(0, 0, True)
            body(0, 1, True)
            with eng.Fori(1, last) as i:
                body(i, 0, False)
                body(i, 1, False)

        def tiles_by_two(eng, body):
            body(0, 0, True)
            body(1, 1, True)
            with eng.Fori(1, TILES // 2) as i:
                body(i * 2, 0, False)
                body(i * 2 + 1, 1, False)
            body(TILES - 1, 0, False)

        @block.sync
        def _(sp):
            sp.wait_ge(pads_set, 1)
            sp.dma_start(x[:, 0:TILES - 1, :],
                         a["x"][0:(TILES - 1) * P, :].rearrange("(t p) f -> p t f", p=P)).then_inc(loaded, 16)
            sp.dma_start(x[0:LAST, TILES - 1, :], a["x"][(TILES - 1) * P:, :]).then_inc(loaded, 16)
            sp.dma_start(eps1[:], every(a["L2_gnn_eps"], 1)).then_inc(loaded, 16)
            full, rest = (EB - 1) * P * P, EDGES // P - (EB - 1) * P
            for q, n in enumerate(("dst", "src", "edge_type_65", "edge_weight")):
                o = raw[:, q] if q < 3 else lists[:, 3]
                sp.dma_start(o[:, 0:EB - 1, :],
                             a[n][0:full].rearrange("(b p e) -> p b e", p=P, e=P)).then_inc(lists_loaded, 16)
                sp.dma_start(o[0:rest, EB - 1, :],
                             a[n][full:full + rest * P].rearrange("(p e) -> p e", e=P)).then_inc(lists_loaded, 16)
                sp.dma_start(o[rest:rest + 1, EB - 1, 0:EDGES % P],
                             a[n][full + rest * P:].rearrange("(a e) -> a e", a=1)).then_inc(lists_loaded, 16)

            for pj, r in gats:
                l = r.layer + 1
                if r.layer:
                    gats[r.layer - 1][1].finished.wait(sp, 1)
                sp.dma_start(wn[:], a[f"L0_gnn_W{l}"]).then_inc(pj.w.sem, 16)
                for k, n in enumerate((f"L0_gnn_a_src{l}", f"L0_gnn_a_dst{l}")):
                    sp.dma_start(vecs[:, k, :], every(a[n].rearrange("h c -> (h c)"))).then_inc(pj.w.sem, 16)
                sp.dma_start(vecs[:, 2, :], every(a[f"L0_gnn_b{l}"])).then_inc(pj.w.sem, 16)
                r.table_ready.wait(sp, 1)
                sp.dma_start(gat_table.rearrange("(t p) f -> p t f", p=P), ht[:]).then_inc(r.table[0].sem, 16)

                def store(i, q, peeled):
                    r.gathered[q].wait(sp, i * (16 * HALF) + 16 * HALF)
                    sp.dma_start(spill[:, bass.ds(i * 2 * HALF + q * HALF, HALF), :], ring[:, q])\
                      .then_inc(r.spilled[q].sem, 16)
                halves(sp, store)
                for q in range(2):
                    r.spilled[q].wait(sp, 16 * ITERS)
                r.taken.wait(sp, HV)

                def load(i, q, peeled):
                    if not peeled:
                        r.msgs.wait(sp, i * 2 + (q - 1))
                    sp.dma_start(ring[:, q], spill[:, bass.ds(i * 2 * HALF + q * HALF, HALF), :])\
                      .then_inc(r.back[q].sem, 16)
                halves(sp, load)

            for ex, r in rels:
                l = r.layer
                prev = rels[0][1] if l else gats[2][1]
                prev.finished.wait(sp, 1)
                n = 13
                for q in range(REL // n):
                    sp.dma_start(rel_w[:, q * n * D:(q + 1) * n * D].rearrange("d (r k) -> d r k", k=D),
                                 a["L1_gnn_W"][l, q * n:(q + 1) * n].rearrange("r d k -> d r k")).then_inc(ex.w.sem, 16)
                sp.dma_start(rel_w[:, REL * D:(REL + 1) * D], a["L1_gnn_root"][l]).then_inc(ex.w.sem, 16)
                sp.dma_start(rel_w[:, (REL + 1) * D:CW * D], a["L1_gnn_res_W"][l]).then_inc(ex.w.sem, 16)
                sp.dma_start(vecs[:, 0, :], every(a["L1_gnn_bias"][l])).then_inc(ex.w.sem, 16)
                sp.dma_start(vecs[:, 1, :], every(a["L1_gnn_res_b"][l])).then_inc(ex.w.sem, 16)
                by_node = rel_table.rearrange("(n r) k -> n (r k)", r=REL)

                def store(t, slot, peeled):
                    ex.out_v.wait(sp, t * 6 + 6)
                    ex.out_a.wait(sp, t * 4 + 4)
                    sp.dma_start(by_node[bass.ds(t * P, P), :], stage[:, slot, 0:REL * D]).then_inc(r.table[slot].sem, 16)
                tiles_by_two(sp, store)
            for r in (gin, wgin):
                r.table_ready.wait(sp, 1)
                sp.dma_start(x_table.rearrange("(t p) f -> p t f", p=P), x[:]).then_inc(r.table[0].sem, 16)
            for l, pj in enumerate(bns):
                if l:
                    sp.wait_ge(bn_done, 1)
                sp.dma_start(wn[:], a[f"L3_gnn_W{l + 1}"]).then_inc(pj.w.sem, 16)
                for k, n in enumerate(("b", "gamma", "beta")):
                    sp.dma_start(vecs[:, k, :], every(a[f"L3_gnn_{n}{l + 1}"])).then_inc(pj.w.sem, 16)
            sp.wait_ge(x_final, 1)
            sp.dma_start(out[0:(TILES - 1) * P, :].rearrange("(t p) f -> p t f", p=P),
                         x[:, 0:TILES - 1, :]).then_inc(out_written, 16)
            sp.dma_start(out[(TILES - 1) * P:, :], x[0:LAST, TILES - 1, :]).then_inc(out_written, 16)
            sp.wait_ge(out_written, 32)

        @block.gpsimd
        def _(pool):
            ok = dict(allow_small_or_imprecise_dtypes=True)
            pool.iota(iota[:], pattern=[[1, P]], base=0, channel_multiplier=0, **ok).then_inc(const_ready, 1)
            pool.iota(iota_rel[:], pattern=[[1, REL]], base=0, channel_multiplier=0, **ok).then_inc(const_ready, 1)
            pool.iota(iota_s[:], pattern=[[1, STEPS]], base=0, channel_multiplier=0, **ok).then_inc(const_ready, 1)
            pool.iota(part[:], pattern=[[0, 1]], base=0, channel_multiplier=1, **ok).then_inc(const_ready, 1)

            def gather(r, table, width):
                if r.kind == "rel":
                    r.table[0].wait(pool, 16 * (TILES - TILES // 2))
                    r.table[1].wait(pool, 16 * (TILES // 2))
                else:
                    r.table[0].wait(pool, 16)

                def body(i, q, peeled):
                    r.staged.wait(pool, i * 2 + (q + 1))
                    pool.sem_inc(gather_begun, 1)
                    for k in range(HALF):
                        pool.indirect_dma_start(
                            out=ring[:, q, k, 0:width], out_offset=None, in_=table,
                            in_offset=bass.IndirectOffsetOnAxis(ap=idx_now[:, q, k:k + 1], axis=0),
                        ).then_inc(r.gathered[q].sem, 16)
                halves(pool, body)

            for _, r in gats:
                gather(r, gat_table, D + HEADS)
            for _, r in rels:
                gather(r, rel_table, D)
            gather(gin, x_table, D)
            gather(wgin, x_table, D)

        @block.scalar
        def _(act):
            def stage_half(r, half, q):
                idx = rel_idx if r.kind == "rel" else src_idx
                act.copy(idx_now[:, q, :], idx[:, bass.ds(half * HALF, HALF)]).then_inc(r.staged.sem, 1)

            def table_written(r):
                if r.kind == "rel":
                    r.table[0].wait(act, 16 * (TILES - TILES // 2))
                    r.table[1].wait(act, 16 * (TILES // 2))
                else:
                    r.table[0].wait(act, 16)

            def project(pj, src):
                pj.inp.wait(act, 1)

                def body(i, peeled):
                    if not peeled:
                        pj.tr.wait(act, i)
                    act.copy(xs[:], src[:, bass.ds(i * 5, 5), :]).then_inc(pj.xs.sem, 1)
                    pj.tr.wait(act, i + 1)
                    if not peeled:
                        pj.mm.wait(act, i)
                    act.copy(xT[:, 0:4, :], ps[0:D, 5, :].rearrange("p (a n) -> p a n", a=4))
                    act.copy(xT[:, 4, :], ps[0:D, 6, 0:P]).then_inc(pj.xT.sem, 1)
                body(0, True)
                with act.Fori(1, 5) as i:
                    body(i, False)

            def sqrt(n, v):
                act.wait_ge(var_ready, n)
                act.activation(v, v, ACT.Sqrt).then_inc(std_ready, 1)

            act.wait_ge(edge_lists_ready, 1)
            for g in range(KG):
                act.wait_ge(keys_T, g + 1)
                act.copy(logit_T[:, g * P:(g + 1) * P], ps[:, 5 + g % 2, 0:P]).then_inc(keys_out, 1)
            for g in range(KG):
                act.wait_ge(starts, g + 1)
                act.copy(first.rearrange("p (k g) -> p k g", g=KG)[:, :, g],
                         ps[:, 5 + g % 2, 0:P].rearrange("p (k h) -> p k h", h=HEADS)[:, :, 0]).then_inc(starts_out, 1)

            for pj, r in gats:
                project(pj, x if r.layer == 0 else y)
                table_written(r)
                stage_half(r, 0, 0)

                def body(i, q, peeled, ahead=True):
                    if ahead:
                        if not (peeled and q == 0):
                            r.taken.wait(act, i * 2 + q)
                            r.spilled[1 - q].wait(act, i * 16 + q * 16)
                        stage_half(r, i * 2 + (q + 1), 1 - q)
                    for b in range(2):
                        r.turned.wait(act, i * 4 + (2 * q + b + 1))
                        if not peeled:
                            r.looked.wait(act, i * 2 + (q - 1))
                        act.copy(onehot_T[:, q, 4 * b:4 * b + 4, :],
                                 ps[:, 5 + b, :].rearrange("p (a n) -> p a n", a=4)).then_inc(r.turned_out.sem, 1)
                halves(act, body, ITERS - 1)
                body(ITERS - 1, 0, False)
                body(ITERS - 1, 1, False, ahead=False)
                for g in range(2 * KG):
                    dst = logit_T if g < KG else own_T
                    r.to_heads.wait(act, g + 1)
                    act.copy(dst[:, (g % KG) * P:(g % KG + 1) * P], ps[:, 5 + g % 2, 0:P])\
                       .then_inc(r.to_heads_out.sem, 1)
                r.less_max.wait(act, 1)
                act.activation(logit_T, logit_T, ACT.Exp).then_inc(r.exped.sem, 1)
                r.less_max.wait(act, 2)
                act.activation(own_T, own_T, ACT.Exp).then_inc(r.exped.sem, 1)
                for g in range(2 * KG):
                    dst = (logit if g < KG else own).rearrange("p (k g) h -> p k g h", g=KG)[:, :, g % KG, :]
                    r.to_edges.wait(act, g + 1)
                    act.copy(dst, ps[:, 5 + g % 2, 0:P].rearrange("p (k h) -> p k h", h=HEADS))\
                       .then_inc(r.to_edges_out.sem, 1)
            sqrt(1, small[:, 1, 0:TILES])

            def stage_all(r):
                table_written(r)
                stage_half(r, 0, 0)

                def body(i, q, peeled):
                    if not (peeled and q == 0):
                        r.summed.wait(act, i * 2 + q)
                    stage_half(r, i * 2 + (q + 1), 1 - q)
                halves(act, body, ITERS - 1)
                body(ITERS - 1, 0, False)

            for ex, r in rels:
                ex.inp.wait(act, 1)

                def body(t, slot, peeled):
                    if not (isinstance(t, int) and t == 0):
                        ex.tr.wait(act, t)
                    act.copy(xs[:, 0, :], (y if r.layer else x)[:, bass.ds(t, 1), :].squeeze(1)).then_inc(ex.xs.sem, 1)
                    ex.tr.wait(act, t + 1)
                    if not (isinstance(t, int) and t == 0):
                        ex.mm.wait(act, t * 9)
                    act.copy(xT[:, 0, :], ps[0:D, 7, 0:P]).then_inc(ex.xT.sem, 1)
                    if not peeled:
                        r.table[slot].wait(act, t * 8 - slot * 8)
                    for n in (1, 3, 5, 7):
                        ex.mm.wait(act, t * 9 + (n + 1))
                        act.copy(stage[:, slot, n * 512:(n + 1) * 512], ps[:, n % 7, :]).then_inc(ex.out_a.sem, 1)
                tiles_by_two(act, body)
                stage_all(r)
            sqrt(2, small[:, 1, 0:TILES])
            stage_all(gin)
            sqrt(3, small[:, 1, 0:TILES])
            stage_all(wgin)
            for l, pj in enumerate(bns):
                project(pj, y)
                sqrt(4 + l, st[:, 3, :])
            sqrt(6, small[:, 1, 0:TILES])

        @block.tensor
        def _(pe):
            def project(pj):
                pj.w.wait(pe, 64)

                def body(i, peeled):
                    pj.xs.wait(pe, i + 1)
                    if not peeled:
                        pj.xT.wait(pe, i)
                        pe.sem_inc(tile_begun, 1)
                    for k in range(5):
                        ins = pe.transpose(ps[0:D, 5 + k // 4, (k % 4) * P:(k % 4 + 1) * P], xs[:, k, :], ident[:])
                    ins.then_inc(pj.tr.sem, 1)
                    pj.xT.wait(pe, i + 1)
                    if not peeled:
                        pj.out.wait(pe, i)
                    for k in range(5):
                        ins = pe.matmul(ps[:, 7, k * D:(k + 1) * D], xT[:, k, :], wn[:], start=True, stop=True)
                    ins.then_inc(pj.mm.sem, 1)
                body(0, True)
                with pe.Fori(1, 5) as i:
                    body(i, False)

            def clear_sums():
                for b in range(BANKS):
                    pe.matmul(ps[:, b, :], zero[:, 0:P], zero[:], start=True, stop=False, skip_group_check=True)

            def places(i, q):
                return [pe.value_load(place[0:1, bass.ds(i * (2 * HALF) + (q * HALF + k), 1)],
                                      min_val=0, max_val=(BANKS - 1) * 512 + PITCH * PERBANK - 81) for k in range(HALF)]

            pe.wait_ge(ones_ready, 1)
            pe.wait_ge(ends_counted, 1)
            pe.matmul(ps[:, 7, 0:TILES - 1], ones[:], ends[:], start=True, stop=True).then_inc(ends_summed, 1)
            pe.wait_ge(picks_ready, 1)
            for q in range(4):
                for b in range(EB):
                    ins = pe.matmul(ps[:, q, 0:STEPS], lists[:, q, b, :], pick[:, b, :],
                                    start=b == 0, stop=b == EB - 1)
            ins.then_inc(picked, 1)
            pe.wait_ge(keys_ready, 1)
            for g in range(KG):
                if g >= 2:
                    pe.wait_ge(keys_out, g - 1)
                pe.transpose(ps[:, 5 + g % 2, 0:P], smax2[:, g * P:(g + 1) * P], ident[:]).then_inc(keys_T, 1)
            pe.wait_ge(keys_out, KG)
            pe.transpose(ps[0:1, 7, 0:P], logit_T[:, 0:1], ident[:])
            pe.transpose(ps[0:1, 7, P:2 * P], logit_T[:, SL - 1:SL], ident[:]).then_inc(key_rows, 1)
            pe.wait_ge(start_row, 1)
            pe.matmul(ps[:, 7, 2 * P:2 * P + 1], rows[:, 10, :], ones[0:1, 0:1], start=True, stop=True).then_inc(start_col, 1)
            pe.wait_ge(starts_T, 1)
            for g in range(KG):
                if g >= 2:
                    pe.wait_ge(starts_out, g - 1)
                pe.transpose(ps[:, 5 + g % 2, 0:P], own_T[:, g * P:(g + 1) * P], ident[:]).then_inc(starts, 1)

            for pj, r in gats:
                pe.wait_ge(starts_out, KG)
                project(pj)
                r.table_ready.wait(pe, 1)
                if r.layer == 0:
                    clear_sums()

                def look(i, q, peeled):
                    at = places(i, q)
                    r.hot.wait(pe, i * 2 + (q + 1))
                    for b in range(2):
                        if not (peeled and q == 0):
                            r.turned_out.wait(pe, i * 4 + (2 * q + b - 1))
                        for k in range(4 * b, 4 * b + 4):
                            ins = pe.transpose(ps[:, 5 + b, (k % 4) * P:(k % 4 + 1) * P], onehot[:, q, k, :], ident[:])
                        ins.then_inc(r.turned.sem, 1)
                    if r.layer == 0:
                        for k in range(HALF):
                            pe.matmul(flat[:, bass.ds(at[k], REL)], onehot[:, q, k, :], relhot[:, q, k, :],
                                      start=False, stop=False, skip_group_check=True)
                    if not peeled:
                        r.taken.wait(pe, i * 2 + (q - 1))
                    for k in range(HALF):
                        if k % 4 == 0:
                            r.turned_out.wait(pe, i * 4 + (2 * q + k // 4 + 1))
                        if r.layer == 1:
                            n, o = 2 * HEADS + REL, ps[:, 2 * q + k // PERBANK, (k % PERBANK) * PITCH:]
                        else:
                            n, o = 2 * HEADS, ps[:, 7, q * 256 + k * 2 * HEADS:]
                        ins = pe.matmul(o[:, 0:n], onehot_T[:, q, k, :], nodeq[:, bass.ds(at[k], n)],
                                        start=True, stop=True, skip_group_check=True)
                    ins.then_inc(r.looked.sem, 1)
                halves(pe, look)
                for g in range(2 * KG):
                    if g % KG == 0:
                        r.regrouped.wait(pe, 1 + g // KG)
                    if g >= 2:
                        r.to_heads_out.wait(pe, g - 1)
                    pe.transpose(ps[:, 5 + g % 2, 0:P], (smax if g < KG else smax2)[:, (g % KG) * P:(g % KG + 1) * P],
                                 ident[:]).then_inc(r.to_heads.sem, 1)
                r.scanned.wait(pe, 1)
                pe.transpose(ps[0:1, 7, 0:P], smax2[:, SL - 1:SL], ident[:])
                pe.transpose(ps[0:1, 7, P:2 * P], smax[:, 0:1], ident[:]).then_inc(r.ends_T.sem, 1)
                r.carried.wait(pe, 1)
                pe.matmul(ps[:, 7, 256:257], rows[:, 10, :], ones[0:1, 0:1], start=True, stop=True)
                pe.matmul(ps[:, 7, 257:258], rows[:, 11, :], ones[0:1, 0:1], start=True, stop=True)\
                  .then_inc(r.carries_T.sem, 1)
                for g in range(2 * KG):
                    if g % KG == 0:
                        r.exped.wait(pe, 1 + g // KG)
                    if g >= 2:
                        r.to_edges_out.wait(pe, g - 1)
                    pe.transpose(ps[:, 5 + g % 2, 0:P], (logit_T if g < KG else own_T)[:, (g % KG) * P:(g % KG + 1) * P],
                                 ident[:]).then_inc(r.to_edges.sem, 1)
                r.acc_clear.wait(pe, 1)
                clear_sums()

                def add(i, q, peeled):
                    at = places(i, q)
                    r.msgs.wait(pe, i * 2 + (q + 1))
                    for k in range(HALF):
                        ins = pe.matmul(flat[:, bass.ds(at[k], D + 2 * HEADS)], onehot[:, q, k, :], msg[:, q, k, :],
                                        start=False, stop=False, skip_group_check=True)
                    ins.then_inc(r.summed.sem, 1)
                halves(pe, add)

            def add_gathered(r, before):
                before.acc_read.wait(pe, 1)
                clear_sums()

                def add(i, q, peeled):
                    at = places(i, q)
                    r.hot.wait(pe, i * 2 + (q + 1))
                    r.gathered[q].wait(pe, i * (16 * HALF) + 16 * HALF)
                    for k in range(HALF):
                        ins = pe.matmul(flat[:, bass.ds(at[k], D)], onehot[:, q, k, :], ring[:, q, k, 0:D],
                                        start=False, stop=False, skip_group_check=True)
                    ins.then_inc(r.summed.sem, 1)
                halves(pe, add)

            for ex, r in rels:
                before = rels[0][1] if r.layer else gats[2][1]
                before.acc_read.wait(pe, 1)
                ex.w.wait(pe, 16 * (REL // 13 + 4))

                def body(t, slot, peeled):
                    zeroth = isinstance(t, int) and t == 0
                    ex.xs.wait(pe, t + 1)
                    pe.sem_inc(tile_begun, 1)
                    pe.transpose(ps[0:D, 7, 0:P], xs[:, 0, :], ident[:]).then_inc(ex.tr.sem, 1)
                    ex.xT.wait(pe, t + 1)
                    for n in range(9):
                        if n == 0 and not zeroth:
                            ex.out_a.wait(pe, t * 4)
                        if n == 1 and not zeroth:
                            ex.out_v.wait(pe, t * 6)
                        if n == 7:
                            ex.out_v.wait(pe, t * 6 + 1)
                        if n == 8:
                            ex.out_a.wait(pe, t * 4 + 1)
                        m = min(512, CW * D - n * 512)
                        pe.matmul(ps[:, n % 7, 0:m], xT[:, 0, :], rel_w[:, n * 512:n * 512 + m],
                                  start=True, stop=True).then_inc(ex.mm.sem, 1)
                tiles_by_two(pe, body)
                ex.out_v.wait(pe, 6 * TILES)
                ex.out_a.wait(pe, 4 * TILES)
                add_gathered(r, before)
            add_gathered(gin, rels[1][1])
            add_gathered(wgin, gin)
            for l, pj in enumerate(bns):
                project(pj)
                for n in range(2):
                    pe.wait_ge(bn_part, 2 * l + n + 1)
                    pe.matmul(ps[:, 6, 256 + n * D:256 + (n + 1) * D], ones[:], st[:, 2 * n, :], start=True, stop=True)\
                      .then_inc(bn_total, 1)

        @block.vector
        def _(v):
            own_order = Order(v, v_own)
            then, done, wait = own_order.then, own_order.done, own_order.wait
            wide = [P, TILES, D]

            done(v.memset(x[:, TILES - 1, :], 0.0))
            done(v.memset(raw[:, 0], int(NEVER)))
            done(v.memset(raw[:, 1:3], 0))
            done(v.memset(lists[:, 3], 0.0))
            wait()
            v.memset(zero[:], 0.0).then_inc(pads_set, 1)
            done(v.memset(ones[:], 1.0))
            done(v.memset(tile_of[:], 0.0))
            done(v.memset(joins[:, 0:1], -BIG))
            done(v.memset(joins[:, SL:SL + 1], -BIG))
            done(v.memset(rows[:], -BIG))
            done(v.memset(nodeq[:], 0.0))
            v.wait_ge(const_ready, 4)
            then(v.tensor_scalar(ident[:], iota[:], part[:, 0:1], None, ALU.is_equal))
            v.memset(ends[:], 0.0).then_inc(ones_ready, 1)

            v.wait_ge(lists_loaded, 16 * 12)
            done(v.tensor_copy(lists[:, 0:2], raw[:, 0:2]))
            then(v.scalar_tensor_tensor(lists[:, 2], raw[:, 1], float(REL), raw[:, 2], ALU.mult, ALU.add))
            dsts = lists[:, 0].rearrange("p b e -> p (b e)")
            below = msg[:].rearrange("p a b c -> p (a b c)")[:, 0:EB * P]
            for t in range(TILES - 1):
                then(v.tensor_scalar(below, dsts, float((t + 1) * P), None, ALU.is_lt))
                then(v.tensor_reduce(ends[:, t:t + 1], below, X, ALU.add))
            v.sem_inc(ends_counted, 1)
            v.wait_ge(ends_summed, 1)
            then(v.tensor_scalar(ends[:], ps[:, 7, 0:TILES - 1], 1.0 / P, CHUNKS - 0.5, ALU.mult, ALU.min))
            then(v.tensor_tensor(ends[:], ends[:], iota[:, 0:TILES - 1], ALU.add))
            for t in range(TILES - 1):
                then(v.scalar_tensor_tensor(tile_of[:], iota_s[:], ends[:, t:t + 1], tile_of[:], ALU.is_gt, ALU.add))
            then(v.tensor_scalar(tmp_s[:], tile_of[:], float(PITCH), None, ALU.mult))
            for b in range(1, BANKS):
                then(v.tensor_scalar(tmp_s2[:], tile_of[:], float(PERBANK * b), float(512 - PERBANK * PITCH),
                                     ALU.is_ge, ALU.mult))
                then(v.tensor_tensor(tmp_s[:], tmp_s[:], tmp_s2[:], ALU.add))
            then(v.tensor_copy(place[:], tmp_s[0:1, :]))
            then(v.tensor_tensor(tmp_s2[:], iota_s[:], tile_of[:], ALU.subtract))
            for b in range(EB):
                then(v.tensor_scalar(pick[:, b, :], tmp_s2[:], part[:, 0:1], float(b * P), ALU.subtract, ALU.is_equal))
            v.sem_inc(picks_ready, 1)

            v.wait_ge(picked, 1)
            dst_ps, src_ps, rel_ps, w_ps = (ps[:, q, 0:STEPS] for q in range(4))
            then(v.scalar_tensor_tensor(node_of[:], tile_of[:], -float(P), dst_ps, ALU.mult, ALU.add))
            then(v.tensor_scalar(tmp_s[:], node_of[:], 0.0, None, ALU.is_ge))
            then(v.scalar_tensor_tensor(tmp_s2[:], node_of[:], float(P), tmp_s[:], ALU.is_lt, ALU.mult))
            then(v.scalar_tensor_tensor(key[:], dst_ps, 1.0, tmp_s2[:], ALU.add, ALU.mult))
            then(v.tensor_scalar(key[:], key[:], -1.0, None, ALU.add))
            then(v.tensor_copy(tmp_s[:], src_ps))
            done(v.scalar_tensor_tensor(rel_of[:], tmp_s[:], -float(REL), rel_ps, ALU.mult, ALU.add))
            done(v.tensor_copy(src_idx[:], src_ps))
            done(v.tensor_copy(rel_idx[:], rel_ps))
            done(v.tensor_copy(weight[:], w_ps))
            apart = lambda m: m.rearrange("p (g k h) -> p g k h", k=KB, h=HEADS)
            then(v.tensor_copy(apart(smax2), key[:].rearrange("p (k g) -> p g k", g=KG).unsqueeze(3)
                               .broadcast_to([P, KG, KB, HEADS])))
            v.sem_inc(keys_ready, 1)
            v.sem_inc(edge_lists_ready, 1)

            v.wait_ge(keys_out, KG)
            flags = smax
            for o, i0, i1 in ((joins[:, 1:SL], logit_T[:, 1:SL], logit_T[:, 0:SL - 1]),
                              (in_first[:], logit_T, None), (in_last[:], logit_T, None)):
                f = flags[:, 0:o.shape[1]]
                if i1 is not None:
                    then(v.tensor_tensor(f, i0, i1, ALU.is_equal))
                else:
                    at = 0 if o.name == in_first[:].name else SL - 1
                    then(v.tensor_scalar(f, i0, logit_T[:, at:at + 1], None, ALU.is_equal))
                then(v.tensor_scalar(o, f, -1.0, BIG, ALU.add, ALU.mult))
            row = lambda n: rows[:, n, :].rearrange("p (h k) -> p h k", h=HEADS)
            row_kh = lambda n: rows[:, n, :].rearrange("p (k h) -> p h k", h=HEADS)
            ps_row = lambda n: ps[0:1, 7, n * P:(n + 1) * P].rearrange("p (k h) -> p h k", h=HEADS)
            v.wait_ge(key_rows, 1)
            done(v.tensor_copy(row(0), ps_row(0)))
            then(v.tensor_copy(row(1), ps_row(1)))
            then(v.tensor_tensor(row(2)[:, :, 1:], row(0)[:, :, 1:], row(1)[:, :, 0:KB - 1], ALU.is_equal))
            then(v.tensor_scalar(row(2)[:, :, 1:], row(2)[:, :, 1:], -1.0, BIG, ALU.add, ALU.mult))
            then(v.tensor_tensor(row(3), row(0), row(1), ALU.is_equal))
            then(v.tensor_scalar(row(3), row(3), -1.0, BIG, ALU.add, ALU.mult))
            done(v.tensor_tensor(row(4), row(2), row(3), ALU.min))
            done(v.tensor_tensor(row(5)[:, :, 0:KB - 1], row(2)[:, :, 1:], row(3)[:, :, 0:KB - 1], ALU.min))
            then(v.tensor_copy(row_kh(10), row(2)))
            v.sem_inc(start_row, 1)
            done(v.tensor_scalar(own_T, joins[:, 0:SL], -1.0, None, ALU.is_lt))
            v.wait_ge(start_col, 1)
            wait()
            then(v.tensor_scalar(own_T[:, 0:1], ps[:, 7, 2 * P:2 * P + 1], -1.0, None, ALU.is_lt))
            v.sem_inc(starts_T, 1)

            def one_hots(at, q, scale=None):
                for k in range(HALF):
                    c = lambda m: m[:, bass.ds(at + k, 1)]
                    if scale is None:
                        ins = v.tensor_scalar(onehot[:, q, k, :], iota[:], c(node_of), None, ALU.is_equal)
                    else:
                        ins = v.tensor_scalar(onehot[:, q, k, :], iota[:], c(node_of), c(scale),
                                              ALU.is_equal, ALU.mult)
                return ins

            def project(pj, dst, bias=None):
                pj.w.wait(v, 64)

                def body(i):
                    pj.mm.wait(v, i + 1)
                    o = dst[:, bass.ds(i * 5, 5), :]
                    p = ps[:, 7, 0:5 * D].rearrange("p (a f) -> p a f", f=D)
                    if bias is None:
                        v.tensor_copy(o, p).then_inc(pj.out.sem, 1)
                    else:
                        v.tensor_tensor(o, p, bias.unsqueeze(1).broadcast_to([P, 5, D]), ALU.add).then_inc(pj.out.sem, 1)
                with v.Fori(0, 5) as i:
                    body(i)
                pj.out.wait(v, 5)

            def layernorm(n):
                s = small[:, :, 0:TILES]
                cent = w1[:]
                then(v.tensor_reduce(s[:, 0], w1[:], X, ALU.add))
                then(v.tensor_scalar(s[:, 0], s[:, 0], 1.0 / D, None, ALU.mult))
                then(v.tensor_tensor(cent, w1[:], s[:, 0].unsqueeze(2).broadcast_to(wide), ALU.subtract))
                then(v.tensor_tensor(w2[:], cent, cent, ALU.mult))
                then(v.tensor_reduce(s[:, 1], w2[:], X, ALU.add))
                v.tensor_scalar(s[:, 1], s[:, 1], 1.0 / D, EPS, ALU.mult, ALU.add).then_inc(var_ready, 1)
                v.wait_ge(std_ready, n)
                then(v.reciprocal(s[:, 2], s[:, 1]))
                then(v.tensor_tensor(x[:], cent, s[:, 2].unsqueeze(2).broadcast_to(wide), ALU.mult))

            def read_sums(r, dst, n):
                r.summed.wait(v, HV)
                for b in range(BANKS):
                    m, ts = of_bank(flat, b, 0, n)
                    done(v.tensor_copy(dst[:, ts, 0:n], m))
                wait()
                v.sem_inc(r.acc_read.sem, 1)

            v.wait_ge(loaded, 48)
            h_of, as_of = ht[:, :, 0:D], ht[:, :, D:D + HEADS]
            sm = [small[:, k, :].rearrange("p (t h) -> p t h", h=HEADS) for k in range(6)]
            for pj, r in gats:
                v.sem_inc(pj.inp.sem, 1)
                project(pj, h_of)
                for k, o in ((0, as_of), (1, sm[0])):
                    then(v.tensor_tensor(w1[:], h_of, vecs[:, k, :].unsqueeze(1).broadcast_to(wide), ALU.mult))
                    then(v.tensor_reduce(o, w1[:].rearrange("p t (h c) -> p t h c", c=C), X, ALU.add))
                then(v.tensor_tensor(sm[1], as_of, sm[0], ALU.add))
                then(v.scalar_tensor_tensor(sm[2], sm[1], 0.2, sm[1], ALU.mult, ALU.max))
                for b in range(BANKS):
                    m, ts = of_bank(nodeq, b, 0, HEADS)
                    done(v.tensor_copy(m, sm[0][:, ts, :]))
                    m, ts = of_bank(nodeq, b, HEADS, HEADS)
                    done(v.tensor_copy(m, sm[2][:, ts, :]))
                wait()
                v.sem_inc(r.table_ready.sem, 1)

                per = 4 if r.layer != 1 else 9

                def take(i, q, peeled):
                    at = i * (2 * HALF) + q * HALF
                    if not peeled:
                        r.looked.wait(v, i * 2 + (q - 1))
                    ins = one_hots(at, q)
                    if r.layer < 2:
                        done(ins)
                        ins = v.tensor_tensor(relhot[:, q], rel_of[:, bass.ds(at, HALF)].unsqueeze(2).broadcast_to([P, HALF, REL]),
                                              iota_rel[:].unsqueeze(1).broadcast_to([P, HALF, REL]), ALU.is_equal)
                    ins.then_inc(r.hot.sem, 1)
                    r.looked.wait(v, i * 2 + (q + 1))
                    r.gathered[q].wait(v, i * (16 * HALF) + 16 * HALF)
                    if r.layer == 1:
                        pieces = [(k, min(PERBANK, HALF - k), ps[:, 2 * q + k // PERBANK, 0:PERBANK * PITCH]
                                   .rearrange("p (s c) -> p s c", c=PITCH)) for k in range(0, HALF, PERBANK)]
                    else:
                        pieces = [(0, HALF, ps[:, 7, q * 256:q * 256 + HALF * 2 * HEADS]
                                   .rearrange("p (s c) -> p s c", c=2 * HEADS))]
                    for k, n, g in pieces:
                        s = bass.ds(at + k, n)
                        done(v.tensor_tensor(gz[:, k:k + n], ring[:, q, k:k + n, D:D + HEADS], g[:, 0:n, 0:HEADS], ALU.add))
                        if r.layer == 1:
                            r.hot.wait(v, i * 2 + (q + 1))
                            done(v.tensor_tensor(relsel[:, k:k + n], relhot[:, q, k:k + n],
                                                 g[:, 0:n, 2 * HEADS:2 * HEADS + REL], ALU.mult))
                            wait()
                            done(v.tensor_reduce(count[:, s], relsel[:, k:k + n], X, ALU.add))
                        wait()
                        done(v.scalar_tensor_tensor(logit[:, s, :], gz[:, k:k + n], 0.2, gz[:, k:k + n], ALU.mult, ALU.max))
                        ins = v.tensor_copy(own[:, s, :], g[:, 0:n, HEADS:2 * HEADS])
                        if k + n < HALF:
                            done(ins)
                        else:
                            ins.then_inc(r.taken.sem, 1)
                per_half = {0: 3, 1: 1 + 4 * 2 + 1, 2: 2}[r.layer]
                take(0, 0, True)
                take(0, 1, True)
                with v.Fori(1, ITERS) as i, own_order.loop(i, 1, ITERS, 2 * per_half):
                    take(i, 0, False)
                    take(i, 1, False)
                wait()
                if r.layer == 0:
                    for b in range(BANKS):
                        m, ts = of_bank(flat, b, 0, REL)
                        done(v.tensor_copy(of_bank(nodeq, b, 2 * HEADS, REL)[0], m))
                    wait()
                if r.layer == 1:
                    then(v.tensor_scalar(count[:], count[:], 1.0, None, ALU.max))
                    then(v.reciprocal(count[:], count[:]))
                v.sem_inc(r.acc_clear.sem, 1)
                v.tensor_copy(apart(smax), logit.rearrange("p (k g) h -> p g k h", g=KG)).then_inc(r.regrouped.sem, 1)
                r.regrouped.wait(v, 1)
                v.tensor_copy(apart(smax2), own.rearrange("p (k g) h -> p g k h", g=KG)).then_inc(r.regrouped.sem, 1)

                r.to_heads_out.wait(v, 2 * KG)
                then(v.tensor_tensor(smax, logit_T, own_T, ALU.max))
                then(v.tensor_tensor_scan(smax2, joins[:, 0:SL], smax, -BIG, ALU.add, ALU.max))
                then(v.tensor_tensor_scan(smax[:, ::-1], joins[:, 1:SL + 1][:, ::-1], smax2[:, ::-1], -BIG, ALU.add, ALU.max))
                v.sem_inc(r.scanned.sem, 1)
                r.ends_T.wait(v, 1)
                done(v.tensor_copy(row(6), ps_row(0)))
                then(v.tensor_copy(row(7), ps_row(1)))
                done(v.tensor_tensor_scan(rows[:, 8, :], rows[:, 4, :], rows[:, 6, :], -BIG, ALU.add, ALU.max))
                then(v.tensor_tensor_scan(rows[:, 9, ::-1], rows[:, 5, ::-1], rows[:, 7, ::-1], -BIG, ALU.add, ALU.max))
                done(v.tensor_tensor(row_kh(10)[:, :, 1:], row(8)[:, :, 0:KB - 1], row(2)[:, :, 1:], ALU.add))
                then(v.tensor_tensor(row_kh(11)[:, :, 0:KB - 1], row(9)[:, :, 1:], row(2)[:, :, 1:], ALU.add))
                v.sem_inc(r.carried.sem, 1)
                r.carries_T.wait(v, 1)
                then(v.tensor_copy(cols[:], ps[:, 7, 256:258]))
                then(v.scalar_tensor_tensor(smax, in_first[:], cols[:, 0:1], smax, ALU.add, ALU.max))
                then(v.scalar_tensor_tensor(smax, in_last[:], cols[:, 1:2], smax, ALU.add, ALU.max))
                v.tensor_tensor(logit_T, logit_T, smax, ALU.subtract).then_inc(r.less_max.sem, 1)
                v.tensor_tensor(own_T, own_T, smax, ALU.subtract).then_inc(r.less_max.sem, 1)
                r.to_edges_out.wait(v, 2 * KG)
                v.wait_ge(starts_out, KG)
                then(v.tensor_tensor(own, own, first[:].unsqueeze(2).broadcast_to([P, STEPS, HEADS]), ALU.mult))

                def weigh(i, q, peeled):
                    at = i * (2 * HALF) + q * HALF
                    if not peeled:
                        r.summed.wait(v, i * 2 + (q - 1))
                    one_hots(at, q)
                    v.tensor_copy(msg[:, q, :, D:D + HEADS], logit[:, bass.ds(at, HALF), :])
                    v.tensor_copy(msg[:, q, :, D + HEADS:D + 2 * HEADS], own[:, bass.ds(at, HALF), :])
                    r.back[q].wait(v, i * 16 + 16)
                    v.tensor_tensor(msg[:, q, :, 0:D].rearrange("p s (h c) -> p s h c", c=C),
                                    ring[:, q, :, 0:D].rearrange("p s (h c) -> p s h c", c=C),
                                    logit[:, bass.ds(at, HALF), :].unsqueeze(3).broadcast_to([P, HALF, HEADS, C]),
                                    ALU.mult).then_inc(r.msgs.sem, 1)
                halves(v, weigh)

                read_sums(r, u, D + 2 * HEADS)
                ex, exs = u[:, :, D:D + HEADS], u[:, :, D + HEADS:D + 2 * HEADS]
                then(v.tensor_tensor(sm[0], ex, exs, ALU.add))
                then(v.tensor_scalar(sm[1], sm[0], 0.5, None, ALU.is_lt))
                then(v.tensor_tensor(sm[2], exs, sm[1], ALU.add))
                then(v.tensor_tensor(sm[3], ex, sm[2], ALU.add))
                then(v.tensor_scalar(sm[3], sm[3], 1e-16, None, ALU.add))
                done(v.reciprocal(sm[4], sm[3]))
                w1h, w2h = (m[:].rearrange("p t (h c) -> p t h c", c=C) for m in (w1, w2))
                then(v.tensor_tensor(w1h, h_of.rearrange("p t (h c) -> p t h c", c=C), per_head(sm[2]), ALU.mult))
                then(v.tensor_tensor(w1[:], w1[:], u[:, :, 0:D], ALU.add))
                then(v.tensor_tensor(w2h, w1h, per_head(sm[4]), ALU.mult))
                then(v.tensor_tensor(y[:], w2[:], vecs[:, 2, :].unsqueeze(1).broadcast_to(wide), ALU.add))
                if r.layer < 2:
                    then(v.tensor_scalar(y[:], y[:], 0.0, None, ALU.max))
                v.sem_inc(r.finished.sem, 1)
            then(v.tensor_tensor(w1[:], x[:], y[:], ALU.add))
            layernorm(1)

            def sum_round(r, scale):
                def body(i, q, peeled):
                    at = i * (2 * HALF) + q * HALF
                    if not peeled:
                        r.summed.wait(v, i * 2 + (q - 1))
                    one_hots(at, q, scale).then_inc(r.hot.sem, 1)
                halves(v, body)
                read_sums(r, u, D)

            for ex_, r in rels:
                v.sem_inc(ex_.inp.sem, 1)

                def body(t, slot, peeled):
                    if not peeled:
                        r.table[slot].wait(v, t * 8 - slot * 8)
                    for n in (0, 2, 4, 6):
                        ex_.mm.wait(v, t * 9 + (n + 1))
                        v.tensor_copy(stage[:, slot, n * 512:(n + 1) * 512], ps[:, n % 7, :]).then_inc(ex_.out_v.sem, 1)
                    ex_.mm.wait(v, t * 9 + 9)
                    v.tensor_copy(stage[:, slot, 8 * 512:REL * D], ps[:, 1, 0:REL * D - 8 * 512]).then_inc(ex_.out_v.sem, 1)
                    v.tensor_copy(rr[:, bass.ds(t, 1), :].squeeze(1), ps[:, 1, REL * D - 8 * 512:CW * D - 8 * 512])\
                     .then_inc(ex_.out_v.sem, 1)
                tiles_by_two(v, body)
                sum_round(r, count)
                ex_.w.wait(v, 16 * (REL // 13 + 4))
                bias = lambda k: vecs[:, k, :].unsqueeze(1).broadcast_to(wide)
                then(v.tensor_tensor(w1[:], u[:, :, 0:D], rr[:, :, 0:D], ALU.add))
                done(v.tensor_tensor(w2[:], rr[:, :, D:2 * D], bias(1), ALU.add))
                then(v.tensor_tensor(w1[:], w1[:], bias(0), ALU.add))
                then(v.tensor_scalar(w2[:], w2[:], 0.0, None, ALU.max))
                then(v.scalar_tensor_tensor(y[:], w1[:], 0.0, w2[:], ALU.max, ALU.add))
                v.sem_inc(r.finished.sem, 1)
            then(v.tensor_tensor(w1[:], x[:], y[:], ALU.add))
            layernorm(2)

            v.sem_inc(gin.table_ready.sem, 1)
            sum_round(gin, None)
            then(v.tensor_scalar(small[:, 0, 0:1], eps1[:, 0:1], 1.0, None, ALU.add))
            then(v.scalar_tensor_tensor(w2[:], x[:], small[:, 0, 0:1], u[:, :, 0:D], ALU.mult, ALU.add))
            then(v.tensor_tensor(w1[:], x[:], w2[:], ALU.add))
            layernorm(3)

            v.sem_inc(wgin.table_ready.sem, 1)
            sum_round(wgin, weight)
            then(v.tensor_tensor(y[:], u[:, :, 0:D], x[:], ALU.add))
            then(v.tensor_scalar(cols[:, 0:1], part[:, 0:1], float(LAST), None, ALU.is_lt))
            for l, pj in enumerate(bns):
                v.sem_inc(pj.inp.sem, 1)
                project(pj, w1, vecs[:, 0, :])
                every_tile = lambda m: m.unsqueeze(1).broadcast_to(wide)
                last = w1[:, TILES - 1, :]
                then(v.tensor_scalar(last, last, cols[:, 0:1], None, ALU.mult))
                then(v.tensor_reduce(st[:, 0, :], w1[:].rearrange("p t f -> p f t"), X, ALU.add))
                v.sem_inc(bn_part, 1)
                v.wait_ge(bn_total, 2 * l + 1)
                then(v.tensor_scalar(st[:, 1, :], ps[:, 6, 256:256 + D], 1.0 / NODES, None, ALU.mult))
                then(v.tensor_tensor(w1[:], w1[:], every_tile(st[:, 1, :]), ALU.subtract))
                then(v.tensor_scalar(last, last, cols[:, 0:1], None, ALU.mult))
                then(v.tensor_tensor(w2[:], w1[:], w1[:], ALU.mult))
                then(v.tensor_reduce(st[:, 2, :], w2[:].rearrange("p t f -> p f t"), X, ALU.add))
                v.sem_inc(bn_part, 1)
                v.wait_ge(bn_total, 2 * l + 2)
                v.tensor_scalar(st[:, 3, :], ps[:, 6, 256 + D:256 + 2 * D], 1.0 / NODES, EPS, ALU.mult, ALU.add)\
                 .then_inc(var_ready, 1)
                v.wait_ge(std_ready, 4 + l)
                then(v.reciprocal(st[:, 4, :], st[:, 3, :]))
                then(v.tensor_tensor(st[:, 5, :], st[:, 4, :], vecs[:, 1, :], ALU.mult))
                then(v.tensor_tensor(w2[:], w1[:], every_tile(st[:, 5, :]), ALU.mult))
                then(v.tensor_tensor(w2[:], w2[:], every_tile(vecs[:, 2, :]), ALU.add))
                then(v.tensor_scalar(y[:], w2[:], 0.0, None, ALU.max))
                v.sem_inc(bn_done, 1)
            then(v.tensor_tensor(w1[:], x[:], y[:], ALU.add))
            layernorm(6)
            v.sem_inc(x_final, 1)


_INS = (["x", "src", "dst", "edge_type_65", "edge_weight"]
        + [f"L0_gnn_{n}{l}" for l in (1, 2, 3) for n in ("W", "a_src", "a_dst", "b")]
        + [f"L1_gnn_{n}" for n in ("W", "root", "bias", "res_W", "res_b")] + ["L2_gnn_eps"]
        + [f"L3_gnn_{n}{l}" for l in (1, 2) for n in ("W", "b", "gamma", "beta")])


def kernel(**inputs):
    import numpy as _np
    import concourse.bacc as _bacc
    from concourse import mybir as _mybir
    from concourse.bass_utils import run_bass_kernel_spmd as _run

    nc = _bacc.Bacc("TRN2", target_bir_lowering=False, num_devices=1)
    arrays, args = {}, {}
    for name in _INS:
        v = _np.ascontiguousarray(inputs[name])
        arrays[f"in_{name}"] = v
        args[name] = nc.dram_tensor(f"in_{name}", v.shape, _mybir.dt.from_np(v.dtype), kind="ExternalInput").ap()
    out = nc.dram_tensor("out_0", (NODES, D), F32, kind="ExternalOutput").ap()
    build(nc, args, out)
    r = _run(nc, [arrays], core_ids=[0])
    return r.results[0]["out_0"]
```

```python
from contextlib import ExitStack, contextmanager

import concourse.bass as bass
from concourse import mybir

F32 = mybir.dt.float32
I32 = mybir.dt.int32
BF16 = mybir.dt.bfloat16
ALU = mybir.AluOpType
ACT = mybir.ActivationFunctionType
X = mybir.AxisListType.X

P = 128
NODES, D = 3125, 64
EDGES = 50000
HEADS, C = 8, 8
REL = 65
TILES = -(-NODES // P)
LAST = NODES - (TILES - 1) * P
CHUNKS = -(-EDGES // P)
EB = -(-CHUNKS // P)
STEPS = CHUNKS + TILES
HALF = 8
ITERS = STEPS // (2 * HALF)
KB = 16
KG = STEPS // KB
SL = KG * P
PITCH, PERBANK = 84, 6
BANKS = -(-TILES // PERBANK)
CW = REL + 2
NEVER = 4000.0
BIG = 1.0e30
EPS = 1e-5
assert STEPS == 2 * HALF * ITERS == KB * KG and KB * HEADS == P


class Signal:

    def __init__(self, sem, base=0):
        self.sem, self.base = sem, base

    def wait(self, eng, count):
        eng.wait_ge(self.sem, count + self.base)


class Order:

    def __init__(self, eng, sem):
        self.eng, self.sem, self.total, self.loop_at = eng, sem, 0, None

    def done(self, ins):
        ins.then_inc(self.sem, 1)
        self.total += 1

    def wait(self):
        if self.loop_at is None:
            self.eng.wait_ge(self.sem, self.total)
        else:
            reg, first, per, base = self.loop_at
            self.eng.wait_ge(self.sem, reg * per + (self.total - first * per))

    def then(self, ins):
        self.done(ins)
        self.wait()

    @contextmanager
    def loop(self, reg, first, last, per):
        base = self.total
        self.loop_at = (reg, first, per, base)
        yield
        assert self.total == base + per, (self.total - base, per)
        self.total = base + (last - first) * per
        self.loop_at = None


def build(nc, a, out):
    with ExitStack() as ctx:
        def sb(name, shape, dt=F32):
            return ctx.enter_context(nc.sbuf_tensor(name, shape, dt))

        def sem(name):
            return ctx.enter_context(nc.semaphore(name))

        def dram(name, shape, dt=F32):
            return nc.dram_tensor(name, shape, dt).ap()

        arena = sb("arena", [P, 5 * SL])
        raw = arena[:, 0:4 * EB * P].bitcast(I32).rearrange("p (q b e) -> p q b e", q=4, b=EB)
        lists = arena[:, 4 * EB * P:8 * EB * P].rearrange("p (q b e) -> p q b e", q=4, b=EB)
        pick = arena[:, 8 * EB * P:8 * EB * P + EB * STEPS].rearrange("p (b s) -> p b s", b=EB)
        logit = arena[:, 0:SL].rearrange("p (s h) -> p s h", h=HEADS)
        own = arena[:, SL:2 * SL].rearrange("p (s h) -> p s h", h=HEADS)
        logit_T, own_T = arena[:, 2 * SL:3 * SL], arena[:, 3 * SL:4 * SL]
        smax, smax2 = arena[:, 4 * SL:5 * SL], arena[:, 0:SL]
        stage = arena[:, 0:2 * REL * D].rearrange("p (s c) -> p s c", s=2)
        w_full = arena[:, 0:CW * D]
        w_part = [arena[:, 2 * REL * D + n * CW * D // 2:2 * REL * D + (n + 1) * CW * D // 2].bitcast(BF16)
                  for n in range(3)]

        ring = sb("ring", [P, 2, HALF, D + HEADS])
        onehot = sb("onehot", [P, 2, HALF, P])
        onehot_h = sb("onehot_h", [P, 2, HALF, P], BF16)
        onehot_T = sb("onehot_T", [P, 2, HALF, P], BF16)
        msg = sb("msg", [P, 2, HALF, D + 2 * HEADS])
        relhot = sb("relhot", [P, 2, HALF, REL], BF16)
        relsel = msg[:].rearrange("p a s c -> p (a s c)")[:, 0:2 * HALF * REL].rearrange("p (a s c) -> p a s c", a=2, c=REL)
        gz = sb("gz", [P, 2, HALF, HEADS])
        idx_now = sb("idx_now", [P, 2, HALF], I32)
        nodeq = sb("nodeq", [P, 3, BANKS * 512], BF16)
        gat_nodes = sb("gat_nodes", [P, TILES * (2 * D + 3 * HEADS)])
        ht = gat_nodes[:, 0:TILES * (D + HEADS)].rearrange("p (t c) -> p t c", t=TILES)
        u = gat_nodes[:, TILES * (D + HEADS):].rearrange("p (t c) -> p t c", t=TILES)
        x3 = gat_nodes[:, 0:TILES * 3 * D // 2].bitcast(BF16).rearrange(
            "p (t c) -> p t c", t=TILES)
        x = sb("x", [P, TILES, D])
        y = sb("y", [P, TILES, D])
        w1 = sb("w1", [P, TILES, D])
        w2 = sb("w2", [P, TILES, D])
        small = sb("small", [P, 6, TILES * HEADS])
        iota = sb("iota", [P, P])
        ident = sb("ident", [P, P])
        iota_h = sb("iota_h", [P, P], BF16)
        ident_h = sb("ident_h", [P, P], BF16)
        ones = sb("ones", [P, P])
        iota_rel = sb("iota_rel", [P, REL])
        iota_s = onehot[:].rearrange("p a s n -> p (a s n)")[:, 0:STEPS]
        part = sb("part", [P, 1])
        zero = sb("zero", [1, P])
        node_of = sb("node_of", [P, STEPS])
        key = msg[:].rearrange("p a s c -> p (a s c)")[:, EB * P:EB * P + STEPS]
        rel_of = sb("rel_of", [P, STEPS])
        weight = sb("weight", [P, STEPS])
        count = sb("count", [P, STEPS])
        first = sb("first", [P, STEPS])
        tile_of = sb("tile_of", [P, STEPS])
        tmp_s, tmp_s2 = (onehot_h[:].rearrange("p a s n -> p (a s n)").bitcast(F32)[:, n * STEPS:(n + 1) * STEPS]
                         for n in range(2))
        src_idx = sb("src_idx", [P, STEPS], I32)
        rel_idx = sb("rel_idx", [P, STEPS], I32)
        place = sb("place", [1, STEPS], I32)
        ends = sb("ends", [P, TILES - 1])
        joins = sb("joins", [P, SL + 1], BF16)
        in_first = sb("in_first", [P, SL], BF16)
        in_last = sb("in_last", [P, SL], BF16)
        rows = sb("rows", [1, 12, P])
        cols = sb("cols", [P, 2])
        wn = sb("wn", [D, D])
        vecs = sb("vecs", [P, 4, D])
        eps1 = sb("eps1", [P, 1])
        xs = sb("xs", [P, 5, D])
        xT = sb("xT", [D, 5, P])
        x3s = sb("x3s", [P, 3 * D], BF16)
        x3T = sb("x3T", [P, 2, 2, P], BF16)
        st = sb("st", [P, 8, D])
        ps = ctx.enter_context(nc.psum_tensor("ps", [P, 8, 512], F32))
        flat = ps[:].rearrange("p b n -> p (b n)")

        gat_table = dram("gat_table", [TILES * P, D + HEADS])
        x_table = dram("x_table", [TILES * P, D])
        rel_table = dram("rel_table", [TILES * P * REL, D])
        spill = dram("spill", [P, STEPS, D + HEADS])

        rr = nodeq[:].rearrange("p a n -> p (a n)").bitcast(F32)[:, 0:TILES * 2 * D].rearrange(
            "p (t c) -> p t c", t=TILES)

        x3_ps = ps[:, 7, 0:P].bitcast(BF16).rearrange("p (a n) -> p a n", a=2)

        turned_ps = ps[:, 5, :].bitcast(BF16).rearrange("p (k n) -> p k n", k=HALF)

        def per_head(ap):
            return ap.unsqueeze(3).broadcast_to([P, ap.shape[1], HEADS, C])

        def of_bank(m, b, col, n):
            k = min(PERBANK, TILES - b * PERBANK)
            v = m[:, b * 512:b * 512 + k * PITCH].rearrange("p (t c) -> p t c", c=PITCH)
            return v[:, :, col:col + n], slice(b * PERBANK, b * PERBANK + k)

        HV = 2 * ITERS
        shared = {}

        def signal(name, base=0):
            if name not in shared:
                shared[name] = sem(name)
            return Signal(shared[name], base)

        class Round:

            def __init__(self, n, name, kind, layer=0):
                self.kind, self.layer = kind, layer
                self.table_ready = signal("table_ready" if kind == "gat" else name + "_table_ready", n if kind == "gat" else 0)
                self.table = [signal(f"{name}_table{q}") for q in range(2)]
                self.staged = signal("staged", HV * n)
                self.gathered = [signal(f"{name}_gathered{q}") for q in range(2)]
                self.hot = signal("hot", HV * n)
                self.summed = signal("summed", HV * n)
                self.acc_read = signal("acc_read", n)
                self.finished = signal("finished", n)
                if kind == "gat":
                    m, q2 = layer, 16 * ITERS * layer
                    self.turned = signal("turned", HV * m)
                    self.turned_out = signal("turned_out", HV * m)
                    self.looked = signal("looked", HV * m)
                    self.taken = signal("taken", HV * m)
                    self.spilled = [signal(f"spilled{q}", q2) for q in range(2)]
                    self.back = [signal(f"back{q}", q2) for q in range(2)]
                    self.msgs = signal("msgs", HV * m)
                    self.acc_clear = signal("acc_clear", m)
                    self.regrouped = signal("regrouped", 2 * m)
                    self.to_heads = signal("to_heads", 2 * KG * m)
                    self.to_heads_out = signal("to_heads_out", 2 * KG * m)
                    self.scanned = signal("scanned", m)
                    self.ends_T = signal("ends_T", m)
                    self.carried = signal("carried", m)
                    self.carries_T = signal("carries_T", m)
                    self.less_max = signal("less_max", 2 * m)
                    self.exped = signal("exped", 2 * m)
                    self.to_edges = signal("to_edges", 2 * KG * m)
                    self.to_edges_out = signal("to_edges_out", 2 * KG * m)

        class Projection:

            def __init__(self, n, weights):
                self.w = signal(f"{weights}")
                self.inp = signal("proj_in", n)
                self.xs, self.tr, self.xT, self.mm, self.out = (
                    signal("proj_" + k, 5 * n) for k in ("xs", "turned", "xT", "made", "out"))

        gats = [(Projection(l, f"gat{l}_w"), Round(l, f"gat{l}", "gat", l)) for l in range(3)]
        bns = [Projection(3 + l, f"bn{l}_w") for l in range(2)]

        class Expansion:

            def __init__(self, l):
                self.w = signal(f"rel{l}_w")
                self.inp = signal("exp_in", l)
                self.xs, self.tr, self.xT = (signal("exp_" + k, TILES * l) for k in ("xs", "turned", "xT"))
                self.mm = signal("exp_made", 9 * TILES * l)
                self.out_v = signal("exp_out_v", 6 * TILES * l)
                self.out_a = signal("exp_out_a", 4 * TILES * l)

        rels = [(Expansion(l), Round(3 + l, f"rel{l}", "rel", l)) for l in range(2)]
        gin, wgin = Round(5, "gin", "sum"), Round(6, "wgin", "weighted")
        loaded, lists_loaded, pads_set = sem("loaded"), sem("lists_loaded"), sem("pads_set")
        const_ready, ends_counted, ends_summed = sem("const_ready"), sem("ends_counted"), sem("ends_summed")
        ones_ready = sem("ones_ready")
        picks_ready, picked, edge_lists_ready = sem("picks_ready"), sem("picked"), sem("edge_lists_ready")
        keys_ready, keys_T, keys_out = sem("keys_ready"), sem("keys_T"), sem("keys_out")
        key_rows, start_row, start_col, starts_T = sem("key_rows"), sem("start_row"), sem("start_col"), sem("starts_T")
        starts, starts_out, setup_read = sem("starts"), sem("starts_out"), sem("setup_read")
        bn_part, bn_total, bn_done = sem("bn_part"), sem("bn_total"), sem("bn_done")
        var_ready, std_ready = sem("var_ready"), sem("std_ready")
        x_final, out_written = sem("x_final"), sem("out_written")
        v_own = sem("v_own")
        gather_begun, tile_begun = sem("gather_begun"), sem("tile_begun")

        block = ctx.enter_context(nc.Block())

        def every(v, n=D):
            return v.rearrange("(a n) -> a n", a=1).broadcast_to([P, n])

        def halves(eng, body, last=ITERS):
            body(0, 0, True)
            body(0, 1, True)
            with eng.Fori(1, last) as i:
                body(i, 0, False)
                body(i, 1, False)

        def tiles_by_two(eng, body):
            body(0, 0, True)
            body(1, 1, True)
            with eng.Fori(1, TILES // 2) as i:
                body(i * 2, 0, False)
                body(i * 2 + 1, 1, False)
            body(TILES - 1, 0, False, True)

        @block.sync
        def _(sp):
            sp.wait_ge(pads_set, 1)
            sp.dma_start(x[:, 0:TILES - 1, :],
                         a["x"][0:(TILES - 1) * P, :].rearrange("(t p) f -> p t f", p=P)).then_inc(loaded, 16)
            sp.dma_start(x[0:LAST, TILES - 1, :], a["x"][(TILES - 1) * P:, :]).then_inc(loaded, 16)
            sp.dma_start(eps1[:], every(a["L2_gnn_eps"], 1)).then_inc(loaded, 16)
            full, rest = (EB - 1) * P * P, EDGES // P - (EB - 1) * P
            for q, n in enumerate(("dst", "src", "edge_type_65", "edge_weight")):
                o = raw[:, q] if q < 3 else lists[:, 3]
                sp.dma_start(o[:, 0:EB - 1, :],
                             a[n][0:full].rearrange("(b p e) -> p b e", p=P, e=P)).then_inc(lists_loaded, 16)
                sp.dma_start(o[0:rest, EB - 1, :],
                             a[n][full:full + rest * P].rearrange("(p e) -> p e", e=P)).then_inc(lists_loaded, 16)
                sp.dma_start(o[rest:rest + 1, EB - 1, 0:EDGES % P],
                             a[n][full + rest * P:].rearrange("(a e) -> a e", a=1)).then_inc(lists_loaded, 16)

            for pj, r in gats:
                l = r.layer + 1
                if r.layer:
                    gats[r.layer - 1][1].finished.wait(sp, 1)
                sp.dma_start(wn[:], a[f"L0_gnn_W{l}"]).then_inc(pj.w.sem, 16)
                for k, n in enumerate((f"L0_gnn_a_src{l}", f"L0_gnn_a_dst{l}")):
                    sp.dma_start(vecs[:, k, :], every(a[n].rearrange("h c -> (h c)"))).then_inc(pj.w.sem, 16)
                sp.dma_start(vecs[:, 2, :], every(a[f"L0_gnn_b{l}"])).then_inc(pj.w.sem, 16)
                r.table_ready.wait(sp, 1)
                sp.dma_start(gat_table.rearrange("(t p) f -> p t f", p=P), ht).then_inc(r.table[0].sem, 16)

                def store(i, q, peeled):
                    r.gathered[q].wait(sp, i * (16 * HALF) + 16 * HALF)
                    sp.dma_start(spill[:, bass.ds(i * 2 * HALF + q * HALF, HALF), :], ring[:, q])\
                      .then_inc(r.spilled[q].sem, 16)
                halves(sp, store)
                for q in range(2):
                    r.spilled[q].wait(sp, 16 * ITERS)
                r.taken.wait(sp, HV)

                def load(i, q, peeled):
                    if not peeled:
                        r.msgs.wait(sp, i * 2 + (q - 1))
                    sp.dma_start(ring[:, q], spill[:, bass.ds(i * 2 * HALF + q * HALF, HALF), :])\
                      .then_inc(r.back[q].sem, 16)
                halves(sp, load)

            for ex, r in rels:
                l = r.layer
                prev = rels[0][1] if l else gats[2][1]
                prev.finished.wait(sp, 1)
                for h in range(2):
                    w = w_full[h * D:(h + 1) * D, :]
                    sp.dma_start(w[:, 0:REL * D].rearrange("d (r k) -> d r k", k=D),
                                 a["L1_gnn_W"][l].rearrange("r d k -> d r k")).then_inc(ex.w.sem, 16)
                    sp.dma_start(w[:, REL * D:(REL + 1) * D], a["L1_gnn_root"][l]).then_inc(ex.w.sem, 16)
                    sp.dma_start(w[:, (REL + 1) * D:CW * D], a["L1_gnn_res_W"][l]).then_inc(ex.w.sem, 16)
                sp.dma_start(vecs[:, 0, :], every(a["L1_gnn_bias"][l])).then_inc(ex.w.sem, 16)
                sp.dma_start(vecs[:, 1, :], every(a["L1_gnn_res_b"][l])).then_inc(ex.w.sem, 16)
                by_node = rel_table.rearrange("(n r) k -> n (r k)", r=REL)

                def store(t, slot, peeled, last=False):
                    ex.out_v.wait(sp, t * 6 + 6)
                    ex.out_a.wait(sp, t * 4 + 4)
                    sp.dma_start(by_node[bass.ds(t * P, P), :], stage[:, slot, 0:REL * D]).then_inc(r.table[slot].sem, 16)
                tiles_by_two(sp, store)
            for r in (gin, wgin):
                r.table_ready.wait(sp, 1)
                sp.dma_start(x_table.rearrange("(t p) f -> p t f", p=P), x[:]).then_inc(r.table[0].sem, 16)
            for l, pj in enumerate(bns):
                if l:
                    sp.wait_ge(bn_done, 1)
                sp.dma_start(wn[:], a[f"L3_gnn_W{l + 1}"]).then_inc(pj.w.sem, 16)
                for k, n in enumerate(("b", "gamma", "beta")):
                    sp.dma_start(vecs[:, k, :], every(a[f"L3_gnn_{n}{l + 1}"])).then_inc(pj.w.sem, 16)
            sp.wait_ge(x_final, 1)
            sp.dma_start(out[0:(TILES - 1) * P, :].rearrange("(t p) f -> p t f", p=P),
                         x[:, 0:TILES - 1, :]).then_inc(out_written, 16)
            sp.dma_start(out[(TILES - 1) * P:, :], x[0:LAST, TILES - 1, :]).then_inc(out_written, 16)
            sp.wait_ge(out_written, 32)

        @block.gpsimd
        def _(pool):
            ok = dict(allow_small_or_imprecise_dtypes=True)
            pool.iota(iota[:], pattern=[[1, P]], base=0, channel_multiplier=0, **ok).then_inc(const_ready, 1)
            pool.iota(iota_rel[:], pattern=[[1, REL]], base=0, channel_multiplier=0, **ok).then_inc(const_ready, 1)
            pool.iota(iota_s, pattern=[[1, STEPS]], base=0, channel_multiplier=0, **ok).then_inc(const_ready, 1)
            pool.iota(part[:], pattern=[[0, 1]], base=0, channel_multiplier=1, **ok).then_inc(const_ready, 1)

            def gather(r, table, width):
                if r.kind == "rel":
                    r.table[0].wait(pool, 16 * (TILES - TILES // 2))
                    r.table[1].wait(pool, 16 * (TILES // 2))
                else:
                    r.table[0].wait(pool, 16)

                def body(i, q, peeled):
                    r.staged.wait(pool, i * 2 + (q + 1))
                    pool.sem_inc(gather_begun, 1)
                    for k in range(HALF):
                        pool.indirect_dma_start(
                            out=ring[:, q, k, 0:width], out_offset=None, in_=table,
                            in_offset=bass.IndirectOffsetOnAxis(ap=idx_now[:, q, k:k + 1], axis=0),
                        ).then_inc(r.gathered[q].sem, 16)
                halves(pool, body)

            for _, r in gats:
                gather(r, gat_table, D + HEADS)
            for _, r in rels:
                gather(r, rel_table, D)
            gather(gin, x_table, D)
            gather(wgin, x_table, D)

        @block.scalar
        def _(act):
            def stage_half(r, half, q):
                idx = rel_idx if r.kind == "rel" else src_idx
                act.copy(idx_now[:, q, :], idx[:, bass.ds(half * HALF, HALF)]).then_inc(r.staged.sem, 1)

            def table_written(r):
                if r.kind == "rel":
                    r.table[0].wait(act, 16 * (TILES - TILES // 2))
                    r.table[1].wait(act, 16 * (TILES // 2))
                else:
                    r.table[0].wait(act, 16)

            def project(pj, src):
                pj.inp.wait(act, 1)

                def body(i, peeled):
                    if not peeled:
                        pj.tr.wait(act, i)
                    act.copy(xs[:], src[:, bass.ds(i * 5, 5), :]).then_inc(pj.xs.sem, 1)
                    pj.tr.wait(act, i + 1)
                    if not peeled:
                        pj.mm.wait(act, i)
                    act.copy(xT[:, 0:4, :], ps[0:D, 5, :].rearrange("p (a n) -> p a n", a=4))
                    act.copy(xT[:, 4, :], ps[0:D, 6, 0:P]).then_inc(pj.xT.sem, 1)
                body(0, True)
                with act.Fori(1, 5) as i:
                    body(i, False)

            def sqrt(n, v):
                act.wait_ge(var_ready, n)
                act.activation(v, v, ACT.Sqrt).then_inc(std_ready, 1)

            act.wait_ge(edge_lists_ready, 1)
            for g in range(KG):
                act.wait_ge(keys_T, g + 1)
                act.copy(logit_T[:, g * P:(g + 1) * P], ps[:, 5 + g % 2, 0:P]).then_inc(keys_out, 1)
            for g in range(KG):
                act.wait_ge(starts, g + 1)
                act.copy(first.rearrange("p (k g) -> p k g", g=KG)[:, :, g],
                         ps[:, 5 + g % 2, 0:P].rearrange("p (k h) -> p k h", h=HEADS)[:, :, 0]).then_inc(starts_out, 1)

            for pj, r in gats:
                project(pj, x if r.layer == 0 else y)
                table_written(r)
                stage_half(r, 0, 0)

                def body(i, q, peeled, ahead=True):
                    if ahead:
                        if not (peeled and q == 0):
                            r.taken.wait(act, i * 2 + q)
                            r.spilled[1 - q].wait(act, i * 16 + q * 16)
                        stage_half(r, i * 2 + (q + 1), 1 - q)
                    r.turned.wait(act, i * 2 + (q + 1))
                    if not peeled:
                        r.looked.wait(act, i * 2 + (q - 1))
                    act.copy(onehot_T[:, q], turned_ps).then_inc(r.turned_out.sem, 1)
                halves(act, body, ITERS - 1)
                body(ITERS - 1, 0, False)
                body(ITERS - 1, 1, False, ahead=False)
                for g in range(2 * KG):
                    dst = logit_T if g < KG else own_T
                    r.to_heads.wait(act, g + 1)
                    act.copy(dst[:, (g % KG) * P:(g % KG + 1) * P], ps[:, 5 + g % 2, 0:P])\
                       .then_inc(r.to_heads_out.sem, 1)
                r.less_max.wait(act, 1)
                act.activation(logit_T, logit_T, ACT.Exp).then_inc(r.exped.sem, 1)
                r.less_max.wait(act, 2)
                act.activation(own_T, own_T, ACT.Exp).then_inc(r.exped.sem, 1)
                for g in range(2 * KG):
                    dst = (logit if g < KG else own).rearrange("p (k g) h -> p k g h", g=KG)[:, :, g % KG, :]
                    r.to_edges.wait(act, g + 1)
                    act.copy(dst, ps[:, 5 + g % 2, 0:P].rearrange("p (k h) -> p k h", h=HEADS))\
                       .then_inc(r.to_edges_out.sem, 1)
            sqrt(1, small[:, 1, 0:TILES])

            def stage_all(r):
                table_written(r)
                stage_half(r, 0, 0)

                def body(i, q, peeled):
                    if not (peeled and q == 0):
                        r.summed.wait(act, i * 2 + q)
                    stage_half(r, i * 2 + (q + 1), 1 - q)
                halves(act, body, ITERS - 1)
                body(ITERS - 1, 0, False)

            for ex, r in rels:
                ex.inp.wait(act, 1)

                def next_tile(t, slot, zeroth=False):
                    if not zeroth:
                        ex.tr.wait(act, t)
                    act.copy(x3s[:], x3[:, bass.ds(t, 1), :].squeeze(1)).then_inc(ex.xs.sem, 1)
                    ex.tr.wait(act, t + 1)
                    act.copy(x3T[:, slot], x3_ps).then_inc(ex.xT.sem, 1)

                def body(t, slot, peeled, last=False):
                    if not peeled:
                        r.table[slot].wait(act, t * 8 - slot * 8)
                    for n in (1, 3, 5, 7):
                        ex.mm.wait(act, t * 9 + (n + 1))
                        act.copy(stage[:, slot, n * 512:(n + 1) * 512], ps[:, n % 7, :]).then_inc(ex.out_a.sem, 1)
                        if n == 3 and not last:
                            next_tile(t + 1, 1 - slot)
                next_tile(0, 0, True)
                tiles_by_two(act, body)
                stage_all(r)
            sqrt(2, small[:, 1, 0:TILES])
            stage_all(gin)
            sqrt(3, small[:, 1, 0:TILES])
            stage_all(wgin)
            for l, pj in enumerate(bns):
                project(pj, y)
                sqrt(4 + l, st[:, 3, :])
            sqrt(6, small[:, 1, 0:TILES])

        @block.tensor
        def _(pe):
            def project(pj):
                pj.w.wait(pe, 64)

                def body(i, peeled):
                    pj.xs.wait(pe, i + 1)
                    if not peeled:
                        pj.xT.wait(pe, i)
                        pe.sem_inc(tile_begun, 1)
                    for k in range(5):
                        ins = pe.transpose(ps[0:D, 5 + k // 4, (k % 4) * P:(k % 4 + 1) * P], xs[:, k, :], ident[:])
                    ins.then_inc(pj.tr.sem, 1)
                    pj.xT.wait(pe, i + 1)
                    if not peeled:
                        pj.out.wait(pe, i)
                    for k in range(5):
                        ins = pe.matmul(ps[:, 7, k * D:(k + 1) * D], xT[:, k, :], wn[:], start=True, stop=True)
                    ins.then_inc(pj.mm.sem, 1)
                body(0, True)
                with pe.Fori(1, 5) as i:
                    body(i, False)

            def clear_sums():
                for b in range(BANKS):
                    pe.matmul(ps[:, b, :], zero[:], zero[:].unsqueeze(1).broadcast_to([1, 4, P]), start=True, stop=False, skip_group_check=True)

            def places(i, q):
                return nc.values_load_multi_w_load_instructions(
                    place[0:1, bass.ds(i * (2 * HALF) + q * HALF, HALF)], engines=(mybir.EngineType.PE,),
                    min_val=0, max_val=(BANKS - 1) * 512 + (PERBANK - 1) * PITCH)[1]

            pe.wait_ge(ones_ready, 1)
            pe.wait_ge(ends_counted, 1)
            pe.matmul(ps[:, 7, 0:TILES - 1], ones[:], ends[:], start=True, stop=True).then_inc(ends_summed, 1)
            pe.wait_ge(picks_ready, 1)
            for q in range(4):
                for b in range(EB):
                    ins = pe.matmul(ps[:, q, 0:STEPS], lists[:, q, b, :], pick[:, b, :],
                                    start=b == 0, stop=b == EB - 1)
            ins.then_inc(picked, 1)
            pe.wait_ge(keys_ready, 1)
            for g in range(KG):
                if g >= 2:
                    pe.wait_ge(keys_out, g - 1)
                pe.transpose(ps[:, 5 + g % 2, 0:P], smax2[:, g * P:(g + 1) * P], ident[:]).then_inc(keys_T, 1)
            pe.wait_ge(keys_out, KG)
            pe.transpose(ps[0:1, 7, 0:P], logit_T[:, 0:1], ident[:])
            pe.transpose(ps[0:1, 7, P:2 * P], logit_T[:, SL - 1:SL], ident[:]).then_inc(key_rows, 1)
            pe.wait_ge(start_row, 1)
            pe.matmul(ps[:, 7, 2 * P:2 * P + 1], rows[:, 10, :], ones[0:1, 0:1], start=True, stop=True).then_inc(start_col, 1)
            pe.wait_ge(starts_T, 1)
            for g in range(KG):
                if g >= 2:
                    pe.wait_ge(starts_out, g - 1)
                pe.transpose(ps[:, 5 + g % 2, 0:P], own_T[:, g * P:(g + 1) * P], ident[:]).then_inc(starts, 1)

            for pj, r in gats:
                pe.wait_ge(starts_out, KG)
                project(pj)
                r.table_ready.wait(pe, 1)
                if r.layer == 0:
                    clear_sums()

                def look(i, q, peeled):
                    at = places(i, q)
                    r.hot.wait(pe, i * 2 + (q + 1))
                    if not (peeled and q == 0):
                        r.turned_out.wait(pe, i * 2 + q)
                    for k in range(HALF):
                        ins = pe.transpose(turned_ps[:, k, :], onehot_h[:, q, k, :], ident_h[:])
                    ins.then_inc(r.turned.sem, 1)
                    if r.layer == 0:
                        for k in range(HALF):
                            pe.matmul(flat[:, bass.ds(at[k], REL)], onehot_h[:, q, k, :], relhot[:, q, k, :],
                                      start=False, stop=False, skip_group_check=True)
                    if not peeled:
                        r.taken.wait(pe, i * 2 + (q - 1))
                    r.turned_out.wait(pe, i * 2 + (q + 1))
                    for k in range(HALF):
                        if r.layer == 1:
                            n, o = 2 * HEADS + REL, ps[:, 2 * q + k // PERBANK, (k % PERBANK) * PITCH:]
                        else:
                            n, o = 2 * HEADS, ps[:, 6 + q, k * 2 * HEADS:]
                        for m in range(3):
                            ins = pe.matmul(o[:, 0:n], onehot_T[:, q, k, :], nodeq[:, m, bass.ds(at[k], n)],
                                            start=m == 0, stop=m == 2, skip_group_check=True)
                    ins.then_inc(r.looked.sem, 1)
                halves(pe, look)
                for g in range(2 * KG):
                    if g % KG == 0:
                        r.regrouped.wait(pe, 1 + g // KG)
                    if g >= 2:
                        r.to_heads_out.wait(pe, g - 1)
                    pe.transpose(ps[:, 5 + g % 2, 0:P], (smax if g < KG else smax2)[:, (g % KG) * P:(g % KG + 1) * P],
                                 ident[:]).then_inc(r.to_heads.sem, 1)
                r.scanned.wait(pe, 1)
                pe.transpose(ps[0:1, 7, 0:P], smax2[:, SL - 1:SL], ident[:])
                pe.transpose(ps[0:1, 7, P:2 * P], smax[:, 0:1], ident[:]).then_inc(r.ends_T.sem, 1)
                r.carried.wait(pe, 1)
                pe.matmul(ps[:, 7, 256:257], rows[:, 10, :], ones[0:1, 0:1], start=True, stop=True)
                pe.matmul(ps[:, 7, 257:258], rows[:, 11, :], ones[0:1, 0:1], start=True, stop=True)\
                  .then_inc(r.carries_T.sem, 1)
                for g in range(2 * KG):
                    if g % KG == 0:
                        r.exped.wait(pe, 1 + g // KG)
                    if g >= 2:
                        r.to_edges_out.wait(pe, g - 1)
                    pe.transpose(ps[:, 5 + g % 2, 0:P], (logit_T if g < KG else own_T)[:, (g % KG) * P:(g % KG + 1) * P],
                                 ident[:]).then_inc(r.to_edges.sem, 1)
                r.acc_clear.wait(pe, 1)
                clear_sums()

                def add(i, q, peeled):
                    at = places(i, q)
                    r.msgs.wait(pe, i * 2 + (q + 1))
                    for k in range(HALF):
                        ins = pe.matmul(flat[:, bass.ds(at[k], D + 2 * HEADS)], onehot[:, q, k, :], msg[:, q, k, :],
                                        start=False, stop=False, skip_group_check=True)
                    ins.then_inc(r.summed.sem, 1)
                halves(pe, add)

            def add_gathered(r, before):
                before.acc_read.wait(pe, 1)
                clear_sums()

                def add(i, q, peeled):
                    at = places(i, q)
                    r.hot.wait(pe, i * 2 + (q + 1))
                    r.gathered[q].wait(pe, i * (16 * HALF) + 16 * HALF)
                    for k in range(HALF):
                        ins = pe.matmul(flat[:, bass.ds(at[k], D)], onehot[:, q, k, :], ring[:, q, k, 0:D],
                                        start=False, stop=False, skip_group_check=True)
                    ins.then_inc(r.summed.sem, 1)
                halves(pe, add)

            for ex, r in rels:
                before = rels[0][1] if r.layer else gats[2][1]
                before.acc_read.wait(pe, 1)
                ex.inp.wait(pe, 1)

                def next_tile(t):
                    ex.xs.wait(pe, t + 1)
                    pe.sem_inc(tile_begun, 1)
                    pe.transpose(x3_ps[:, 0, :], x3s[:, 0:2 * D], ident_h[:])
                    pe.transpose(x3_ps[:, 1, :], x3s[:, D:3 * D], ident_h[:]).then_inc(ex.tr.sem, 1)
                next_tile(0)

                def body(t, slot, peeled, last=False):
                    zeroth = isinstance(t, int) and t == 0
                    ex.xT.wait(pe, t + 1)
                    for n in range(9):
                        if n == 0 and not zeroth:
                            ex.out_a.wait(pe, t * 4)
                        if n == 1 and not zeroth:
                            ex.out_v.wait(pe, t * 6)
                        if n == 7:
                            ex.out_v.wait(pe, t * 6 + 1)
                        if n == 8:
                            ex.out_a.wait(pe, t * 4 + 1)
                        m = min(512, CW * D - n * 512)
                        for k, turned in ((0, 0), (1, 0), (2, 1)):
                            ins = pe.matmul(ps[:, n % 7, 0:m], x3T[:, slot, turned, :], w_part[k][:, n * 512:n * 512 + m],
                                            start=k == 0, stop=k == 2)
                        ins.then_inc(ex.mm.sem, 1)
                        if n == 4 and not last:
                            next_tile(t + 1)
                tiles_by_two(pe, body)
                ex.out_v.wait(pe, 6 * TILES)
                ex.out_a.wait(pe, 4 * TILES)
                add_gathered(r, before)
            add_gathered(gin, rels[1][1])
            add_gathered(wgin, gin)
            for l, pj in enumerate(bns):
                project(pj)
                for n in range(2):
                    pe.wait_ge(bn_part, 2 * l + n + 1)
                    pe.matmul(ps[:, 6, 256 + n * D:256 + (n + 1) * D], ones[:], st[:, 2 * n, :], start=True, stop=True)\
                      .then_inc(bn_total, 1)

        @block.vector
        def _(v):
            own_order = Order(v, v_own)
            then, done, wait = own_order.then, own_order.done, own_order.wait
            wide = [P, TILES, D]

            done(v.memset(x[:, TILES - 1, :], 0.0))
            done(v.memset(raw[:, 0], int(NEVER)))
            done(v.memset(raw[:, 1:3], 0))
            done(v.memset(lists[:, 3], 0.0))
            wait()
            v.memset(zero[:], 0.0).then_inc(pads_set, 1)
            done(v.memset(ones[:], 1.0))
            done(v.memset(tile_of[:], 0.0))
            done(v.memset(joins[:, 0:1], -BIG))
            done(v.memset(joins[:, SL:SL + 1], -BIG))
            done(v.memset(rows[:], -BIG))
            done(v.memset(nodeq[:], 0.0))
            v.wait_ge(const_ready, 4)
            then(v.tensor_scalar(ident[:], iota[:], part[:, 0:1], None, ALU.is_equal))
            done(v.tensor_copy(iota_h[:], iota[:]))
            then(v.tensor_copy(ident_h[:], ident[:]))
            v.memset(ends[:], 0.0).then_inc(ones_ready, 1)

            v.wait_ge(lists_loaded, 16 * 12)
            done(v.tensor_copy(lists[:, 0:2], raw[:, 0:2]))
            then(v.scalar_tensor_tensor(lists[:, 2], raw[:, 1], float(REL), raw[:, 2], ALU.mult, ALU.add))
            dsts = lists[:, 0].rearrange("p b e -> p (b e)")
            below = msg[:].rearrange("p a b c -> p (a b c)")[:, 0:EB * P]
            for t in range(TILES - 1):
                then(v.tensor_scalar(below, dsts, float((t + 1) * P), None, ALU.is_lt))
                then(v.tensor_reduce(ends[:, t:t + 1], below, X, ALU.add))
            v.sem_inc(ends_counted, 1)
            v.wait_ge(ends_summed, 1)
            then(v.tensor_scalar(ends[:], ps[:, 7, 0:TILES - 1], 1.0 / P, CHUNKS - 0.5, ALU.mult, ALU.min))
            then(v.tensor_tensor(ends[:], ends[:], iota[:, 0:TILES - 1], ALU.add))
            for t in range(TILES - 1):
                then(v.scalar_tensor_tensor(tile_of[:], iota_s, ends[:, t:t + 1], tile_of[:], ALU.is_gt, ALU.add))
            then(v.tensor_scalar(tmp_s, tile_of[:], float(PITCH), None, ALU.mult))
            for b in range(1, BANKS):
                then(v.tensor_scalar(tmp_s2, tile_of[:], float(PERBANK * b), float(512 - PERBANK * PITCH),
                                     ALU.is_ge, ALU.mult))
                then(v.tensor_tensor(tmp_s, tmp_s, tmp_s2, ALU.add))
            then(v.tensor_copy(place[:], tmp_s[0:1, :]))
            then(v.tensor_tensor(tmp_s2, iota_s, tile_of[:], ALU.subtract))
            for b in range(EB):
                then(v.tensor_scalar(pick[:, b, :], tmp_s2, part[:, 0:1], float(b * P), ALU.subtract, ALU.is_equal))
            v.sem_inc(picks_ready, 1)

            v.wait_ge(picked, 1)
            dst_ps, src_ps, rel_ps, w_ps = (ps[:, q, 0:STEPS] for q in range(4))
            then(v.scalar_tensor_tensor(node_of[:], tile_of[:], -float(P), dst_ps, ALU.mult, ALU.add))
            then(v.tensor_scalar(tmp_s, node_of[:], 0.0, None, ALU.is_ge))
            then(v.scalar_tensor_tensor(tmp_s2, node_of[:], float(P), tmp_s, ALU.is_lt, ALU.mult))
            then(v.scalar_tensor_tensor(key, dst_ps, 1.0, tmp_s2, ALU.add, ALU.mult))
            then(v.tensor_scalar(key, key, -1.0, None, ALU.add))
            then(v.tensor_copy(tmp_s, src_ps))
            done(v.scalar_tensor_tensor(rel_of[:], tmp_s, -float(REL), rel_ps, ALU.mult, ALU.add))
            done(v.tensor_copy(src_idx[:], src_ps))
            done(v.tensor_copy(rel_idx[:], rel_ps))
            done(v.tensor_copy(weight[:], w_ps))
            apart = lambda m: m.rearrange("p (g k h) -> p g k h", k=KB, h=HEADS)
            then(v.tensor_copy(apart(smax2), key.rearrange("p (k g) -> p g k", g=KG).unsqueeze(3)
                               .broadcast_to([P, KG, KB, HEADS])))
            v.sem_inc(keys_ready, 1)
            v.sem_inc(edge_lists_ready, 1)

            v.wait_ge(keys_out, KG)
            flags = smax
            for o, i0, i1 in ((joins[:, 1:SL], logit_T[:, 1:SL], logit_T[:, 0:SL - 1]),
                              (in_first[:], logit_T, None), (in_last[:], logit_T, None)):
                f = flags[:, 0:o.shape[1]]
                if i1 is not None:
                    then(v.tensor_tensor(f, i0, i1, ALU.is_equal))
                else:
                    at = 0 if o.name == in_first[:].name else SL - 1
                    then(v.tensor_scalar(f, i0, logit_T[:, at:at + 1], None, ALU.is_equal))
                then(v.tensor_scalar(o, f, -1.0, BIG, ALU.add, ALU.mult))
            row = lambda n: rows[:, n, :].rearrange("p (h k) -> p h k", h=HEADS)
            row_kh = lambda n: rows[:, n, :].rearrange("p (k h) -> p h k", h=HEADS)
            ps_row = lambda n: ps[0:1, 7, n * P:(n + 1) * P].rearrange("p (k h) -> p h k", h=HEADS)
            v.wait_ge(key_rows, 1)
            done(v.tensor_copy(row(0), ps_row(0)))
            then(v.tensor_copy(row(1), ps_row(1)))
            then(v.tensor_tensor(row(2)[:, :, 1:], row(0)[:, :, 1:], row(1)[:, :, 0:KB - 1], ALU.is_equal))
            then(v.tensor_scalar(row(2)[:, :, 1:], row(2)[:, :, 1:], -1.0, BIG, ALU.add, ALU.mult))
            then(v.tensor_tensor(row(3), row(0), row(1), ALU.is_equal))
            then(v.tensor_scalar(row(3), row(3), -1.0, BIG, ALU.add, ALU.mult))
            done(v.tensor_tensor(row(4), row(2), row(3), ALU.min))
            done(v.tensor_tensor(row(5)[:, :, 0:KB - 1], row(2)[:, :, 1:], row(3)[:, :, 0:KB - 1], ALU.min))
            then(v.tensor_copy(row_kh(10), row(2)))
            v.sem_inc(start_row, 1)
            done(v.tensor_scalar(own_T, joins[:, 0:SL], -1.0, None, ALU.is_lt))
            v.wait_ge(start_col, 1)
            wait()
            then(v.tensor_scalar(own_T[:, 0:1], ps[:, 7, 2 * P:2 * P + 1], -1.0, None, ALU.is_lt))
            v.sem_inc(starts_T, 1)

            def one_hots(at, q, scale=None, half_width=False):
                for k in range(HALF):
                    c = lambda m: m[:, bass.ds(at + k, 1)]
                    if half_width:
                        ins = v.tensor_scalar(onehot_h[:, q, k, :], iota_h[:], c(node_of), None, ALU.is_equal)
                    elif scale is None:
                        ins = v.tensor_scalar(onehot[:, q, k, :], iota[:], c(node_of), None, ALU.is_equal)
                    else:
                        ins = v.tensor_scalar(onehot[:, q, k, :], iota[:], c(node_of), c(scale),
                                              ALU.is_equal, ALU.mult)
                return ins

            def project(pj, dst, bias=None):
                pj.w.wait(v, 64)

                def body(i):
                    pj.mm.wait(v, i + 1)
                    o = dst[:, bass.ds(i * 5, 5), :]
                    p = ps[:, 7, 0:5 * D].rearrange("p (a f) -> p a f", f=D)
                    if bias is None:
                        v.tensor_copy(o, p).then_inc(pj.out.sem, 1)
                    else:
                        v.tensor_tensor(o, p, bias.unsqueeze(1).broadcast_to([P, 5, D]), ALU.add).then_inc(pj.out.sem, 1)
                with v.Fori(0, 5) as i:
                    body(i)
                pj.out.wait(v, 5)

            def layernorm(n):
                s = small[:, :, 0:TILES]
                cent = w1[:]
                then(v.tensor_reduce(s[:, 0], w1[:], X, ALU.add))
                then(v.tensor_scalar(s[:, 0], s[:, 0], 1.0 / D, None, ALU.mult))
                then(v.tensor_tensor(cent, w1[:], s[:, 0].unsqueeze(2).broadcast_to(wide), ALU.subtract))
                then(v.tensor_tensor(w2[:], cent, cent, ALU.mult))
                then(v.tensor_reduce(s[:, 1], w2[:], X, ALU.add))
                v.tensor_scalar(s[:, 1], s[:, 1], 1.0 / D, EPS, ALU.mult, ALU.add).then_inc(var_ready, 1)
                v.wait_ge(std_ready, n)
                then(v.reciprocal(s[:, 2], s[:, 1]))
                then(v.tensor_tensor(x[:], cent, s[:, 2].unsqueeze(2).broadcast_to(wide), ALU.mult))

            def in_parts(m, col):
                for k in range(3):
                    for b in range(BANKS):
                        o, ts = of_bank(nodeq[:, k], b, col, m.shape[2])
                        done(v.tensor_copy(o, m[:, ts, :]))
                    wait()
                    if k < 2:
                        for b in range(BANKS):
                            o, ts = of_bank(nodeq[:, k], b, col, m.shape[2])
                            done(v.tensor_tensor(m[:, ts, :], m[:, ts, :], o, ALU.subtract))
                        wait()

            def read_sums(r, dst, n):
                r.summed.wait(v, HV)
                for b in range(BANKS):
                    m, ts = of_bank(flat, b, 0, n)
                    done(v.tensor_copy(dst[:, ts, 0:n], m))
                wait()
                v.sem_inc(r.acc_read.sem, 1)

            v.wait_ge(loaded, 48)
            h_of, as_of = ht[:, :, 0:D], ht[:, :, D:D + HEADS]
            sm = [small[:, k, :].rearrange("p (t h) -> p t h", h=HEADS) for k in range(6)]
            for pj, r in gats:
                v.sem_inc(pj.inp.sem, 1)
                project(pj, h_of)
                for k, o in ((0, as_of), (1, sm[0])):
                    then(v.tensor_tensor(w1[:], h_of, vecs[:, k, :].unsqueeze(1).broadcast_to(wide), ALU.mult))
                    then(v.tensor_reduce(o, w1[:].rearrange("p t (h c) -> p t h c", c=C), X, ALU.add))
                then(v.tensor_tensor(sm[1], as_of, sm[0], ALU.add))
                then(v.scalar_tensor_tensor(sm[2], sm[1], 0.2, sm[1], ALU.mult, ALU.max))
                done(v.tensor_copy(w1[:, :, 0:HEADS], sm[0]))
                then(v.tensor_copy(w1[:, :, HEADS:2 * HEADS], sm[2]))
                in_parts(w1[:, :, 0:2 * HEADS], 0)
                v.sem_inc(r.table_ready.sem, 1)

                def mark(half, q, free):
                    at = half * HALF
                    if free is not None:
                        r.looked.wait(v, free)
                    ins = one_hots(at, q, half_width=True)
                    if r.layer < 2:
                        done(ins)
                        ins = v.tensor_tensor(relhot[:, q], rel_of[:, bass.ds(at, HALF)].unsqueeze(2).broadcast_to([P, HALF, REL]),
                                              iota_rel[:].unsqueeze(1).broadcast_to([P, HALF, REL]), ALU.is_equal)
                    ins.then_inc(r.hot.sem, 1)

                def take(i, q):
                    at = i * (2 * HALF) + q * HALF
                    r.looked.wait(v, i * 2 + (q + 1))
                    r.gathered[q].wait(v, i * (16 * HALF) + 16 * HALF)
                    if r.layer == 1:
                        pieces = [(k, min(PERBANK, HALF - k), ps[:, 2 * q + k // PERBANK, 0:PERBANK * PITCH]
                                   .rearrange("p (s c) -> p s c", c=PITCH)) for k in range(0, HALF, PERBANK)]
                    else:
                        pieces = [(0, HALF, ps[:, 6 + q, 0:HALF * 2 * HEADS]
                                   .rearrange("p (s c) -> p s c", c=2 * HEADS))]
                    for k, n, g in pieces:
                        s = bass.ds(at + k, n)
                        done(v.tensor_tensor(gz[:, q, k:k + n], ring[:, q, k:k + n, D:D + HEADS], g[:, 0:n, 0:HEADS], ALU.add))
                        if r.layer == 1:
                            r.hot.wait(v, i * 2 + (q + 1))
                            done(v.tensor_tensor(relsel[:, q, k:k + n], relhot[:, q, k:k + n],
                                                 g[:, 0:n, 2 * HEADS:2 * HEADS + REL], ALU.mult))
                            wait()
                            done(v.tensor_reduce(count[:, s], relsel[:, q, k:k + n], X, ALU.add))
                        wait()
                        done(v.scalar_tensor_tensor(logit[:, s, :], gz[:, q, k:k + n], 0.2, gz[:, q, k:k + n], ALU.mult, ALU.max))
                        ins = v.tensor_copy(own[:, s, :], g[:, 0:n, HEADS:2 * HEADS])
                        if k + n < HALF:
                            done(ins)
                        else:
                            ins.then_inc(r.taken.sem, 1)
                per_half = {0: 3, 1: 1 + 4 * 2 + 1, 2: 2}[r.layer]
                mark(0, 0, None)
                mark(1, 1, None)
                take(0, 0)
                with v.Fori(1, ITERS) as i, own_order.loop(i, 1, ITERS, 2 * per_half):
                    mark(i * 2, 0, i * 2 - 1)
                    take(i - 1, 1)
                    mark(i * 2 + 1, 1, i * 2)
                    take(i, 0)
                take(ITERS - 1, 1)
                wait()
                if r.layer == 0:
                    for b in range(BANKS):
                        m, ts = of_bank(flat, b, 0, REL)
                        done(v.tensor_copy(u[:, ts, 0:REL], m))
                    wait()
                    in_parts(u[:, :, 0:REL], 2 * HEADS)
                if r.layer == 1:
                    then(v.tensor_scalar(count[:], count[:], 1.0, None, ALU.max))
                    then(v.reciprocal(count[:], count[:]))
                v.sem_inc(r.acc_clear.sem, 1)
                v.tensor_copy(apart(smax), logit.rearrange("p (k g) h -> p g k h", g=KG)).then_inc(r.regrouped.sem, 1)
                r.regrouped.wait(v, 1)
                v.tensor_copy(apart(smax2), own.rearrange("p (k g) h -> p g k h", g=KG)).then_inc(r.regrouped.sem, 1)

                r.to_heads_out.wait(v, 2 * KG)
                then(v.tensor_tensor(smax, logit_T, own_T, ALU.max))
                then(v.tensor_tensor_scan(smax2, joins[:, 0:SL], smax, -BIG, ALU.add, ALU.max))
                then(v.tensor_tensor_scan(smax[:, ::-1], joins[:, 1:SL + 1][:, ::-1], smax2[:, ::-1], -BIG, ALU.add, ALU.max))
                v.sem_inc(r.scanned.sem, 1)
                r.ends_T.wait(v, 1)
                done(v.tensor_copy(row(6), ps_row(0)))
                then(v.tensor_copy(row(7), ps_row(1)))
                done(v.tensor_tensor_scan(rows[:, 8, :], rows[:, 4, :], rows[:, 6, :], -BIG, ALU.add, ALU.max))
                then(v.tensor_tensor_scan(rows[:, 9, ::-1], rows[:, 5, ::-1], rows[:, 7, ::-1], -BIG, ALU.add, ALU.max))
                done(v.tensor_tensor(row_kh(10)[:, :, 1:], row(8)[:, :, 0:KB - 1], row(2)[:, :, 1:], ALU.add))
                then(v.tensor_tensor(row_kh(11)[:, :, 0:KB - 1], row(9)[:, :, 1:], row(2)[:, :, 1:], ALU.add))
                v.sem_inc(r.carried.sem, 1)
                r.carries_T.wait(v, 1)
                then(v.tensor_copy(cols[:], ps[:, 7, 256:258]))
                then(v.scalar_tensor_tensor(smax, in_first[:], cols[:, 0:1], smax, ALU.add, ALU.max))
                then(v.scalar_tensor_tensor(smax, in_last[:], cols[:, 1:2], smax, ALU.add, ALU.max))
                v.tensor_tensor(logit_T, logit_T, smax, ALU.subtract).then_inc(r.less_max.sem, 1)
                v.tensor_tensor(own_T, own_T, smax, ALU.subtract).then_inc(r.less_max.sem, 1)
                r.to_edges_out.wait(v, 2 * KG)
                v.wait_ge(starts_out, KG)
                then(v.tensor_tensor(own, own, first[:].unsqueeze(2).broadcast_to([P, STEPS, HEADS]), ALU.mult))

                def weigh(i, q, peeled):
                    at = i * (2 * HALF) + q * HALF
                    if not peeled:
                        r.summed.wait(v, i * 2 + (q - 1))
                    one_hots(at, q)
                    v.tensor_copy(msg[:, q, :, D:D + HEADS], logit[:, bass.ds(at, HALF), :])
                    v.tensor_copy(msg[:, q, :, D + HEADS:D + 2 * HEADS], own[:, bass.ds(at, HALF), :])
                    r.back[q].wait(v, i * 16 + 16)
                    v.tensor_tensor(msg[:, q, :, 0:D].rearrange("p s (h c) -> p s h c", c=C),
                                    ring[:, q, :, 0:D].rearrange("p s (h c) -> p s h c", c=C),
                                    logit[:, bass.ds(at, HALF), :].unsqueeze(3).broadcast_to([P, HALF, HEADS, C]),
                                    ALU.mult).then_inc(r.msgs.sem, 1)
                halves(v, weigh)

                read_sums(r, u, D + 2 * HEADS)
                ex, exs = u[:, :, D:D + HEADS], u[:, :, D + HEADS:D + 2 * HEADS]
                then(v.tensor_tensor(sm[0], ex, exs, ALU.add))
                then(v.tensor_scalar(sm[1], sm[0], 0.5, None, ALU.is_lt))
                then(v.tensor_tensor(sm[2], exs, sm[1], ALU.add))
                then(v.tensor_tensor(sm[3], ex, sm[2], ALU.add))
                then(v.tensor_scalar(sm[3], sm[3], 1e-16, None, ALU.add))
                done(v.reciprocal(sm[4], sm[3]))
                w1h, w2h = (m[:].rearrange("p t (h c) -> p t h c", c=C) for m in (w1, w2))
                then(v.tensor_tensor(w1h, h_of.rearrange("p t (h c) -> p t h c", c=C), per_head(sm[2]), ALU.mult))
                then(v.tensor_tensor(w1[:], w1[:], u[:, :, 0:D], ALU.add))
                then(v.tensor_tensor(w2h, w1h, per_head(sm[4]), ALU.mult))
                then(v.tensor_tensor(y[:], w2[:], vecs[:, 2, :].unsqueeze(1).broadcast_to(wide), ALU.add))
                if r.layer < 2:
                    then(v.tensor_scalar(y[:], y[:], 0.0, None, ALU.max))
                v.sem_inc(r.finished.sem, 1)
            then(v.tensor_tensor(w1[:], x[:], y[:], ALU.add))
            layernorm(1)

            def sum_round(r, scale):
                def body(i, q, peeled):
                    at = i * (2 * HALF) + q * HALF
                    if not peeled:
                        r.summed.wait(v, i * 2 + (q - 1))
                    one_hots(at, q, scale).then_inc(r.hot.sem, 1)
                halves(v, body)
                read_sums(r, u, D)

            for ex_, r in rels:
                xin, mid, high, low = (y if r.layer else x)[:], x3[:, :, 0:D], x3[:, :, D:2 * D], x3[:, :, 2 * D:]
                then(v.tensor_copy(high, xin))
                then(v.tensor_tensor(w1[:], xin, high, ALU.subtract))
                then(v.tensor_copy(mid, w1[:]))
                then(v.tensor_tensor(low, w1[:], mid, ALU.subtract))
                ex_.w.wait(v, 16 * 8)
                then(v.tensor_copy(w_part[0], w_full))
                then(v.tensor_tensor(w_full, w_full, w_part[0], ALU.subtract))
                then(v.tensor_copy(w_part[1], w_full))
                then(v.tensor_tensor(w_part[2][0:D], w_full[0:D], w_part[1][0:D], ALU.subtract))
                then(v.tensor_copy(w_part[2][D:P], w_part[0][D:P]))
                v.sem_inc(ex_.inp.sem, 1)

                def body(t, slot, peeled, last=False):
                    if not peeled:
                        r.table[slot].wait(v, t * 8 - slot * 8)
                    for n in (0, 2, 4, 6):
                        ex_.mm.wait(v, t * 9 + (n + 1))
                        v.tensor_copy(stage[:, slot, n * 512:(n + 1) * 512], ps[:, n % 7, :]).then_inc(ex_.out_v.sem, 1)
                    ex_.mm.wait(v, t * 9 + 9)
                    v.tensor_copy(stage[:, slot, 8 * 512:REL * D], ps[:, 1, 0:REL * D - 8 * 512]).then_inc(ex_.out_v.sem, 1)
                    v.tensor_copy(rr[:, bass.ds(t, 1), :].squeeze(1), ps[:, 1, REL * D - 8 * 512:CW * D - 8 * 512])\
                     .then_inc(ex_.out_v.sem, 1)
                tiles_by_two(v, body)
                sum_round(r, count)
                bias = lambda k: vecs[:, k, :].unsqueeze(1).broadcast_to(wide)
                then(v.tensor_tensor(w1[:], u[:, :, 0:D], rr[:, :, 0:D], ALU.add))
                done(v.tensor_tensor(w2[:], rr[:, :, D:2 * D], bias(1), ALU.add))
                then(v.tensor_tensor(w1[:], w1[:], bias(0), ALU.add))
                then(v.tensor_scalar(w2[:], w2[:], 0.0, None, ALU.max))
                then(v.scalar_tensor_tensor(y[:], w1[:], 0.0, w2[:], ALU.max, ALU.add))
                v.sem_inc(r.finished.sem, 1)
            then(v.tensor_tensor(w1[:], x[:], y[:], ALU.add))
            layernorm(2)

            v.sem_inc(gin.table_ready.sem, 1)
            sum_round(gin, None)
            then(v.tensor_scalar(small[:, 0, 0:1], eps1[:, 0:1], 1.0, None, ALU.add))
            then(v.scalar_tensor_tensor(w2[:], x[:], small[:, 0, 0:1], u[:, :, 0:D], ALU.mult, ALU.add))
            then(v.tensor_tensor(w1[:], x[:], w2[:], ALU.add))
            layernorm(3)

            v.sem_inc(wgin.table_ready.sem, 1)
            sum_round(wgin, weight)
            then(v.tensor_tensor(y[:], u[:, :, 0:D], x[:], ALU.add))
            then(v.tensor_scalar(cols[:, 0:1], part[:, 0:1], float(LAST), None, ALU.is_lt))
            for l, pj in enumerate(bns):
                v.sem_inc(pj.inp.sem, 1)
                project(pj, w1, vecs[:, 0, :])
                every_tile = lambda m: m.unsqueeze(1).broadcast_to(wide)
                last = w1[:, TILES - 1, :]
                then(v.tensor_scalar(last, last, cols[:, 0:1], None, ALU.mult))
                then(v.tensor_reduce(st[:, 0, :], w1[:].rearrange("p t f -> p f t"), X, ALU.add))
                v.sem_inc(bn_part, 1)
                v.wait_ge(bn_total, 2 * l + 1)
                then(v.tensor_scalar(st[:, 1, :], ps[:, 6, 256:256 + D], 1.0 / NODES, None, ALU.mult))
                then(v.tensor_tensor(w1[:], w1[:], every_tile(st[:, 1, :]), ALU.subtract))
                then(v.tensor_scalar(last, last, cols[:, 0:1], None, ALU.mult))
                then(v.tensor_tensor(w2[:], w1[:], w1[:], ALU.mult))
                then(v.tensor_reduce(st[:, 2, :], w2[:].rearrange("p t f -> p f t"), X, ALU.add))
                v.sem_inc(bn_part, 1)
                v.wait_ge(bn_total, 2 * l + 2)
                v.tensor_scalar(st[:, 3, :], ps[:, 6, 256 + D:256 + 2 * D], 1.0 / NODES, EPS, ALU.mult, ALU.add)\
                 .then_inc(var_ready, 1)
                v.wait_ge(std_ready, 4 + l)
                then(v.reciprocal(st[:, 4, :], st[:, 3, :]))
                then(v.tensor_tensor(st[:, 5, :], st[:, 4, :], vecs[:, 1, :], ALU.mult))
                then(v.tensor_tensor(w2[:], w1[:], every_tile(st[:, 5, :]), ALU.mult))
                then(v.tensor_tensor(w2[:], w2[:], every_tile(vecs[:, 2, :]), ALU.add))
                then(v.tensor_scalar(y[:], w2[:], 0.0, None, ALU.max))
                v.sem_inc(bn_done, 1)
            then(v.tensor_tensor(w1[:], x[:], y[:], ALU.add))
            layernorm(6)
            v.sem_inc(x_final, 1)


_INS = (["x", "src", "dst", "edge_type_65", "edge_weight"]
        + [f"L0_gnn_{n}{l}" for l in (1, 2, 3) for n in ("W", "a_src", "a_dst", "b")]
        + [f"L1_gnn_{n}" for n in ("W", "root", "bias", "res_W", "res_b")] + ["L2_gnn_eps"]
        + [f"L3_gnn_{n}{l}" for l in (1, 2) for n in ("W", "b", "gamma", "beta")])


def kernel(**inputs):
    import numpy as _np
    import concourse.bacc as _bacc
    from concourse import mybir as _mybir
    from concourse.bass_utils import run_bass_kernel_spmd as _run

    nc = _bacc.Bacc("TRN2", target_bir_lowering=False, num_devices=1)
    arrays, args = {}, {}
    for name in _INS:
        v = _np.ascontiguousarray(inputs[name])
        arrays[f"in_{name}"] = v
        args[name] = nc.dram_tensor(f"in_{name}", v.shape, _mybir.dt.from_np(v.dtype), kind="ExternalInput").ap()
    out = nc.dram_tensor("out_0", (NODES, D), F32, kind="ExternalOutput").ap()
    build(nc, args, out)
    r = _run(nc, [arrays], core_ids=[0])
    return r.results[0]["out_0"]
```

```python
from contextlib import ExitStack, contextmanager

import concourse.bass as bass
from concourse import mybir

F32 = mybir.dt.float32
I32 = mybir.dt.int32
BF16 = mybir.dt.bfloat16
ALU = mybir.AluOpType
ACT = mybir.ActivationFunctionType
X = mybir.AxisListType.X

P = 128
NODES, D = 3125, 64
EDGES = 50000
HEADS, C = 8, 8
REL = 65
TILES = -(-NODES // P)
LAST = NODES - (TILES - 1) * P
CHUNKS = -(-EDGES // P)
EB = -(-CHUNKS // P)
STEPS = CHUNKS + TILES
HALF = 8
ITERS = STEPS // (2 * HALF)
RUN = 2 * HALF
SL = STEPS * P // RUN
PITCH, PERBANK = 84, 6
BANKS = -(-TILES // PERBANK)
CW = REL + 2
PIECES = 16
WIDE = CW * D // PIECES
GROUPS = [(t, min(4, TILES - t)) for t in range(0, TILES, 4)]
NEVER = 4000.0
BIG = 1.0e30
EPS = 1e-5
assert STEPS == RUN * ITERS and RUN * HEADS == P and ITERS % 2 == 0
assert CW * D % PIECES == 0 and PIECES < ITERS


class Signal:

    def __init__(self, sem, base=0):
        self.sem, self.base = sem, base

    def wait(self, eng, count):
        eng.wait_ge(self.sem, count + self.base)


class Order:

    def __init__(self, eng, sem):
        self.eng, self.sem, self.total, self.loop_at = eng, sem, 0, None

    def done(self, ins):
        ins.then_inc(self.sem, 1)
        self.total += 1

    def wait(self):
        if self.loop_at is None:
            self.eng.wait_ge(self.sem, self.total)
        else:
            reg, first, per, base = self.loop_at
            self.eng.wait_ge(self.sem, reg * per + (self.total - first * per))

    def then(self, ins):
        self.done(ins)
        self.wait()

    @contextmanager
    def loop(self, reg, first, last, per):
        base = self.total
        self.loop_at = (reg, first, per, base)
        yield
        assert self.total == base + per, (self.total - base, per)
        self.total = base + (last - first) * per
        self.loop_at = None


def build(nc, a, out):
    with ExitStack() as ctx:
        def sb(name, shape, dt=F32):
            return ctx.enter_context(nc.sbuf_tensor(name, shape, dt))

        def sem(name):
            return ctx.enter_context(nc.semaphore(name))

        def dram(name, shape, dt=F32):
            return nc.dram_tensor(name, shape, dt).ap()

        arena = sb("arena", [P, 2 * REL * D + 3 * CW * D // 2])
        raw = arena[:, 0:4 * EB * P].bitcast(I32).rearrange("p (q b e) -> p q b e", q=4, b=EB)
        lists = arena[:, 4 * EB * P:8 * EB * P].rearrange("p (q b e) -> p q b e", q=4, b=EB)
        pick = arena[:, 8 * EB * P:8 * EB * P + EB * STEPS].rearrange("p (b s) -> p b s", b=EB)
        below = arena[:, 8 * EB * P + EB * STEPS:8 * EB * P + EB * STEPS + (TILES - 1) * EB * P // 2].bitcast(BF16).rearrange(
            "p (t n) -> p t n", t=TILES - 1)
        both_T = arena[:, 0:2 * SL].rearrange("p (i a e) -> p i a e", a=2, e=P)
        smax = arena[:, 2 * SL:3 * SL].rearrange("p (i e) -> p i e", e=P)
        key_s = arena[:, 0:SL].rearrange("p (s h) -> p s h", h=HEADS)
        key_T = arena[:, 3 * SL:4 * SL].rearrange("p (i e) -> p i e", e=P)
        flags = arena[:, 2 * SL:3 * SL].rearrange("p (i e) -> p i e", e=P)
        stage = arena[:, 0:2 * REL * D].rearrange("p (s c) -> p s c", s=2)
        w_full = arena[:, 0:CW * D]
        w_halves = slice(0, CW * D // 2), slice(CW * D // 2, CW * D)
        w_part = [arena[:, 2 * REL * D + n * CW * D // 2:2 * REL * D + (n + 1) * CW * D // 2].bitcast(BF16)
                  for n in range(3)]

        ring = sb("ring", [P, 2, HALF, D + HEADS])
        onehot = sb("onehot", [P, 2, HALF, P])
        onehot_h = onehot[:].rearrange("p a s n -> p (a s n)").bitcast(BF16).rearrange(
            "p (q n k) -> p q n k", q=4, k=HALF)
        onehot_T = sb("onehot_T", [P, 2, HALF, P], BF16)
        scratch = sb("scratch", [P, 2 * HALF * (D + 2 * HEADS)])
        relhot = sb("relhot", [P, 2, REL, HALF], BF16)
        relsel = scratch[:, 0:2 * HALF * REL].rearrange("p (a s c) -> p a s c", a=2, c=REL)
        gz = sb("gz", [P, 2, HALF, HEADS])
        idx_now = sb("idx_now", [P, 2, HALF], I32)
        nodeq = sb("nodeq", [P, 3, BANKS * 512], BF16)
        gat_nodes = sb("gat_nodes", [P, TILES * (2 * D + 3 * HEADS)])
        ht = gat_nodes[:, 0:TILES * (D + HEADS)].rearrange("p (t c) -> p t c", t=TILES)
        u = gat_nodes[:, TILES * (D + HEADS):].rearrange("p (t c) -> p t c", t=TILES)
        x3 = gat_nodes[:, 0:TILES * 3 * D // 2].bitcast(BF16).rearrange(
            "p (t c) -> p t c", t=TILES)
        x = sb("x", [P, TILES, D])
        y = sb("y", [P, TILES, D])
        work = sb("work", [P, 2 * TILES * D])
        w1, w2 = (work[:, n * TILES * D:(n + 1) * TILES * D].rearrange("p (t f) -> p t f", f=D) for n in range(2))
        msg4 = work[:, 0:4 * HALF * (D + 2 * HEADS)].rearrange("p (q s c) -> p q s c", q=4, s=HALF)
        msg3 = arena[:, 3 * SL:3 * SL + 6 * HALF * (D + 2 * HEADS)].bitcast(BF16).rearrange(
            "p (q m s c) -> p q m s c", q=4, m=3, s=HALF)
        first_end, last_end, ahead, behind, carry_f, carry_b = (
            work[0:HEADS, n * STEPS:(n + 1) * STEPS] for n in range(6))
        small = sb("small", [P, 5, TILES * HEADS])
        iota = sb("iota", [P, P])
        ident = sb("ident", [P, P])
        ident_h = sb("ident_h", [P, P], BF16)
        ones = sb("ones", [P, P])
        iota_k = sb("iota_k", [P, P, HALF], BF16)
        iota_rel = sb("iota_rel", [P, REL, HALF], BF16)
        iota_s = onehot[:].rearrange("p a s n -> p (a s n)")[:, 0:STEPS]
        part = sb("part", [P, 1])
        zero = sb("zero", [1, P])
        node_of = sb("node_of", [P, STEPS])
        key = scratch[:, EB * P:EB * P + STEPS]
        rel_of = sb("rel_of", [P, STEPS], BF16)
        node_h = sb("node_h", [P, STEPS], BF16)
        weight = sb("weight", [P, STEPS])
        count = sb("count", [P, STEPS])
        inv_degree = sb("inv_degree", [P, TILES])
        tile_of = sb("tile_of", [P, STEPS])
        tmp_s, tmp_s2 = (onehot[:].rearrange("p a s n -> p (a s n)")[:, n * STEPS:(n + 1) * STEPS]
                         for n in (1, 2))
        src_idx = sb("src_idx", [P, STEPS], I32)
        rel_idx = sb("rel_idx", [P, STEPS], I32)
        place = sb("place", [1, STEPS], I32)
        ends = sb("ends", [TILES - 1, 1])
        a_column = sb("a_column", [P, 2 * TILES - 1], BF16)
        joins = sb("joins", [P, SL + 1], BF16)
        joins_back = sb("joins_back", [P, ITERS, P], BF16)
        in_first = sb("in_first", [P, SL], BF16)
        in_last = sb("in_last", [P, SL], BF16)
        goes_on, pass_f, pass_b = (sb(n, [HEADS, STEPS]) for n in ("goes_on", "pass_f", "pass_b"))
        shift = sb("shift", [HEADS, 2 * P - HEADS])
        run_max = sb("run_max", [P, 2, P])
        logits_now = sb("logits_now", [P, 2, P])
        weights_now = sb("weights_now", [P, 2, P])
        carries = sb("carries", [P, 2, ITERS])
        cols = sb("cols", [P, 1])
        wn = sb("wn", [D, 5, D + 2 * HEADS])
        att = sb("att", [D, 3, 2, D])
        gat_bias = sb("gat_bias", [P, 3, D])
        rel_bias = sb("rel_bias", [P, 2, 2, D])
        bn_vecs = sb("bn_vecs", [P, 2, 3, D])
        eps1 = sb("eps1", [P, 1])
        xT = sb("xT", [D, 2, 4, P])
        x3s = sb("x3s", [P, 3 * D], BF16)
        x3T = sb("x3T", [P, 2, 2, P], BF16)
        st = sb("st", [P, 6, D])
        ps = ctx.enter_context(nc.psum_tensor("ps", [P, 8, 512], F32))
        flat = ps[:].rearrange("p b n -> p (b n)")

        gat_table = dram("gat_table", [TILES * P, D + HEADS])
        x_table = dram("x_table", [TILES * P, D])
        rel_table = dram("rel_table", [NODES * REL, D])
        spill = dram("spill", [P, STEPS, D + HEADS])

        rr = nodeq[:].rearrange("p a n -> p (a n)").bitcast(F32)[:, 0:TILES * 2 * D].rearrange(
            "p (t c) -> p t c", t=TILES)

        both_ps = ps[:, 7, 0:2 * P].rearrange("p (a n) -> p a n", a=2)

        x3_ps = ps[:, 7, 0:P].bitcast(BF16).rearrange("p (a n) -> p a n", a=2)

        turned_ps = ps[:, 5, :].bitcast(BF16).rearrange("p (k n) -> p k n", k=HALF)

        def per_head(ap):
            return ap.unsqueeze(3).broadcast_to([P, ap.shape[1], HEADS, C])

        def of_bank(m, b, col, n):
            k = min(PERBANK, TILES - b * PERBANK)
            v = m[:, b * 512:b * 512 + k * PITCH].rearrange("p (t c) -> p t c", c=PITCH)
            return v[:, :, col:col + n], slice(b * PERBANK, b * PERBANK + k)

        HV = 2 * ITERS
        shared = {}

        def signal(name, base=0):
            if name not in shared:
                shared[name] = sem(name)
            return Signal(shared[name], base)

        class Round:

            def __init__(self, n, name, kind, layer=0):
                self.kind, self.layer = kind, layer
                self.table_ready = signal("table_ready" if kind == "gat" else name + "_table_ready", n if kind == "gat" else 0)
                self.table = [signal(f"{name}_table{q}") for q in range(2)]
                self.staged = signal("staged", HV * n)
                self.gathered = [signal(f"{name}_gathered{q}") for q in range(2)]
                self.hot = signal("hot", HV * n)
                self.summed = signal("summed", HV * n)
                self.acc_read = signal("acc_read", n)
                self.finished = signal("finished", n)
                if kind == "gat":
                    m, q2 = layer, 16 * ITERS * layer
                    self.turned = signal("turned", HV * m)
                    self.turned_out = signal("turned_out", HV * m)
                    self.looked = signal("looked", HV * m)
                    self.taken = signal("taken", HV * m)
                    self.spilled = [signal(f"spilled{q}", q2) for q in range(2)]
                    self.back = [signal(f"back{q}", q2) for q in range(2)]
                    self.acc_clear = signal("acc_clear", m)
                    self.to_heads = signal("to_heads", ITERS * m)
                    self.to_heads_out = signal("to_heads_out", ITERS * m)
                    self.scanned = signal("scanned", m)
                    self.ends_T = signal("ends_T", m)
                    self.carried = signal("carried", m)
                    self.carries_T = signal("carries_T", m)
                    self.maxed = signal("maxed", ITERS * m)
                    self.less_max = signal("less_max", ITERS * m)
                    self.exped = signal("exped", ITERS * m)
                    self.to_edges = signal("to_edges", ITERS * m)
                    self.to_edges_out = signal("to_edges_out", HV * m)
                    self.weighed = signal("weighed", HV * m)
                    self.high = signal("high", HV * m)
                    self.rest = signal("rest", HV * m)
                    self.mid = signal("mid", HV * m)
                    self.msgs = signal("msgs", HV * m)

        class Projection:

            def __init__(self, n, weights):
                self.w = signal(f"{weights}")
                self.inp = signal("proj_in", n)
                self.tr, self.xT, self.mm, self.out = (
                    signal("proj_" + k, len(GROUPS) * n) for k in ("turned", "xT", "made", "out"))

        gats = [(Projection(l, f"gat{l}_w"), Round(l, f"gat{l}", "gat", l)) for l in range(3)]
        bns = [Projection(3 + l, f"bn{l}_w") for l in range(2)]

        def bank_of(slot, n):
            return (n + 2 * slot) % 7

        class Expansion:

            def __init__(self, l):
                self.w = signal(f"rel{l}_w")
                self.vec = signal(f"rel{l}_vec")
                self.inp = signal("exp_in", l)
                self.xs, self.tr, self.xT = (signal("exp_" + k, TILES * l) for k in ("xs", "turned", "xT"))
                self.mm = signal("exp_made", 9 * TILES * l)
                self.out_v = signal("exp_out_v", 6 * TILES * l)
                self.out_a = signal("exp_out_a", 4 * TILES * l)

        rels = [(Expansion(l), Round(3 + l, f"rel{l}", "rel", l)) for l in range(2)]
        gin, wgin = Round(5, "gin", "sum"), Round(6, "wgin", "weighted")
        w_cast, w_rest = sem("w_cast"), sem("w_rest")
        loaded, lists_loaded, pads_set = sem("loaded"), sem("lists_loaded"), sem("pads_set")
        const_ready, below_ready, ends_summed = sem("const_ready"), sem("below_ready"), sem("ends_summed")
        passed_ready, tiles_counted = sem("passed_ready"), sem("tiles_counted")
        ones_ready = sem("ones_ready")
        picks_ready, picked, edge_lists_ready = sem("picks_ready"), sem("picked"), sem("edge_lists_ready")
        keys_ready, keys_T, keys_out = sem("keys_ready"), sem("keys_T"), sem("keys_out")
        key_ends = sem("key_ends")
        bn_part, bn_total = sem("bn_part"), sem("bn_total")
        var_ready, std_ready = sem("var_ready"), sem("std_ready")
        x_final, out_written = sem("x_final"), sem("out_written")
        v_own = sem("v_own")
        gather_begun, tile_begun = sem("gather_begun"), sem("tile_begun")

        block = ctx.enter_context(nc.Block())

        def every(v, n=D):
            return v.rearrange("(a n) -> a n", a=1).broadcast_to([P, n])

        def halves(eng, body, last=ITERS):
            body(0, 0, True)
            body(0, 1, True)
            with eng.Fori(1, last) as i:
                body(i, 0, False)
                body(i, 1, False)

        def halves_by_four(eng, body, before=None, last=HV // 4):
            for b in range(4):
                body(b // 2, b % 2, b, b, True)
            with eng.Fori(1, last) as j:
                with (before(j) if before else ExitStack()):
                    for b in range(4):
                        body(j * 2 + b // 2, b % 2, j * 4 + b, b, False)

        def tiles_by_two(eng, body):
            body(0, 0, True)
            body(1, 1, True)
            with eng.Fori(1, TILES // 2) as i:
                body(i * 2, 0, False)
                body(i * 2 + 1, 1, False)
            body(TILES - 1, 0, False, True)

        @block.sync
        def _(sp):
            sp.wait_ge(pads_set, 1)
            sp.dma_start(x[:, 0:TILES - 1, :],
                         a["x"][0:(TILES - 1) * P, :].rearrange("(t p) f -> p t f", p=P)).then_inc(loaded, 16)
            sp.dma_start(x[0:LAST, TILES - 1, :], a["x"][(TILES - 1) * P:, :]).then_inc(loaded, 16)
            sp.dma_start(eps1[:], every(a["L2_gnn_eps"], 1)).then_inc(loaded, 16)
            full, rest = (EB - 1) * P * P, EDGES // P - (EB - 1) * P
            for q, n in enumerate(("dst", "src", "edge_type_65", "edge_weight")):
                o = raw[:, q] if q < 3 else lists[:, 3]
                sp.dma_start(o[:, 0:EB - 1, :],
                             a[n][0:full].rearrange("(b p e) -> p b e", p=P, e=P)).then_inc(lists_loaded, 16)
                sp.dma_start(o[0:rest, EB - 1, :],
                             a[n][full:full + rest * P].rearrange("(p e) -> p e", e=P)).then_inc(lists_loaded, 16)
                sp.dma_start(o[rest:rest + 1, EB - 1, 0:EDGES % P],
                             a[n][full + rest * P:].rearrange("(a e) -> a e", a=1)).then_inc(lists_loaded, 16)

            def broad(o, n, s):
                sp.dma_start(o, n.rearrange("(a n) -> a n", a=1).broadcast_to([o.shape[0], D])).then_inc(s.sem, 16)

            for l, (pj, _) in enumerate(gats):
                sp.dma_start(wn[:, l, 0:D], a[f"L0_gnn_W{l + 1}"]).then_inc(pj.w.sem, 16)
                for k, n in enumerate((f"L0_gnn_a_src{l + 1}", f"L0_gnn_a_dst{l + 1}")):
                    broad(att[:, l, k, :], a[n].rearrange("h c -> (h c)"), pj.w)
                broad(gat_bias[:, l, :], a[f"L0_gnn_b{l + 1}"], pj.w)
            for l, (ex, _) in enumerate(rels):
                broad(rel_bias[:, l, 0, :], a["L1_gnn_bias"][l], ex.vec)
                broad(rel_bias[:, l, 1, :], a["L1_gnn_res_b"][l], ex.vec)
            for l, pj in enumerate(bns):
                sp.dma_start(wn[:, 3 + l, 0:D], a[f"L3_gnn_W{l + 1}"]).then_inc(pj.w.sem, 16)
                for k, n in enumerate(("b", "gamma", "beta")):
                    broad(bn_vecs[:, l, k, :], a[f"L3_gnn_{n}{l + 1}"], pj.w)

            for pj, r in gats:
                r.table_ready.wait(sp, 1)
                sp.dma_start(gat_table.rearrange("(t p) f -> p t f", p=P), ht).then_inc(r.table[0].sem, 16)

                def store(i, q, peeled):
                    r.gathered[q].wait(sp, i * (16 * HALF) + 16 * HALF)
                    sp.dma_start(spill[:, bass.ds(i * 2 * HALF + q * HALF, HALF), :], ring[:, q])\
                      .then_inc(r.spilled[q].sem, 16)
                halves(sp, store)
                for q in range(2):
                    r.spilled[q].wait(sp, 16 * ITERS)
                r.taken.wait(sp, HV)

                def load(i, q, peeled):
                    if not peeled:
                        r.weighed.wait(sp, i * 2 + (q - 1))
                    sp.dma_start(ring[:, q], spill[:, bass.ds(i * 2 * HALF + q * HALF, HALF), :])\
                      .then_inc(r.back[q].sem, 16)
                halves(sp, load)

            def load_weights(ex, l):
                for h in range(2):
                    w = w_full[h * D:(h + 1) * D, :]
                    sp.dma_start(w[:, 0:REL * D].rearrange("d (r k) -> d r k", k=D),
                                 a["L1_gnn_W"][l].rearrange("r d k -> d r k")).then_inc(ex.w.sem, 16)
                    sp.dma_start(w[:, REL * D:(REL + 1) * D], a["L1_gnn_root"][l]).then_inc(ex.w.sem, 16)
                    sp.dma_start(w[:, (REL + 1) * D:CW * D], a["L1_gnn_res_W"][l]).then_inc(ex.w.sem, 16)

            for ex, r in rels:
                l = r.layer
                if l == 0:
                    gats[2][1].exped.wait(sp, ITERS)
                    load_weights(ex, 0)
                by_node = rel_table.rearrange("(n r) k -> n (r k)", r=REL)

                def store(t, slot, peeled, last=False):
                    ex.out_v.wait(sp, t * 6 + 6)
                    ex.out_a.wait(sp, t * 4 + 4)
                    rows = LAST if last else P
                    sp.dma_start(by_node[bass.ds(t * P, rows), :], stage[0:rows, slot, 0:REL * D]).then_inc(r.table[slot].sem, 16)
                tiles_by_two(sp, store)
                if l == 0:
                    r.table[0].wait(sp, 16 * (TILES - TILES // 2))
                    r.table[1].wait(sp, 16 * (TILES // 2))
                    load_weights(rels[1][0], 1)
            for r in (gin, wgin):
                r.table_ready.wait(sp, 1)
                sp.dma_start(x_table.rearrange("(t p) f -> p t f", p=P), x[:]).then_inc(r.table[0].sem, 16)
            sp.wait_ge(x_final, 1)
            sp.dma_start(out[0:(TILES - 1) * P, :].rearrange("(t p) f -> p t f", p=P),
                         x[:, 0:TILES - 1, :]).then_inc(out_written, 16)
            sp.dma_start(out[(TILES - 1) * P:, :], x[0:LAST, TILES - 1, :]).then_inc(out_written, 16)
            sp.wait_ge(out_written, 32)

        @block.gpsimd
        def _(pool):
            ok = dict(allow_small_or_imprecise_dtypes=True)
            pool.iota(iota[:], pattern=[[1, P]], base=0, channel_multiplier=0, **ok).then_inc(const_ready, 1)
            pool.iota(iota_k[:], pattern=[[1, P], [0, HALF]], base=0, channel_multiplier=0, **ok).then_inc(const_ready, 1)
            pool.iota(iota_rel[:], pattern=[[1, REL], [0, HALF]], base=0, channel_multiplier=0, **ok).then_inc(const_ready, 1)
            pool.iota(shift[:], pattern=[[1, 2 * P - HEADS]], base=HEADS - P, channel_multiplier=-1, **ok).then_inc(const_ready, 1)
            pool.iota(iota_s, pattern=[[1, STEPS]], base=0, channel_multiplier=0, **ok).then_inc(const_ready, 1)
            pool.iota(part[:], pattern=[[0, 1]], base=0, channel_multiplier=1, **ok).then_inc(const_ready, 1)

            def gather(r, table, width):
                if r.kind == "rel":
                    r.table[0].wait(pool, 16 * (TILES - TILES // 2))
                    r.table[1].wait(pool, 16 * (TILES // 2))
                else:
                    r.table[0].wait(pool, 16)

                def body(i, q, peeled):
                    r.staged.wait(pool, i * 2 + (q + 1))
                    pool.sem_inc(gather_begun, 1)
                    for k in range(HALF):
                        pool.indirect_dma_start(
                            out=ring[:, q, k, 0:width], out_offset=None, in_=table,
                            in_offset=bass.IndirectOffsetOnAxis(ap=idx_now[:, q, k:k + 1], axis=0),
                        ).then_inc(r.gathered[q].sem, 16)
                halves(pool, body)

            for _, r in gats:
                gather(r, gat_table, D + HEADS)

                def exponents(i):
                    r.maxed.wait(pool, i + 1)
                    o = both_T[:, bass.ds(i, 1)].squeeze(1)
                    pool.tensor_tensor(o, o, smax[:, bass.ds(i, 1)].broadcast_to([P, 2, P]), ALU.subtract)\
                        .then_inc(r.less_max.sem, 1)

                def rest(i, q, b, slot, peeled, last=False):
                    if q == 0 and not (last and slot == 2):
                        exponents(i + 1)
                    r.high.wait(pool, b + 1)
                    pool.tensor_tensor(msg4[:, slot], msg4[:, slot], msg3[:, slot, 0], ALU.subtract).then_inc(r.rest.sem, 1)
                exponents(0)
                halves_by_four(pool, rest, last=HV // 4 - 1)
                for b in range(4):
                    rest(ITERS - 2 + b // 2, b % 2, HV - 4 + b, b, False, True)

            for n, c in enumerate(w_halves):
                pool.wait_ge(w_cast, n + 1)
                pool.tensor_tensor(w_full[:, c], w_full[:, c], w_part[0][:, c], ALU.subtract).then_inc(w_rest, 1)
            for n, c in enumerate(w_halves):
                pool.wait_ge(w_cast, n + 3)
                pool.tensor_tensor(w_part[2][0:D, c], w_full[0:D, c], w_part[1][0:D, c], ALU.subtract).then_inc(w_rest, 1)
            for _, r in rels:
                gather(r, rel_table, D)
            gather(gin, x_table, D)
            gather(wgin, x_table, D)

        @block.scalar
        def _(act):
            def stage_half(r, half, q):
                idx = rel_idx if r.kind == "rel" else src_idx
                act.copy(idx_now[:, q, :], idx[:, bass.ds(half * HALF, HALF)]).then_inc(r.staged.sem, 1)

            def table_written(r):
                if r.kind == "rel":
                    r.table[0].wait(act, 16 * (TILES - TILES // 2))
                    r.table[1].wait(act, 16 * (TILES // 2))
                else:
                    r.table[0].wait(act, 16)

            def project(pj):
                for g, (t, n) in enumerate(GROUPS):
                    pj.tr.wait(act, g + 1)
                    if g >= 2:
                        pj.mm.wait(act, g - 1)
                    act.copy(xT[:, g % 2, 0:n, :], ps[0:D, 5 + g % 2, 0:n * P].rearrange("p (a n) -> p a n", n=P))\
                       .then_inc(pj.xT.sem, 1)

            def sqrt(n, v):
                act.wait_ge(var_ready, n)
                act.activation(v, v, ACT.Sqrt).then_inc(std_ready, 1)

            act.wait_ge(edge_lists_ready, 1)
            for pj, r in gats:
                project(pj)
                table_written(r)
                stage_half(r, 0, 0)
                if r.layer == 0:
                    stage_half(r, 1, 1)
                    for g in range(0, ITERS, 4):
                        n = min(4, ITERS - g)
                        act.wait_ge(keys_T, g // 4 + 1)
                        act.copy(key_T[:, g:g + n, :], ps[:, 5 + g // 4 % 2, 0:n * P].rearrange("p (i e) -> p i e", e=P))\
                           .then_inc(keys_out, 1)

                def body(i, q, peeled, ahead=True):
                    if ahead:
                        if not (peeled and q == 0):
                            r.taken.wait(act, i * 2 + q)
                            r.spilled[1 - q].wait(act, i * 16 + q * 16)
                        stage_half(r, i * 2 + (q + 1), 1 - q)
                    r.turned.wait(act, i * 2 + (q + 1))
                    if not peeled:
                        r.looked.wait(act, i * 2 + (q - 1))
                    act.copy(onehot_T[:, q], turned_ps).then_inc(r.turned_out.sem, 1)
                def heads_out(i):
                    r.to_heads.wait(act, i + 1)
                    act.copy(both_T[:, bass.ds(i, 1)].squeeze(1), both_ps).then_inc(r.to_heads_out.sem, 1)
                body(0, 0, True, ahead=r.layer > 0)
                body(0, 1, True)
                with act.Fori(1, ITERS - 1) as i:
                    body(i, 0, False)
                    heads_out(i - 1)
                    body(i, 1, False)
                body(ITERS - 1, 0, False)
                heads_out(ITERS - 2)
                body(ITERS - 1, 1, False, ahead=False)
                heads_out(ITERS - 1)

                def exps(i):
                    r.less_max.wait(act, i + 1)
                    act.activation(weights_now[:], both_T[:, bass.ds(i, 1)].squeeze(1), ACT.Exp)\
                       .then_inc(r.exped.sem, 1)

                def weights_out(i, q, slot, free):
                    r.to_edges.wait(act, i + 1)
                    if free:
                        r.msgs.wait(act, i * 2 + (q - 3))
                    act.copy(msg4[:, slot, :, D:].rearrange("p s (a h) -> p a s h", a=2),
                             both_ps[:, :, q * HALF * HEADS:(q + 1) * HALF * HEADS].rearrange("p a (s h) -> p a s h", h=HEADS))\
                       .then_inc(r.to_edges_out.sem, 1)

                def mids(half, slot):
                    r.rest.wait(act, half + 1)
                    act.copy(msg3[:, slot, 1], msg4[:, slot]).then_inc(r.mid.sem, 1)

                def parts(i, q, b, slot, peeled, last=False):
                    if q == 0:
                        if not last or slot < 2:
                            exps(i + 1)
                        weights_out(i, 1, slot + 1, not peeled)
                    elif not last or slot < 2:
                        weights_out(i + 1, 0, (slot + 1) % 4, not (peeled and slot < 3))
                    if not peeled:
                        r.summed.wait(act, b - 3)
                    r.weighed.wait(act, b + 1)
                    act.copy(msg3[:, slot, 0], msg4[:, slot]).then_inc(r.high.sem, 1)
                    if not (peeled and slot == 0):
                        mids(b - 1, (slot - 1) % 4)
                exps(0)
                weights_out(0, 0, 0, False)
                halves_by_four(act, parts, last=HV // 4 - 1)
                for b in range(4):
                    parts(ITERS - 2 + b // 2, b % 2, HV - 4 + b, b, False, True)
                mids(HV - 1, 3)
            rels[0][0].w.wait(act, 16 * 6)
            gats[2][1].summed.wait(act, HV)
            for c in w_halves:
                act.copy(w_part[0][:, c], w_full[:, c]).then_inc(w_cast, 1)
            for n, c in enumerate(w_halves):
                act.wait_ge(w_rest, n + 1)
                act.copy(w_part[1][:, c], w_full[:, c]).then_inc(w_cast, 1)
            act.copy(w_part[2][D:P], w_part[0][D:P]).then_inc(w_cast, 1)
            sqrt(1, small[:, 1, 0:TILES])

            def stage_all(r):
                table_written(r)
                stage_half(r, 0, 0)

                def body(i, q, peeled):
                    if not (peeled and q == 0):
                        r.summed.wait(act, i * 2 + q)
                    stage_half(r, i * 2 + (q + 1), 1 - q)
                halves(act, body, ITERS - 1)
                body(ITERS - 1, 0, False)

            for ex, r in rels:
                ex.inp.wait(act, 1)

                def parts_out(t, zeroth=False):
                    if not zeroth:
                        ex.tr.wait(act, t)
                    act.copy(x3s[:], x3[:, bass.ds(t, 1), :].squeeze(1)).then_inc(ex.xs.sem, 1)

                def turned_out(t, slot):
                    ex.tr.wait(act, t + 1)
                    act.copy(x3T[:, slot], x3_ps).then_inc(ex.xT.sem, 1)

                def body(t, slot, peeled, last=False):
                    if not peeled:
                        r.table[slot].wait(act, t * 8 - slot * 8)
                    if not last:
                        parts_out(t + 1)
                    for n in (1, 3, 5, 7):
                        ex.mm.wait(act, t * 9 + (n + 1))
                        act.copy(stage[:, slot, n * 512:(n + 1) * 512], ps[:, bank_of(slot, n), :]).then_inc(ex.out_a.sem, 1)
                        if n == 3 and not last:
                            turned_out(t + 1, 1 - slot)
                parts_out(0, True)
                turned_out(0, 0)
                tiles_by_two(act, body)
                stage_all(r)
            sqrt(2, small[:, 1, 0:TILES])
            stage_all(gin)
            sqrt(3, small[:, 1, 0:TILES])
            stage_all(wgin)
            for l, pj in enumerate(bns):
                project(pj)
                sqrt(4 + l, st[:, 3, :])
            sqrt(6, small[:, 1, 0:TILES])

        @block.tensor
        def _(pe):
            def project(l, pj, src, width):
                pj.inp.wait(pe, 1)
                pj.w.wait(pe, 64)

                def turn(g):
                    t, n = GROUPS[g]
                    if g >= 2:
                        pj.xT.wait(pe, g - 1)
                    for k in range(n):
                        ins = pe.transpose(ps[0:D, 5 + g % 2, k * P:(k + 1) * P], src[:, t + k, :], ident[:])
                    ins.then_inc(pj.tr.sem, 1)
                turn(0)
                for g, (t, n) in enumerate(GROUPS):
                    if g + 1 < len(GROUPS):
                        turn(g + 1)
                    pj.xT.wait(pe, g + 1)
                    if g >= 2:
                        pj.out.wait(pe, g - 1)
                    for k in range(n):
                        ins = pe.matmul(ps[:, (7, 4)[g % 2], k * width:(k + 1) * width], xT[:, g % 2, k, :],
                                        wn[:, l, 0:width], start=True, stop=True)
                    ins.then_inc(pj.mm.sem, 1)

            def clear_sums():
                for b in range(BANKS):
                    pe.matmul(ps[:, b, :], zero[:], zero[:].unsqueeze(1).broadcast_to([1, 4, P]), start=True, stop=False, skip_group_check=True)

            def places(i, q):
                return nc.values_load_multi_w_load_instructions(
                    place[0:1, bass.ds(i * (2 * HALF) + q * HALF, HALF)], engines=(mybir.EngineType.PE,),
                    min_val=0, max_val=(BANKS - 1) * 512 + (PERBANK - 1) * PITCH,
                    skip_runtime_bounds_check_because="a step's tile is a count of TILES - 1 comparisons, "
                                                      "so its place is one of the TILES places")[1]

            pe.wait_ge(ones_ready, 1)
            for t in range(TILES - 1):
                pe.wait_ge(below_ready, t + 1)
                ins = pe.matmul(ps[0:TILES - 1, 7, 0:EB * P], a_column[:, TILES - 1 - t:2 * TILES - 2 - t], below[:, t, :],
                                start=t == 0, stop=t == TILES - 2)
            ins.then_inc(ends_summed, 1)
            pe.wait_ge(passed_ready, 1)
            pe.matmul(ps[:, 7, 0:STEPS], ones[0:TILES - 1, :], tmp_s[0:TILES - 1, :], start=True, stop=True)\
              .then_inc(tiles_counted, 1)
            pe.wait_ge(picks_ready, 1)
            for q in range(4):
                for b in range(EB):
                    ins = pe.matmul(ps[:, q, 0:STEPS], lists[:, q, b, :], pick[:, b, :],
                                    start=b == 0, stop=b == EB - 1)
            ins.then_inc(picked, 1)
            def by_head(bank, m):
                for j in range(RUN):
                    ins = pe.matmul(ps[0:HEADS, bank, j:STEPS:RUN], ident[:, j * HEADS:(j + 1) * HEADS], m,
                                    start=True, stop=True, skip_group_check=True)
                return ins

            def by_pair(bank, m):
                for j in range(RUN):
                    at = (RUN - 1 - j) * HEADS
                    ins = pe.matmul(ps[:, bank, 0:ITERS], shift[:, at:at + P], m[:, j:STEPS:RUN],
                                    start=j == 0, stop=j == RUN - 1)
                return ins

            for pj, r in gats:
                project(r.layer, pj, x if r.layer == 0 else y, D + 2 * HEADS)
                r.table_ready.wait(pe, 1)
                if r.layer == 0:
                    clear_sums()
                    pe.wait_ge(keys_ready, 1)
                    for g in range(ITERS):
                        if g % 4 == 0 and g >= 8:
                            pe.wait_ge(keys_out, g // 4 - 1)
                        ins = pe.transpose(ps[:, 5 + g // 4 % 2, g % 4 * P:(g % 4 + 1) * P],
                                           key_s[:, g * RUN:(g + 1) * RUN, :].rearrange("p s h -> p (s h)"), ident[:])
                        if g % 4 == 3 or g == ITERS - 1:
                            ins.then_inc(keys_T, 1)
                    pe.wait_ge(keys_out, -(-ITERS // 4))
                    by_head(6, key_T[:, :, 0])
                    by_head(7, key_T[:, :, P - 1]).then_inc(key_ends, 1)

                def look(i, q, peeled):
                    at = places(i, q)
                    r.hot.wait(pe, i * 2 + (q + 1))
                    if not (peeled and q == 0):
                        r.turned_out.wait(pe, i * 2 + q)
                    for k in range(HALF):
                        ins = pe.transpose(turned_ps[:, k, :], onehot_h[:, q, :, k], ident_h[:])
                    ins.then_inc(r.turned.sem, 1)
                    if r.layer == 0:
                        for k in range(HALF):
                            pe.matmul(flat[:, bass.ds(at[k], REL)], onehot_h[:, q, :, k], relhot[:, q, :, k],
                                      start=False, stop=False, skip_group_check=True)
                    if r.layer != 1 and not (peeled and q == 0):
                        r.taken.wait(pe, i * 2 + q)
                    if r.layer == 1 and not peeled:
                        r.taken.wait(pe, i * 2 + (q - 1))
                    r.turned_out.wait(pe, i * 2 + (q + 1))
                    for k in range(HALF):
                        if r.layer == 1:
                            n, o = 2 * HEADS + REL, ps[:, 2 * q + k // PERBANK, (k % PERBANK) * PITCH:]
                        else:
                            n, o = 2 * HEADS, ps[:, 6, k * 2 * HEADS:]
                        for m in range(3):
                            ins = pe.matmul(o[:, 0:n], onehot_T[:, q, k, :], nodeq[:, m, bass.ds(at[k], n)],
                                            start=m == 0, stop=m == 2, skip_group_check=True)
                    ins.then_inc(r.looked.sem, 1)
                def turn_logits(i):
                    r.taken.wait(pe, i * 2 + 2)
                    if not (isinstance(i, int) and i == 0):
                        r.to_heads_out.wait(pe, i)
                    for n in range(2):
                        ins = pe.transpose(both_ps[:, n, :], logits_now[:, n, :], ident[:])
                    ins.then_inc(r.to_heads.sem, 1)
                look(0, 0, True)
                look(0, 1, True)
                with pe.Fori(1, ITERS) as i:
                    look(i, 0, False)
                    turn_logits(i - 1)
                    look(i, 1, False)
                turn_logits(ITERS - 1)
                r.scanned.wait(pe, 1)
                by_head(5, smax[:, :, 0])
                by_head(6, smax[:, :, P - 1]).then_inc(r.ends_T.sem, 1)
                r.carried.wait(pe, 1)
                by_pair(5, carry_f)
                by_pair(6, carry_b).then_inc(r.carries_T.sem, 1)
                r.acc_clear.wait(pe, 1)
                clear_sums()

                def turn_weights(i):
                    r.exped.wait(pe, i + 1)
                    if not (isinstance(i, int) and i == 0):
                        r.to_edges_out.wait(pe, i * 2)
                    for n in range(2):
                        ins = pe.transpose(both_ps[:, n, :], weights_now[:, n, :], ident[:])
                    ins.then_inc(r.to_edges.sem, 1)

                def add(i, q, b, slot, peeled, last=False):
                    if q == 0 and not last:
                        turn_weights(i + 2)
                    at = places(i, q)
                    r.msgs.wait(pe, b + 1)
                    for k in range(HALF):
                        for m in range(3):
                            ins = pe.matmul(flat[:, bass.ds(at[k], D + 2 * HEADS)], onehot_h[:, slot, :, k],
                                            msg3[:, slot, m, k, :], start=False, stop=False, skip_group_check=True)
                    ins.then_inc(r.summed.sem, 1)
                turn_weights(0)
                turn_weights(1)
                halves_by_four(pe, add, last=HV // 4 - 1)
                for b in range(4):
                    add(ITERS - 2 + b // 2, b % 2, HV - 4 + b, b, False, True)

            def add_gathered(r, before):
                before.acc_read.wait(pe, 1)
                clear_sums()

                def add(i, q, peeled):
                    at = places(i, q)
                    r.hot.wait(pe, i * 2 + (q + 1))
                    r.gathered[q].wait(pe, i * (16 * HALF) + 16 * HALF)
                    for k in range(HALF):
                        ins = pe.matmul(flat[:, bass.ds(at[k], D)], onehot[:, q, k, :], ring[:, q, k, 0:D],
                                        start=False, stop=False, skip_group_check=True)
                    ins.then_inc(r.summed.sem, 1)
                halves(pe, add)

            for ex, r in rels:
                before = rels[0][1] if r.layer else gats[2][1]
                before.acc_read.wait(pe, 1)
                ex.inp.wait(pe, 1)
                if r.layer == 0:
                    pe.wait_ge(w_cast, 5)
                    pe.wait_ge(w_rest, 4)

                def next_tile(t):
                    ex.xs.wait(pe, t + 1)
                    pe.sem_inc(tile_begun, 1)
                    pe.transpose(x3_ps[:, 0, :], x3s[:, 0:2 * D], ident_h[:])
                    pe.transpose(x3_ps[:, 1, :], x3s[:, D:3 * D], ident_h[:]).then_inc(ex.tr.sem, 1)
                next_tile(0)

                def body(t, slot, peeled, last=False):
                    zeroth = isinstance(t, int) and t == 0
                    ex.xT.wait(pe, t + 1)
                    for n in range(9):
                        if n >= 7:
                            o, k = 0, n - 7
                        else:
                            o, k = 1, max(m for m in range(9) if bank_of(1 - slot, m) == bank_of(slot, n))
                        if n >= 7 or not zeroth:
                            if k % 2:
                                ex.out_a.wait(pe, t * 4 + (k // 2 + 1 - 4 * o))
                            else:
                                ex.out_v.wait(pe, t * 6 + (6 * (k == 8) or k // 2 + 1) - 6 * o)
                        m = min(512, CW * D - n * 512)
                        for k, turned in ((0, 0), (1, 0), (2, 1)):
                            ins = pe.matmul(ps[:, bank_of(slot, n), 0:m], x3T[:, slot, turned, :], w_part[k][:, n * 512:n * 512 + m],
                                            start=k == 0, stop=k == 2)
                        ins.then_inc(ex.mm.sem, 1)
                        if n == 4 and not last:
                            next_tile(t + 1)
                tiles_by_two(pe, body)
                ex.out_v.wait(pe, 6 * TILES)
                ex.out_a.wait(pe, 4 * TILES)
                add_gathered(r, before)
            add_gathered(gin, rels[1][1])
            add_gathered(wgin, gin)
            for l, pj in enumerate(bns):
                project(3 + l, pj, y, D)
                for n in range(2):
                    pe.wait_ge(bn_part, 2 * l + n + 1)
                    pe.matmul(ps[:, 6, 256 + n * D:256 + (n + 1) * D], ones[:], st[:, 2 * n, :], start=True, stop=True)\
                      .then_inc(bn_total, 1)

        @block.vector
        def _(v):
            own_order = Order(v, v_own)
            then, done, wait = own_order.then, own_order.done, own_order.wait
            wide = [P, TILES, D]

            done(v.memset(x[:, TILES - 1, :], 0.0))
            done(v.memset(raw[:, 0], int(NEVER)))
            done(v.memset(raw[:, 1:3], 0))
            done(v.memset(lists[:, 3], 0.0))
            wait()
            v.memset(zero[:], 0.0).then_inc(pads_set, 1)
            done(v.memset(ones[:], 1.0))
            done(v.memset(goes_on[:, 0:1], -BIG))
            done(v.memset(pass_b[:, STEPS - 1:STEPS], -BIG))
            done(v.memset(nodeq[:], 0.0))
            v.wait_ge(const_ready, 6)
            then(v.tensor_scalar(ident[:], iota[:], part[:, 0:1], None, ALU.is_equal))
            done(v.tensor_scalar(shift[:], shift[:], 0.0, None, ALU.is_equal))
            then(v.tensor_copy(ident_h[:], ident[:]))
            v.tensor_scalar(a_column[:], iota[:, 0:2 * TILES - 1], float(TILES - 1), None, ALU.is_equal).then_inc(ones_ready, 1)

            def attention_weights(l):
                gats[l][0].w.wait(v, 64)
                then(v.tensor_tensor(st[0:D, 0:2, :], att[:, l], wn[:, l:l + 1, 0:D].broadcast_to([D, 2, D]), ALU.mult))
                then(v.tensor_reduce(wn[:, l, D:], st[0:D, 0:2, :].rearrange("p a (h c) -> p (a h) c", c=C), X, ALU.add))
            attention_weights(0)

            v.wait_ge(lists_loaded, 16 * 12)
            done(v.tensor_copy(lists[:, 0:2], raw[:, 0:2]))
            then(v.scalar_tensor_tensor(lists[:, 2], raw[:, 1], float(REL), raw[:, 2], ALU.mult, ALU.add))
            dsts = lists[:, 0].rearrange("p b e -> p (b e)")
            for t in range(TILES - 1):
                v.tensor_scalar(below[:, t, :], dsts, float((t + 1) * P), None, ALU.is_lt).then_inc(below_ready, 1)
            v.wait_ge(ends_summed, 1)
            then(v.tensor_reduce(ends[:], ps[0:TILES - 1, 7, 0:EB * P], X, ALU.add))
            then(v.tensor_scalar(ends[:], ends[:], 1.0 / P, CHUNKS - 0.5, ALU.mult, ALU.min))
            then(v.tensor_tensor(ends[:], ends[:], part[0:TILES - 1, :], ALU.add))
            then(v.tensor_scalar(tmp_s[0:TILES - 1, :], iota_s[0:TILES - 1, :], ends[:, 0:1], None, ALU.is_gt))
            v.sem_inc(passed_ready, 1)
            v.wait_ge(tiles_counted, 1)
            then(v.tensor_copy(tile_of[:], ps[:, 7, 0:STEPS]))
            then(v.tensor_scalar(tmp_s, tile_of[:], float(PITCH), None, ALU.mult))
            for b in range(1, BANKS):
                then(v.tensor_scalar(tmp_s2, tile_of[:], float(PERBANK * b), float(512 - PERBANK * PITCH),
                                     ALU.is_ge, ALU.mult))
                then(v.tensor_tensor(tmp_s, tmp_s, tmp_s2, ALU.add))
            then(v.tensor_copy(place[:], tmp_s[0:1, :]))
            then(v.tensor_tensor(tmp_s2, iota_s, tile_of[:], ALU.subtract))
            for b in range(EB):
                then(v.tensor_scalar(pick[:, b, :], tmp_s2, part[:, 0:1], float(b * P), ALU.subtract, ALU.is_equal))
            v.sem_inc(picks_ready, 1)

            v.wait_ge(picked, 1)
            dst_ps, src_ps, rel_ps, w_ps = (ps[:, q, 0:STEPS] for q in range(4))
            then(v.scalar_tensor_tensor(node_of[:], tile_of[:], -float(P), dst_ps, ALU.mult, ALU.add))
            then(v.tensor_scalar(tmp_s, node_of[:], 0.0, None, ALU.is_ge))
            then(v.scalar_tensor_tensor(tmp_s2, node_of[:], float(P), tmp_s, ALU.is_lt, ALU.mult))
            then(v.scalar_tensor_tensor(key, dst_ps, 1.0, tmp_s2, ALU.add, ALU.mult))
            then(v.tensor_copy(tmp_s, src_ps))
            done(v.scalar_tensor_tensor(rel_of[:], tmp_s, -float(REL), rel_ps, ALU.mult, ALU.add))
            done(v.tensor_copy(src_idx[:], src_ps))
            done(v.tensor_copy(rel_idx[:], rel_ps))
            done(v.tensor_copy(weight[:], w_ps))
            then(v.tensor_copy(key_s, key.unsqueeze(2).broadcast_to([P, STEPS, HEADS])))
            v.sem_inc(keys_ready, 1)
            then(v.tensor_scalar(tmp_s, node_of[:], 1.0, None, ALU.add))
            then(v.tensor_tensor(tmp_s, tmp_s, tmp_s2, ALU.mult))
            then(v.tensor_scalar(node_h[:], tmp_s, -1.0, None, ALU.add))
            v.sem_inc(edge_lists_ready, 1)

            wait()

            def segments():
                v.wait_ge(keys_out, -(-ITERS // 4))
                by_slot = lambda m: m.rearrange("p (i e) -> p i e", e=P)
                then(v.tensor_tensor(flags[:, :, 1:], key_T[:, :, 1:], key_T[:, :, 0:P - 1], ALU.not_equal))
                done(v.tensor_scalar(by_slot(joins[:, 0:SL])[:, :, 1:], flags[:, :, 1:], -BIG, None, ALU.mult))
                done(v.memset(by_slot(joins[:, 0:SL])[:, :, 0:1], -BIG))
                then(v.memset(joins[:, SL:SL + 1], -BIG))
                done(v.tensor_copy(joins_back[:, :, ::-1], by_slot(joins[:, 1:SL + 1])))
                v.wait_ge(key_ends, 1)
                done(v.tensor_copy(first_end, ps[0:HEADS, 6, 0:STEPS]))
                then(v.tensor_copy(last_end, ps[0:HEADS, 7, 0:STEPS]))
                single = ahead
                done(v.tensor_tensor(goes_on[:, 1:], first_end[:, 1:], last_end[:, 0:STEPS - 1], ALU.not_equal))
                then(v.tensor_tensor(single, first_end, last_end, ALU.not_equal))
                done(v.tensor_scalar(goes_on[:, 1:], goes_on[:, 1:], -BIG, None, ALU.mult))
                then(v.tensor_scalar(single, single, -BIG, None, ALU.mult))
                done(v.tensor_tensor(pass_f[:], goes_on[:], single, ALU.min))
                then(v.tensor_tensor(pass_b[:, 0:STEPS - 1], goes_on[:, 1:], single[:, 0:STEPS - 1], ALU.min))

            def one_hots(at, q, scale=None):
                for k in range(HALF):
                    c = lambda m: m[:, bass.ds(at + k, 1)]
                    if scale is None:
                        ins = v.tensor_scalar(onehot[:, q, k, :], iota[:], c(node_of), None, ALU.is_equal)
                    else:
                        ins = v.tensor_scalar(onehot[:, q, k, :], iota[:], c(node_of), c(scale),
                                              ALU.is_equal, ALU.mult)
                return ins

            def one_hots_h(at, slot):
                return v.tensor_tensor(onehot_h[:, slot], iota_k[:],
                                       node_h[:, bass.ds(at, HALF)].unsqueeze(1).broadcast_to([P, P, HALF]), ALU.is_equal)

            def project(pj, width, outs):
                pj.w.wait(v, 64)
                for g, (t, n) in enumerate(GROUPS):
                    pj.mm.wait(v, g + 1)
                    p = ps[:, (7, 4)[g % 2], 0:n * width].rearrange("p (a f) -> p a f", f=width)
                    for dst, col, bias in outs:
                        o, c = dst[:, t:t + n, :], p[:, :, col:col + dst.shape[2]]
                        if bias is None:
                            ins = v.tensor_copy(o, c)
                        else:
                            ins = v.tensor_tensor(o, c, bias.unsqueeze(1).broadcast_to([P, n, D]), ALU.add)
                    ins.then_inc(pj.out.sem, 1)
                pj.out.wait(v, len(GROUPS))

            def layernorm(n):
                s = small[:, :, 0:TILES]
                cent = w1
                then(v.tensor_reduce(s[:, 0], w1, X, ALU.add))
                then(v.tensor_scalar(s[:, 0], s[:, 0], 1.0 / D, None, ALU.mult))
                then(v.tensor_tensor(cent, w1, s[:, 0].unsqueeze(2).broadcast_to(wide), ALU.subtract))
                then(v.tensor_tensor(w2, cent, cent, ALU.mult))
                then(v.tensor_reduce(s[:, 1], w2, X, ALU.add))
                v.tensor_scalar(s[:, 1], s[:, 1], 1.0 / D, EPS, ALU.mult, ALU.add).then_inc(var_ready, 1)
                v.wait_ge(std_ready, n)
                then(v.reciprocal(s[:, 2], s[:, 1]))
                then(v.tensor_tensor(x[:], cent, s[:, 2].unsqueeze(2).broadcast_to(wide), ALU.mult))

            def in_parts(m, col):
                for k in range(3):
                    for b in range(BANKS):
                        o, ts = of_bank(nodeq[:, k], b, col, m.shape[2])
                        done(v.tensor_copy(o, m[:, ts, :]))
                    wait()
                    if k < 2:
                        for b in range(BANKS):
                            o, ts = of_bank(nodeq[:, k], b, col, m.shape[2])
                            done(v.tensor_tensor(m[:, ts, :], m[:, ts, :], o, ALU.subtract))
                        wait()

            def read_sums(r, dst, n):
                r.summed.wait(v, HV)
                for b in range(BANKS):
                    m, ts = of_bank(flat, b, 0, n)
                    done(v.tensor_copy(dst[:, ts, 0:n], m))
                wait()
                v.sem_inc(r.acc_read.sem, 1)

            v.wait_ge(loaded, 48)
            h_of, as_of = ht[:, :, 0:D], ht[:, :, D:D + HEADS]
            sm = [small[:, k, :].rearrange("p (t h) -> p t h", h=HEADS) for k in range(5)]
            for pj, r in gats:
                v.sem_inc(pj.inp.sem, 1)
                project(pj, D + 2 * HEADS, ((ht, 0, None), (sm[0], D + HEADS, None)))
                then(v.tensor_tensor(sm[1], as_of, sm[0], ALU.add))
                then(v.scalar_tensor_tensor(sm[2], sm[1], 0.2, sm[1], ALU.mult, ALU.max))
                done(v.tensor_copy(w1[:, :, 0:HEADS], sm[0]))
                then(v.tensor_copy(w1[:, :, HEADS:2 * HEADS], sm[2]))
                in_parts(w1[:, :, 0:2 * HEADS], 0)
                v.sem_inc(r.table_ready.sem, 1)
                if r.layer == 0:
                    segments()
                if r.layer < 2:
                    attention_weights(r.layer + 1)

                def mark(half, q, free):
                    at = half * HALF
                    if free is not None:
                        r.looked.wait(v, free)
                    ins = one_hots_h(at, q)
                    if r.layer < 2:
                        done(ins)
                        ins = v.tensor_tensor(relhot[:, q], iota_rel[:],
                                              rel_of[:, bass.ds(at, HALF)].unsqueeze(1).broadcast_to([P, REL, HALF]),
                                              ALU.is_equal)
                    ins.then_inc(r.hot.sem, 1)

                def take(i, q):
                    at = i * (2 * HALF) + q * HALF
                    r.looked.wait(v, i * 2 + (q + 1))
                    r.gathered[q].wait(v, i * (16 * HALF) + 16 * HALF)
                    if q == 0 and not (isinstance(i, int) and i == 0):
                        r.to_heads.wait(v, i)
                    if r.layer == 1:
                        pieces = [(k, min(PERBANK, HALF - k), ps[:, 2 * q + k // PERBANK, 0:PERBANK * PITCH]
                                   .rearrange("p (s c) -> p s c", c=PITCH)) for k in range(0, HALF, PERBANK)]
                    else:
                        pieces = [(0, HALF, ps[:, 6, 0:HALF * 2 * HEADS]
                                   .rearrange("p (s c) -> p s c", c=2 * HEADS))]
                    for k, n, g in pieces:
                        s = bass.ds(at + k, n)
                        now = logits_now[:, :, (q * HALF + k) * HEADS:(q * HALF + k + n) * HEADS].rearrange(
                            "p a (s h) -> p a s h", h=HEADS)
                        done(v.tensor_tensor(gz[:, q, k:k + n], ring[:, q, k:k + n, D:D + HEADS], g[:, 0:n, 0:HEADS], ALU.add))
                        if r.layer == 1:
                            r.hot.wait(v, i * 2 + (q + 1))
                            done(v.tensor_tensor(relsel[:, q, k:k + n], relhot[:, q, :, k:k + n].rearrange("p r k -> p k r"),
                                                 g[:, 0:n, 2 * HEADS:2 * HEADS + REL], ALU.mult))
                            wait()
                            done(v.tensor_reduce(count[:, s], relsel[:, q, k:k + n], X, ALU.add))
                        wait()
                        done(v.scalar_tensor_tensor(now[:, 0], gz[:, q, k:k + n], 0.2, gz[:, q, k:k + n], ALU.mult, ALU.max))
                        ins = v.tensor_copy(now[:, 1], g[:, 0:n, HEADS:2 * HEADS])
                        if k + n < HALF:
                            done(ins)
                        else:
                            ins.then_inc(r.taken.sem, 1)

                def scan(i):
                    r.to_heads_out.wait(v, i + 1)
                    if r.layer == 0:
                        for o, at in ((in_first, 0), (in_last, P - 1)):
                            done(v.tensor_scalar(o[:, bass.ds(i * P, P)], key_T[:, bass.ds(i, 1)].squeeze(1),
                                                 key_T[:, bass.ds(i, 1), at:at + 1].squeeze(1), -BIG, ALU.not_equal, ALU.mult))
                    m = both_T[:, bass.ds(i, 1)].squeeze(1)
                    then(v.tensor_tensor(run_max[:, 0], m[:, 0], m[:, 1], ALU.max))
                    then(v.tensor_tensor_scan(run_max[:, 1, ::-1], joins_back[:, bass.ds(i, 1)].squeeze(1), run_max[:, 0, ::-1],
                                              -BIG, ALU.add, ALU.max))
                    then(v.tensor_tensor_scan(smax[:, bass.ds(i, 1)].squeeze(1), joins[:, bass.ds(i * P, P)], run_max[:, 1],
                                              -BIG, ALU.add, ALU.max))
                per_half = {0: 3, 1: 1 + 4 * 2 + 1, 2: 2}[r.layer]
                mark(0, 0, None)
                mark(1, 1, None)
                take(0, 0)
                with v.Fori(1, ITERS) as i, own_order.loop(i, 1, ITERS, 2 * per_half + (5 if r.layer == 0 else 3)):
                    mark(i * 2, 0, i * 2 - 1)
                    take(i - 1, 1)
                    mark(i * 2 + 1, 1, i * 2)
                    take(i, 0)
                    scan(i - 1)
                take(ITERS - 1, 1)
                scan(ITERS - 1)
                v.sem_inc(r.scanned.sem, 1)
                wait()
                if r.layer == 0:
                    for b in range(BANKS):
                        m, ts = of_bank(flat, b, 0, REL)
                        done(v.tensor_copy(u[:, ts, 0:REL], m))
                    wait()
                    then(v.tensor_reduce(inv_degree[:], u[:, :, 0:REL], X, ALU.add))
                    then(v.tensor_scalar(inv_degree[:], inv_degree[:], 1.0, None, ALU.max))
                    then(v.reciprocal(inv_degree[:], inv_degree[:]))
                    in_parts(u[:, :, 0:REL], 2 * HEADS)
                if r.layer == 1:
                    then(v.tensor_scalar(count[:], count[:], 1.0, None, ALU.max))
                    then(v.reciprocal(count[:], count[:]))
                v.sem_inc(r.acc_clear.sem, 1)

                r.ends_T.wait(v, 1)
                done(v.tensor_copy(first_end, ps[0:HEADS, 5, 0:STEPS]))
                done(v.tensor_copy(last_end, ps[0:HEADS, 6, 0:STEPS]))
                done(v.memset(carry_f[:, 0:1], -BIG))
                then(v.memset(carry_b[:, STEPS - 1:STEPS], -BIG))
                done(v.tensor_tensor_scan(ahead, pass_f[:], last_end, -BIG, ALU.add, ALU.max))
                then(v.tensor_tensor_scan(behind[:, ::-1], pass_b[:, ::-1], first_end[:, ::-1], -BIG, ALU.add, ALU.max))
                done(v.tensor_tensor(carry_f[:, 1:], ahead[:, 0:STEPS - 1], goes_on[:, 1:], ALU.add))
                then(v.tensor_tensor(carry_b[:, 0:STEPS - 1], behind[:, 1:], goes_on[:, 1:], ALU.add))
                v.sem_inc(r.carried.sem, 1)
                r.carries_T.wait(v, 1)
                then(v.tensor_copy(carries[:], ps[:, 5:7, 0:ITERS]))

                def maxima(i):
                    m = smax[:, bass.ds(i, 1)].squeeze(1)
                    for n, block in enumerate((in_first, in_last)):
                        ins = v.scalar_tensor_tensor(m, block[:, bass.ds(i * P, P)], carries[:, n, bass.ds(i, 1)], m,
                                                     ALU.add, ALU.max)
                        if n == 0:
                            then(ins)
                    ins.then_inc(r.maxed.sem, 1)

                def low(half, slot):
                    r.mid.wait(v, half + 1)
                    v.tensor_tensor(msg3[:, slot, 2], msg4[:, slot], msg3[:, slot, 1], ALU.subtract).then_inc(r.msgs.sem, 1)

                def mark_half(b, slot, peeled):
                    if not peeled:
                        r.summed.wait(v, b - 3)
                    one_hots_h(b * HALF, slot)

                def weigh(i, q, b, slot, peeled, last=False):
                    at = i * (2 * HALF) + q * HALF
                    if not (peeled and slot < 1):
                        mark_half(b - 1, (slot - 1) % 4, peeled)
                    if q == 0 and not (last and slot == 2):
                        maxima(i + 1)
                    if not (peeled and slot < 3):
                        low(b - 3, (slot - 3) % 4)
                    if not peeled:
                        r.msgs.wait(v, b - 3)
                    r.to_edges_out.wait(v, b + 1)
                    r.back[q].wait(v, i * 16 + 16)
                    v.tensor_tensor(msg4[:, slot, :, 0:D].rearrange("p s (h c) -> p s h c", c=C),
                                    ring[:, q, :, 0:D].rearrange("p s (h c) -> p s h c", c=C),
                                    msg4[:, slot, :, D:D + HEADS].unsqueeze(3).broadcast_to([P, HALF, HEADS, C]),
                                    ALU.mult).then_inc(r.weighed.sem, 1)
                maxima(0)
                halves_by_four(v, weigh, before=lambda j: own_order.loop(j, 1, HV // 4 - 1, 2), last=HV // 4 - 1)
                for b in range(4):
                    weigh(ITERS - 2 + b // 2, b % 2, HV - 4 + b, b, False, True)
                low(HV - 3, 1)
                low(HV - 2, 2)
                mark_half(HV - 1, 3, False)
                low(HV - 1, 3)

                read_sums(r, u, D + 2 * HEADS)
                ex, exs = u[:, :, D:D + HEADS], u[:, :, D + HEADS:D + 2 * HEADS]
                then(v.tensor_tensor(exs, exs, inv_degree[:].unsqueeze(2).broadcast_to([P, TILES, HEADS]), ALU.mult))
                then(v.tensor_tensor(sm[0], ex, exs, ALU.add))
                then(v.tensor_scalar(sm[1], sm[0], 0.5, None, ALU.is_lt))
                then(v.tensor_tensor(sm[2], exs, sm[1], ALU.add))
                then(v.tensor_tensor(sm[3], ex, sm[2], ALU.add))
                then(v.tensor_scalar(sm[3], sm[3], 1e-16, None, ALU.add))
                done(v.reciprocal(sm[4], sm[3]))
                w1h, w2h = (m[:].rearrange("p t (h c) -> p t h c", c=C) for m in (w1, w2))
                then(v.tensor_tensor(w1h, h_of.rearrange("p t (h c) -> p t h c", c=C), per_head(sm[2]), ALU.mult))
                then(v.tensor_tensor(w1, w1, u[:, :, 0:D], ALU.add))
                then(v.tensor_tensor(w2h, w1h, per_head(sm[4]), ALU.mult))
                then(v.tensor_tensor(y[:], w2, gat_bias[:, r.layer, :].unsqueeze(1).broadcast_to(wide), ALU.add))
                if r.layer < 2:
                    then(v.tensor_scalar(y[:], y[:], 0.0, None, ALU.max))
                v.sem_inc(r.finished.sem, 1)
            then(v.tensor_tensor(w1, x[:], y[:], ALU.add))
            layernorm(1)

            def split_weights(n):
                c = lambda m: m[:, bass.ds(n * WIDE, WIDE)]
                high, mid, low = (c(m) for m in w_part)
                then(v.tensor_copy(high, c(w_full)))
                then(v.tensor_tensor(c(w_full), c(w_full), high, ALU.subtract))
                done(v.tensor_copy(low[D:P], high[D:P]))
                then(v.tensor_copy(mid, c(w_full)))
                then(v.tensor_tensor(low[0:D], c(w_full)[0:D], mid[0:D], ALU.subtract))

            def sum_round(r, scale, split=False):
                def body(i, q, peeled):
                    at = i * (2 * HALF) + q * HALF
                    if not peeled:
                        r.summed.wait(v, i * 2 + (q - 1))
                    one_hots(at, q, scale).then_inc(r.hot.sem, 1)
                if split:
                    halves(v, body, ITERS - PIECES)
                    rels[1][0].w.wait(v, 16 * 6)
                    with v.Fori(ITERS - PIECES, ITERS) as i, own_order.loop(i, ITERS - PIECES, ITERS, 5):
                        body(i, 0, False)
                        body(i, 1, False)
                        split_weights(i - (ITERS - PIECES))
                else:
                    halves(v, body)
                read_sums(r, u, D)

            for ex_, r in rels:
                xin, mid, high, low = (y if r.layer else x)[:], x3[:, :, 0:D], x3[:, :, D:2 * D], x3[:, :, 2 * D:]
                then(v.tensor_copy(high, xin))
                then(v.tensor_tensor(w1, xin, high, ALU.subtract))
                then(v.tensor_copy(mid, w1))
                then(v.tensor_tensor(low, w1, mid, ALU.subtract))
                v.sem_inc(ex_.inp.sem, 1)

                def body(t, slot, peeled, last=False):
                    if not peeled:
                        r.table[slot].wait(v, t * 8 - slot * 8)
                    for n in (0, 2, 4, 6):
                        ex_.mm.wait(v, t * 9 + (n + 1))
                        v.tensor_copy(stage[:, slot, n * 512:(n + 1) * 512], ps[:, bank_of(slot, n), :]).then_inc(ex_.out_v.sem, 1)
                    ex_.mm.wait(v, t * 9 + 9)
                    v.tensor_copy(stage[:, slot, 8 * 512:REL * D], ps[:, bank_of(slot, 8), 0:REL * D - 8 * 512]).then_inc(ex_.out_v.sem, 1)
                    v.tensor_copy(rr[:, bass.ds(t, 1), :].squeeze(1), ps[:, bank_of(slot, 8), REL * D - 8 * 512:CW * D - 8 * 512])\
                     .then_inc(ex_.out_v.sem, 1)
                tiles_by_two(v, body)
                sum_round(r, count, split=r.layer == 0)
                ex_.vec.wait(v, 16 * 2)
                bias = lambda k: rel_bias[:, r.layer, k, :].unsqueeze(1).broadcast_to(wide)
                then(v.tensor_tensor(w1, u[:, :, 0:D], rr[:, :, 0:D], ALU.add))
                done(v.tensor_tensor(w2, rr[:, :, D:2 * D], bias(1), ALU.add))
                then(v.tensor_tensor(w1, w1, bias(0), ALU.add))
                then(v.tensor_scalar(w2, w2, 0.0, None, ALU.max))
                then(v.scalar_tensor_tensor(y[:], w1, 0.0, w2, ALU.max, ALU.add))
                v.sem_inc(r.finished.sem, 1)
            then(v.tensor_tensor(w1, x[:], y[:], ALU.add))
            layernorm(2)

            v.sem_inc(gin.table_ready.sem, 1)
            sum_round(gin, None)
            then(v.tensor_scalar(small[:, 0, 0:1], eps1[:, 0:1], 1.0, None, ALU.add))
            then(v.scalar_tensor_tensor(w2, x[:], small[:, 0, 0:1], u[:, :, 0:D], ALU.mult, ALU.add))
            then(v.tensor_tensor(w1, x[:], w2, ALU.add))
            layernorm(3)

            v.sem_inc(wgin.table_ready.sem, 1)
            sum_round(wgin, weight)
            then(v.tensor_tensor(y[:], u[:, :, 0:D], x[:], ALU.add))
            then(v.tensor_scalar(cols[:, 0:1], part[:, 0:1], float(LAST), None, ALU.is_lt))
            for l, pj in enumerate(bns):
                v.sem_inc(pj.inp.sem, 1)
                project(pj, D, ((w1, 0, bn_vecs[:, l, 0, :]),))
                every_tile = lambda m: m.unsqueeze(1).broadcast_to(wide)
                last = w1[:, TILES - 1, :]
                then(v.tensor_scalar(last, last, cols[:, 0:1], None, ALU.mult))
                then(v.tensor_reduce(st[:, 0, :], w1.rearrange("p t f -> p f t"), X, ALU.add))
                v.sem_inc(bn_part, 1)
                v.wait_ge(bn_total, 2 * l + 1)
                then(v.tensor_scalar(st[:, 1, :], ps[:, 6, 256:256 + D], 1.0 / NODES, None, ALU.mult))
                then(v.tensor_tensor(w1, w1, every_tile(st[:, 1, :]), ALU.subtract))
                then(v.tensor_scalar(last, last, cols[:, 0:1], None, ALU.mult))
                then(v.tensor_tensor(w2, w1, w1, ALU.mult))
                then(v.tensor_reduce(st[:, 2, :], w2.rearrange("p t f -> p f t"), X, ALU.add))
                v.sem_inc(bn_part, 1)
                v.wait_ge(bn_total, 2 * l + 2)
                v.tensor_scalar(st[:, 3, :], ps[:, 6, 256 + D:256 + 2 * D], 1.0 / NODES, EPS, ALU.mult, ALU.add)\
                 .then_inc(var_ready, 1)
                v.wait_ge(std_ready, 4 + l)
                then(v.reciprocal(st[:, 4, :], st[:, 3, :]))
                then(v.tensor_tensor(st[:, 5, :], st[:, 4, :], bn_vecs[:, l, 1, :], ALU.mult))
                then(v.tensor_tensor(w2, w1, every_tile(st[:, 5, :]), ALU.mult))
                then(v.tensor_tensor(w2, w2, every_tile(bn_vecs[:, l, 2, :]), ALU.add))
                then(v.tensor_scalar(y[:], w2, 0.0, None, ALU.max))
            then(v.tensor_tensor(w1, x[:], y[:], ALU.add))
            layernorm(6)
            v.sem_inc(x_final, 1)


_INS = (["x", "src", "dst", "edge_type_65", "edge_weight"]
        + [f"L0_gnn_{n}{l}" for l in (1, 2, 3) for n in ("W", "a_src", "a_dst", "b")]
        + [f"L1_gnn_{n}" for n in ("W", "root", "bias", "res_W", "res_b")] + ["L2_gnn_eps"]
        + [f"L3_gnn_{n}{l}" for l in (1, 2) for n in ("W", "b", "gamma", "beta")])


def kernel(**inputs):
    import numpy as _np
    import concourse.bacc as _bacc
    from concourse import mybir as _mybir
    from concourse.bass_utils import run_bass_kernel_spmd as _run

    nc = _bacc.Bacc("TRN2", target_bir_lowering=False, num_devices=1)
    arrays, args = {}, {}
    for name in _INS:
        v = _np.ascontiguousarray(inputs[name])
        arrays[f"in_{name}"] = v
        args[name] = nc.dram_tensor(f"in_{name}", v.shape, _mybir.dt.from_np(v.dtype), kind="ExternalInput").ap()
    out = nc.dram_tensor("out_0", (NODES, D), F32, kind="ExternalOutput").ap()
    build(nc, args, out)
    r = _run(nc, [arrays], core_ids=[0])
    return r.results[0]["out_0"]
```
